# Optimizing a Trainium2 kernel written in Bass

```python
import numpy as np
import jax
import jax.numpy as jnp

def _softmax(x, axis=-1):
    return jax.nn.softmax(x, axis=axis)

def _gelu(x):
    return jax.nn.gelu(x, approximate=True)

def _silu(x):
    return jax.nn.silu(x)

def _sigmoid(x):
    return jax.nn.sigmoid(x)

def _layernorm(x, axis=-1, eps=1e-05):
    m = jnp.mean(x, axis=axis, keepdims=True)
    v = jnp.var(x, axis=axis, keepdims=True)
    return (x - m) / jnp.sqrt(v + eps)

def _scatter_add(tgt, idx, src, axis=0):
    return tgt.at[idx].add(src)

def _segment_sum(src, seg, n):
    return jax.ops.segment_sum(src, seg, n)
kernel_name = 'mk_gps_d2_gnn_r8_f6369f'

def setup_inputs(seed: int=0):
    np.random.seed(seed)
    _w = jnp.asarray

    def _rec_inputs():
        import jax
        import jax.numpy as jnp
        _gk = jax.random.key(seed)
        x = -0.0003713 + 1 * jax.random.normal(jax.random.fold_in(_gk, 1), (6250, 256), jnp.float32)
        src = jax.random.randint(jax.random.fold_in(_gk, 2), (200000,), 0, 6250, jnp.int32)
        dst = jax.random.randint(jax.random.fold_in(_gk, 3), (200000,), 0, 6250, jnp.int32)
        _o = jnp.argsort(dst, stable=True)
        src = src[_o]
        dst = dst[_o]
        edge_type_8 = jax.random.randint(jax.random.fold_in(_gk, 12), (200000,), 0, 8, jnp.int32)
        edge_weight = jax.random.uniform(jax.random.fold_in(_gk, 13), (200000,), jnp.float32, 0.0, 0.999998)
        return (x, src, dst, edge_type_8, edge_weight)
    x, src, dst, edge_type_8, edge_weight = _rec_inputs()

    def _L0_gnn_setup():
        import jax, jax.numpy as jnp
        import numpy as np
        N_NODES = 6250
        N_EDGES = 37500
        D = 256
        EPS = 1e-12

        def _gcn_layer(x, W, b, src, dst, norm, n_nodes):
            xt = x @ W
            msg = xt[src] * norm[:, None]
            agg = jax.ops.segment_sum(msg, dst, num_segments=n_nodes)
            return jax.nn.relu(agg + b)
        key = jax.random.key(seed)
        ks = jax.random.split(key, 10)
        h5_all = jax.random.normal(ks[0], (N_NODES, D), dtype=jnp.float32)
        edge_index = jax.random.randint(ks[1], (2, N_EDGES), 0, N_NODES, dtype=jnp.int64)
        edge_weight = jax.random.uniform(ks[2], (N_EDGES,), dtype=jnp.float32)
        s = 1.0 / np.sqrt(D)
        W6 = jax.random.normal(ks[3], (D, D), dtype=jnp.float32) * s
        b6 = jnp.zeros((D,), dtype=jnp.float32)
        W7 = jax.random.normal(ks[4], (D, D), dtype=jnp.float32) * s
        b7 = jnp.zeros((D,), dtype=jnp.float32)
        Wp = jax.random.normal(ks[5], (D, D), dtype=jnp.float32) * s
        bp = jnp.zeros((D,), dtype=jnp.float32)
        return {'h5_all': h5_all, 'edge_index': edge_index, 'edge_weight': edge_weight, 'W6': W6, 'b6': b6, 'W7': W7, 'b7': b7, 'Wp': Wp, 'bp': bp}
    _L0_gnn_all = _L0_gnn_setup()
    _L0_gnn_in = {k: v for k, v in _L0_gnn_all.items() if k in ('W6', 'b6', 'W7', 'b7', 'Wp', 'bp')}
    del _L0_gnn_all

    def _L0_mix_setup():
        import jax, jax.numpy as jnp
        import numpy as np
        NUM_HEADS = 8
        key = jax.random.key(seed)
        ks = jax.random.split(key, 5)
        B, N, C = (8, 2048, 256)
        x = jax.random.normal(ks[0], (B, N, C), dtype=jnp.float32)
        Wq = jax.random.normal(ks[1], (C, C), dtype=jnp.float32) * 0.02
        Wkv = jax.random.normal(ks[2], (2 * C, C), dtype=jnp.float32) * 0.02
        Wproj = jax.random.normal(ks[3], (C, C), dtype=jnp.float32) * 0.02
        bproj = jnp.zeros((C,), dtype=jnp.float32)
        return {'x': x, 'Wq': Wq, 'Wkv': Wkv, 'Wproj': Wproj, 'bproj': bproj}
    _L0_mix_all = _L0_mix_setup()
    _L0_mix_in = {k: v for k, v in _L0_mix_all.items() if k in ('Wq', 'Wkv', 'Wproj', 'bproj')}
    del _L0_mix_all

    def _L0_ffn_setup():
        import jax, jax.numpy as jnp
        import numpy as np
        DIM = 256
        H = 8
        D = 64
        G = 64
        INNER = H * D
        SCALE = D ** (-0.5)
        key = jax.random.key(seed)
        ks = jax.random.split(key, 12)
        B, N = (4, 2048)
        x = jax.random.normal(ks[0], (B, N, DIM), dtype=jnp.float32)
        s = lambda fan_in: 1.0 / np.sqrt(fan_in)
        W_fx = jax.random.normal(ks[1], (DIM, INNER), dtype=jnp.float32) * s(DIM)
        b_fx = jnp.zeros((INNER,), dtype=jnp.float32)
        W_x = jax.random.normal(ks[2], (DIM, INNER), dtype=jnp.float32) * s(DIM)
        b_x = jnp.zeros((INNER,), dtype=jnp.float32)
        A = jax.random.normal(ks[3], (G, D), dtype=jnp.float32)
        Q, _ = jnp.linalg.qr(A.T)
        W_slice = Q[:, :G].astype(jnp.float32)
        b_slice = jnp.zeros((G,), dtype=jnp.float32)
        W_q = jax.random.normal(ks[4], (D, D), dtype=jnp.float32) * s(D)
        W_k = jax.random.normal(ks[5], (D, D), dtype=jnp.float32) * s(D)
        W_v = jax.random.normal(ks[6], (D, D), dtype=jnp.float32) * s(D)
        W_out = jax.random.normal(ks[7], (INNER, DIM), dtype=jnp.float32) * s(INNER)
        b_out = jnp.zeros((DIM,), dtype=jnp.float32)
        temperature = jnp.ones((1, H, 1, 1), dtype=jnp.float32) * 0.5
        return {'x': x, 'W_fx': W_fx, 'b_fx': b_fx, 'W_x': W_x, 'b_x': b_x, 'W_slice': W_slice, 'b_slice': b_slice, 'W_q': W_q, 'W_k': W_k, 'W_v': W_v, 'W_out': W_out, 'b_out': b_out, 'temperature': temperature}
    _L0_ffn_all = _L0_ffn_setup()
    _L0_ffn_in = {k: v for k, v in _L0_ffn_all.items() if k in ('W_fx', 'b_fx', 'W_x', 'b_x', 'W_slice', 'b_slice', 'W_q', 'W_k', 'W_v', 'W_out', 'b_out', 'temperature')}
    del _L0_ffn_all

    def _L1_gnn_setup():
        import jax, jax.numpy as jnp
        import numpy as np
        N_NODES = 6250
        N_EDGES = 100000
        D_IN = 256
        D_OUT = 256
        N_REL = 8
        key = jax.random.key(seed)
        k_x, k_ei, k_et, k_w = jax.random.split(key, 4)
        x = jax.random.normal(k_x, (N_NODES, D_IN), dtype=jnp.float32)
        edge_index = jax.random.randint(k_ei, (2, N_EDGES), 0, N_NODES, dtype=jnp.int32)
        edge_type = jax.random.randint(k_et, (N_EDGES,), 0, N_REL, dtype=jnp.int32)
        limit = float(np.sqrt(6.0 / (D_IN + D_OUT)))
        weight = jax.random.uniform(k_w, (N_REL, D_IN, D_OUT), dtype=jnp.float32, minval=-limit, maxval=limit)
        bias = jnp.zeros((D_OUT,), dtype=jnp.float32)
        return {'x': x, 'edge_index': edge_index, 'edge_type': edge_type, 'weight': weight, 'bias': bias}
    _L1_gnn_all = _L1_gnn_setup()
    _L1_gnn_in = {k: v for k, v in _L1_gnn_all.items() if k in ('weight', 'bias')}
    del _L1_gnn_all

    def _L1_mix_setup():
        import jax, jax.numpy as jnp
        import numpy as np
        DIM = 256
        HEADS = 4
        DIM_HEAD = 32
        NUM_MEM = 4
        HIDDEN = HEADS * DIM_HEAD
        SCALE = DIM_HEAD ** (-0.5)

        def rmsnorm(x, g):
            n = jnp.linalg.norm(x, axis=-1, keepdims=True)
            return x / jnp.maximum(n, 1e-12) * g * x.shape[-1] ** 0.5
        key = jax.random.key(seed)
        ks = jax.random.split(key, 8)
        B, N = (4, 2048)
        return {'x': jax.random.normal(ks[0], (B, N, DIM), jnp.float32), 't': jax.random.normal(ks[1], (B,), jnp.float32), 'w_qkv': jax.random.normal(ks[2], (DIM, 3 * HIDDEN), jnp.float32) * 0.02, 'mem_kv': jax.random.normal(ks[3], (2, HEADS, DIM_HEAD, NUM_MEM), jnp.float32), 'w_out': jax.random.normal(ks[4], (HIDDEN, DIM), jnp.float32) * 0.02, 'b_out': jnp.zeros((DIM,), jnp.float32), 'g_out': jnp.ones((DIM,), jnp.float32), 'g_pre': jnp.ones((DIM,), jnp.float32)}
    _L1_mix_all = _L1_mix_setup()
    _L1_mix_in = {k: v for k, v in _L1_mix_all.items() if k in ('t', 'w_qkv', 'mem_kv', 'w_out', 'b_out', 'g_out', 'g_pre')}
    del _L1_mix_all

    def _L1_ffn_setup():
        import math
        import jax, jax.numpy as jnp
        import numpy as np
        CAPACITY_FACTOR = 1.25
        TOP_K = 2
        LN_EPS = 1e-05

        def _layer_norm(x, gamma, beta):
            mu = jnp.mean(x, axis=-1, keepdims=True)
            var = jnp.var(x, axis=-1, keepdims=True)
            return (x - mu) * jax.lax.rsqrt(var + LN_EPS) * gamma + beta
        key = jax.random.key(seed)
        ks = jax.random.split(key, 4)
        B, S, D, F, E = (8, 512, 256, 512, 8)
        x = jax.random.normal(ks[0], (B, S, D), dtype=jnp.float32)
        Wr = jax.random.normal(ks[1], (D, E), dtype=jnp.float32) / np.sqrt(D)
        br = jnp.zeros((E,), jnp.float32)
        W1 = jax.random.normal(ks[2], (E, D, F), dtype=jnp.float32) / np.sqrt(D)
        b1 = jnp.zeros((E, F), jnp.float32)
        W2 = jax.random.normal(ks[3], (E, F, D), dtype=jnp.float32) / np.sqrt(F)
        b2 = jnp.zeros((E, D), jnp.float32)
        gamma = jnp.ones((D,), jnp.float32)
        beta = jnp.zeros((D,), jnp.float32)
        return {'x': x, 'Wr': Wr, 'br': br, 'W1': W1, 'b1': b1, 'W2': W2, 'b2': b2, 'gamma': gamma, 'beta': beta}
    _L1_ffn_all = _L1_ffn_setup()
    _L1_ffn_in = {k: v for k, v in _L1_ffn_all.items() if k in ('Wr', 'br', 'W1', 'b1', 'W2', 'b2', 'gamma', 'beta')}
    del _L1_ffn_all
    return {'x': x, 'src': src, 'dst': dst, 'edge_type_8': edge_type_8, 'edge_weight': edge_weight, 'L0_gnn_W6': _L0_gnn_in['W6'], 'L0_gnn_b6': _L0_gnn_in['b6'], 'L0_gnn_W7': _L0_gnn_in['W7'], 'L0_gnn_b7': _L0_gnn_in['b7'], 'L0_gnn_Wp': _L0_gnn_in['Wp'], 'L0_gnn_bp': _L0_gnn_in['bp'], 'L0_mix_Wq': _L0_mix_in['Wq'], 'L0_mix_Wkv': _L0_mix_in['Wkv'], 'L0_mix_Wproj': _L0_mix_in['Wproj'], 'L0_mix_bproj': _L0_mix_in['bproj'], 'L0_ffn_W_fx': _L0_ffn_in['W_fx'], 'L0_ffn_b_fx': _L0_ffn_in['b_fx'], 'L0_ffn_W_x': _L0_ffn_in['W_x'], 'L0_ffn_b_x': _L0_ffn_in['b_x'], 'L0_ffn_W_slice': _L0_ffn_in['W_slice'], 'L0_ffn_b_slice': _L0_ffn_in['b_slice'], 'L0_ffn_W_q': _L0_ffn_in['W_q'], 'L0_ffn_W_k': _L0_ffn_in['W_k'], 'L0_ffn_W_v': _L0_ffn_in['W_v'], 'L0_ffn_W_out': _L0_ffn_in['W_out'], 'L0_ffn_b_out': _L0_ffn_in['b_out'], 'L0_ffn_temperature': _L0_ffn_in['temperature'], 'L1_gnn_weight': _L1_gnn_in['weight'], 'L1_gnn_bias': _L1_gnn_in['bias'], 'L1_mix_t': _L1_mix_in['t'], 'L1_mix_w_qkv': _L1_mix_in['w_qkv'], 'L1_mix_mem_kv': _L1_mix_in['mem_kv'], 'L1_mix_w_out': _L1_mix_in['w_out'], 'L1_mix_b_out': _L1_mix_in['b_out'], 'L1_mix_g_out': _L1_mix_in['g_out'], 'L1_mix_g_pre': _L1_mix_in['g_pre'], 'L1_ffn_Wr': _L1_ffn_in['Wr'], 'L1_ffn_br': _L1_ffn_in['br'], 'L1_ffn_W1': _L1_ffn_in['W1'], 'L1_ffn_b1': _L1_ffn_in['b1'], 'L1_ffn_W2': _L1_ffn_in['W2'], 'L1_ffn_b2': _L1_ffn_in['b2'], 'L1_ffn_gamma': _L1_ffn_in['gamma'], 'L1_ffn_beta': _L1_ffn_in['beta']}

def reference(x, src, dst, edge_type_8, edge_weight, L0_gnn_W6, L0_gnn_b6, L0_gnn_W7, L0_gnn_b7, L0_gnn_Wp, L0_gnn_bp, L0_mix_Wq, L0_mix_Wkv, L0_mix_Wproj, L0_mix_bproj, L0_ffn_W_fx, L0_ffn_b_fx, L0_ffn_W_x, L0_ffn_b_x, L0_ffn_W_slice, L0_ffn_b_slice, L0_ffn_W_q, L0_ffn_W_k, L0_ffn_W_v, L0_ffn_W_out, L0_ffn_b_out, L0_ffn_temperature, L1_gnn_weight, L1_gnn_bias, L1_mix_t, L1_mix_w_qkv, L1_mix_mem_kv, L1_mix_w_out, L1_mix_b_out, L1_mix_g_out, L1_mix_g_pre, L1_ffn_Wr, L1_ffn_br, L1_ffn_W1, L1_ffn_b1, L1_ffn_W2, L1_ffn_b2, L1_ffn_gamma, L1_ffn_beta):
    import jax
    import jax.numpy as jnp

    def _L0_gnn_ref(h5_all, edge_index, edge_weight, W6, b6, W7, b7, Wp, bp):
        import jax, jax.numpy as jnp
        import numpy as np
        N_NODES = 6250
        N_EDGES = 37500
        D = 256
        EPS = 1e-12

        def _gcn_layer(x, W, b, src, dst, norm, n_nodes):
            xt = x @ W
            msg = xt[src] * norm[:, None]
            agg = jax.ops.segment_sum(msg, dst, num_segments=n_nodes)
            return jax.nn.relu(agg + b)
        src, dst = (edge_index[0], edge_index[1])
        deg_out = jax.ops.segment_sum(edge_weight, src, num_segments=N_NODES)
        deg_in = jax.ops.segment_sum(edge_weight, dst, num_segments=N_NODES)
        norm = edge_weight * jax.lax.rsqrt(deg_out[src] * deg_in[dst] + EPS)
        h6 = _gcn_layer(h5_all, W6, b6, src, dst, norm, N_NODES)
        h7 = _gcn_layer(h6, W7, b7, src, dst, norm, N_NODES)
        out = h7 @ Wp + bp
        return out

    def _L0_mix_ref(x, Wq, Wkv, Wproj, bproj):
        import jax, jax.numpy as jnp
        import numpy as np
        NUM_HEADS = 8
        B, N, C = x.shape
        h = NUM_HEADS
        d = C // h
        q = jnp.einsum('bnc,oc->bno', x, Wq).reshape(B, N, h, d).transpose(0, 2, 1, 3)
        kv = jnp.einsum('bnc,oc->bno', x, Wkv).reshape(B, N, 2, h, d)
        k = kv[:, :, 0].transpose(0, 2, 1, 3)
        v = kv[:, :, 1].transpose(0, 2, 1, 3)
        q = jax.nn.elu(q) + 1.0
        k = jax.nn.elu(k) + 1.0
        k_sum = k.sum(axis=2)
        D_inv = 1.0 / jnp.maximum(jnp.einsum('bhnd,bhd->bhn', q, k_sum), 1e-06)
        context = jnp.einsum('bhnd,bhne->bhde', k, v)
        attn = jnp.einsum('bhnd,bhde->bhne', q, context) * D_inv[..., None]
        out = attn.transpose(0, 2, 1, 3).reshape(B, N, C)
        out = jnp.einsum('bnc,oc->bno', out, Wproj) + bproj
        return out

    def _L0_ffn_ref(x, W_fx, b_fx, W_x, b_x, W_slice, b_slice, W_q, W_k, W_v, W_out, b_out, temperature):
        import jax, jax.numpy as jnp
        import numpy as np
        DIM = 256
        H = 8
        D = 64
        G = 64
        INNER = H * D
        SCALE = D ** (-0.5)
        B, N, _ = x.shape
        fx_mid = (x @ W_fx + b_fx).reshape(B, N, H, D).transpose(0, 2, 1, 3)
        x_mid = (x @ W_x + b_x).reshape(B, N, H, D).transpose(0, 2, 1, 3)
        temp = jnp.clip(temperature, 0.1, 5.0)
        slice_weights = jax.nn.softmax((x_mid @ W_slice + b_slice) / temp, axis=-1)
        slice_norm = slice_weights.sum(axis=2)
        slice_token = jnp.einsum('bhnc,bhng->bhgc', fx_mid, slice_weights)
        slice_token = slice_token / (slice_norm[..., None] + 1e-05)
        q = slice_token @ W_q
        k = slice_token @ W_k
        v = slice_token @ W_v
        attn = jax.nn.softmax(jnp.einsum('bhgc,bhkc->bhgk', q, k) * SCALE, axis=-1)
        out_slice = jnp.einsum('bhgk,bhkc->bhgc', attn, v)
        out_x = jnp.einsum('bhgc,bhng->bhnc', out_slice, slice_weights)
        out_x = out_x.transpose(0, 2, 1, 3).reshape(B, N, INNER)
        return out_x @ W_out + b_out

    def _L1_gnn_ref(x, edge_index, edge_type, weight, bias):
        import jax, jax.numpy as jnp
        import numpy as np
        N_NODES = 6250
        N_EDGES = 100000
        D_IN = 256
        D_OUT = 256
        N_REL = 8
        num_nodes = x.shape[0]
        row, col = (edge_index[0], edge_index[1])
        xt = jnp.einsum('ni,rio->rno', x, weight)
        messages = xt[edge_type, col]
        out = jax.ops.segment_sum(messages, row, num_segments=num_nodes)
        return jax.nn.relu(out + bias)

    def _L1_mix_ref(x, t, w_qkv, mem_kv, w_out, b_out, g_out, g_pre):
        import jax, jax.numpy as jnp
        import numpy as np
        DIM = 256
        HEADS = 4
        DIM_HEAD = 32
        NUM_MEM = 4
        HIDDEN = HEADS * DIM_HEAD
        SCALE = DIM_HEAD ** (-0.5)

        def rmsnorm(x, g):
            n = jnp.linalg.norm(x, axis=-1, keepdims=True)
            return x / jnp.maximum(n, 1e-12) * g * x.shape[-1] ** 0.5
        b, n, c = x.shape
        xn = rmsnorm(x, g_pre)
        qkv = xn @ w_qkv
        q, k, v = jnp.split(qkv, 3, axis=-1)

        def to_heads(z):
            return z.reshape(b, n, HEADS, DIM_HEAD).transpose(0, 2, 3, 1)
        q, k, v = map(to_heads, (q, k, v))
        mk = jnp.broadcast_to(mem_kv[0], (b, HEADS, DIM_HEAD, NUM_MEM))
        mv = jnp.broadcast_to(mem_kv[1], (b, HEADS, DIM_HEAD, NUM_MEM))
        k = jnp.concatenate([mk, k], axis=-1)
        v = jnp.concatenate([mv, v], axis=-1)
        q = jax.nn.softmax(q, axis=-2) * SCALE
        k = jax.nn.softmax(k, axis=-1)
        context = jnp.einsum('bhdn,bhen->bhde', k, v)
        out = jnp.einsum('bhde,bhdn->bhen', context, q)
        out = out.transpose(0, 3, 1, 2).reshape(b, n, HIDDEN)
        out = rmsnorm(out @ w_out + b_out, g_out)
        return out + x

    def _L1_ffn_ref(x, Wr, br, W1, b1, W2, b2, gamma, beta):
        import math
        import jax, jax.numpy as jnp
        import numpy as np
        CAPACITY_FACTOR = 1.25
        TOP_K = 2
        LN_EPS = 1e-05

        def _layer_norm(x, gamma, beta):
            mu = jnp.mean(x, axis=-1, keepdims=True)
            var = jnp.var(x, axis=-1, keepdims=True)
            return (x - mu) * jax.lax.rsqrt(var + LN_EPS) * gamma + beta
        B, S, D = x.shape
        E = Wr.shape[1]
        N = B * S
        K = TOP_K
        logits = jnp.mean(x, axis=1) @ Wr + br
        routing_weights = jax.nn.softmax(logits, axis=-1)
        capacity = float(math.ceil(N * CAPACITY_FACTOR / E))
        expected_loads = routing_weights.sum(axis=0) * (N / B)
        scale = jnp.where(expected_loads > capacity, capacity / expected_loads, 1.0)
        routing_weights = jax.nn.softmax(routing_weights * scale, axis=-1)
        rw_tok = jnp.broadcast_to(routing_weights[:, None, :], (B, S, E)).reshape(N, E)
        top_w, top_i = jax.lax.top_k(rw_tok, K)
        top_w = jax.nn.softmax(top_w, axis=-1)
        xf = x.reshape(N, D)
        h = jax.nn.gelu(jnp.einsum('nd,edf->enf', xf, W1) + b1[:, None, :], approximate=False)
        y = jnp.einsum('enf,efd->end', h, W2) + b2[:, None, :]
        w_dense = jnp.zeros((N, E), x.dtype).at[jnp.arange(N)[:, None], top_i].add(top_w)
        out = jnp.einsum('ne,end->nd', w_dense, y).reshape(B, S, D)
        out = _layer_norm(out + x, gamma, beta)
        return out
    edge_index = jnp.stack([src, dst])
    xn = _layernorm(x, axis=-1)
    x = x + _L0_gnn_ref(xn, edge_index, edge_weight, L0_gnn_W6, L0_gnn_b6, L0_gnn_W7, L0_gnn_b7, L0_gnn_Wp, L0_gnn_bp) + _L0_mix_ref(xn[None], L0_mix_Wq, L0_mix_Wkv, L0_mix_Wproj, L0_mix_bproj)[0]
    x = x + _L0_ffn_ref(_layernorm(x, axis=-1)[None], L0_ffn_W_fx, L0_ffn_b_fx, L0_ffn_W_x, L0_ffn_b_x, L0_ffn_W_slice, L0_ffn_b_slice, L0_ffn_W_q, L0_ffn_W_k, L0_ffn_W_v, L0_ffn_W_out, L0_ffn_b_out, L0_ffn_temperature)[0]
    xn = _layernorm(x, axis=-1)
    x = x + _L1_gnn_ref(xn, edge_index, edge_type_8, L1_gnn_weight, L1_gnn_bias) + _L1_mix_ref(xn[None], L1_mix_t, L1_mix_w_qkv, L1_mix_mem_kv, L1_mix_w_out, L1_mix_b_out, L1_mix_g_out, L1_mix_g_pre)[0]
    x = x + _L1_ffn_ref(_layernorm(x, axis=-1)[None], L1_ffn_Wr, L1_ffn_br, L1_ffn_W1, L1_ffn_b1, L1_ffn_W2, L1_ffn_b2, L1_ffn_gamma, L1_ffn_beta)[0]
    return x

_drawn_inputs = setup_inputs


def setup_inputs(seed=0):
    import zlib

    import numpy as np

    out = dict(_drawn_inputs(seed))
    spreads = {'L0_gnn_b6': (0.0, 0.1),
     'L0_gnn_b7': (0.0, 0.1),
     'L0_gnn_bp': (0.0, 0.1),
     'L0_mix_bproj': (0.0, 0.1),
     'L0_ffn_b_fx': (0.0, 0.1),
     'L0_ffn_b_x': (0.0, 0.8),
     'L0_ffn_b_slice': (0.0, 0.8),
     'L0_ffn_b_out': (0.0, 0.1),
     'L0_ffn_temperature': (0.5, 0.6),
     'L1_gnn_bias': (0.0, 0.539),
     'L1_mix_b_out': (0.0, 0.1),
     'L1_mix_g_out': (1.0, 0.2),
     'L1_mix_g_pre': (1.0, 0.6),
     'L1_ffn_br': (0.0, 0.1),
     'L1_ffn_b1': (0.0, 0.8),
     'L1_ffn_b2': (0.0, 0.765),
     'L1_ffn_gamma': (1.0, 0.2),
     'L1_ffn_beta': (0.0, 0.489)}
    factors = {'edge_weight': 4.927,
     'L0_gnn_W6': 2.857,
     'L0_mix_Wq': 8.0,
     'L0_mix_Wkv': 8.0,
     'L0_mix_Wproj': 8.0,
     'L0_ffn_W_x': 4.618,
     'L0_ffn_W_slice': 7.388,
     'L0_ffn_W_q': 8.0,
     'L0_ffn_W_k': 8.0,
     'L1_mix_w_qkv': 8.0,
     'L1_mix_mem_kv': 8.0,
     'L1_mix_w_out': 8.0}
    for name, (base, spread) in spreads.items():
        noise = np.random.default_rng([zlib.crc32(name.encode()), seed]).standard_normal(out[name].shape)
        drawn = base * np.exp(spread * noise) if base else spread * noise
        out[name] = jnp.asarray(drawn.astype(out[name].dtype))
    for name, factor in factors.items():
        out[name] = (out[name] * factor).astype(out[name].dtype)
    return out
```

```python
import math
from contextlib import ExitStack

import concourse.bass as bass
from concourse import mybir

F32 = mybir.dt.float32
I32 = mybir.dt.int32
ALU = mybir.AluOpType
ACT = mybir.ActivationFunctionType
AX = mybir.AxisListType.X
P = 128
ds = bass.ds

LN_EPS = 1e-05
NORM_EPS = 1e-12
RING = 16
HALF = RING // 2
BANKS = 4


class Chain:

    def __init__(self, eng, sem, base=0):
        self.eng, self.sem, self.base, self.n = eng, sem, base, 0

    def link(self, ins):
        self.n += 1
        ins.then_inc(self.sem, 1)
        self.eng.wait_ge(self.sem, self.base + self.n)


def gps_layers(nc, a, dram, out):
    N, D = a["x"].shape
    E = a["src"].shape[0]
    H = D // P
    NT = -(-N // P)
    NPAD = NT * P
    TAIL = N - (NT - 1) * P
    J = -(-E // P)
    JTAIL = E - (P - 1) * J
    CB = -(-J // P)
    QB = -(-(J + NT - 1) // P)
    QR = -(-(J + NT - 1) // RING)
    NB = NT + 1
    TW = D + 4
    R = a["L1_gnn_weight"].shape[0]
    INNER = a["L0_ffn_W_fx"].shape[1]
    G = a["L0_ffn_W_slice"].shape[1]
    FH = INNER // G
    HID = a["L1_mix_w_out"].shape[0]
    MEM = a["L1_mix_mem_kv"].shape[3]
    MH = a["L1_mix_mem_kv"].shape[1]
    MD = HID // MH
    EX = a["L1_ffn_Wr"].shape[1]
    FF = a["L1_ffn_W1"].shape[2]
    KH = 8
    KD = D // KH
    assert D == 256 and G == 64 and HID == P and 0 < JTAIL <= J

    ctx = ExitStack()
    with ctx:
        def sb(name, shape, dt=F32):
            return ctx.enter_context(nc.sbuf_tensor(name, shape, dt))

        def dma_sem(name):
            return ctx.enter_context(nc.semaphore(name))

        in_use = []

        def sem(name):
            held = nc.semaphore(name)
            in_use.append((held, held.__enter__()))
            return in_use[-1][1]

        def recycle():
            with nc.Block() as block:
                @block.sync
                def _(sp):
                    for _, s in in_use:
                        sp.sem_clear(s)

            while in_use:
                in_use.pop()[0].__exit__(None, None, None)

        X = sb("X", [P, NT * D])
        ACC = sb("ACC", [P, NB * D])
        BIG = sb("BIG", [P, max(4 * J, NB * P, 6144)])
        pair_idx = sb("pair_idx", [P, QB * P], I32)
        pair_lo = sb("pair_lo", [P, QB * P])
        norm = sb("norm", [P, QB * P])
        AR = sb("AR", [P, 6144 + 8 * 512])
        W = AR[:, 0:6144]
        TT = AR[:, 6144:6144 + 8 * 512]
        T = [TT[:, k * 512:(k + 1) * 512] for k in range(8)]
        ring = AR[:, 0:RING * TW].rearrange("p (k c) -> p k c", k=RING)
        rows = [AR[:, k * TW:(k + 1) * TW] for k in range(RING)]
        sel = [AR[:, RING * TW + k * P:RING * TW + (k + 1) * P] for k in range(RING)]
        pos = AR[:, 0:J].bitcast(I32)
        idx_st = AR[:, J:J + RING].bitcast(I32)
        rec_st = AR[:, J + RING:J + 5 * RING]
        brow = sb("brow", [1, 2048])
        pair_off = brow[:, 0:QB * P].bitcast(I32)
        iota = sb("iota", [P, P])
        ident = sb("ident", [P, P])
        tri = sb("tri", [P, P])
        ones = sb("ones", [P, P])
        zeros = sb("zeros", [P, 132])
        bcol = sb("bcol", [P, NB])
        qcol = sb("qcol", [P, QB])
        eps_ln = sb("eps_ln", [P, 1])
        eps_norm = sb("eps_norm", [P, 1])
        mean_var = sb("mean_var", [P, NT * 2])
        rstd = sb("rstd", [P, NT])
        hmask = sb("hmask", [P, KH // H])
        bdiag = sb("bdiag", [P, H * 132])
        sumsq = sb("sumsq", [P, NT])
        small = sb("small", [P, 256])
        bank = [ctx.enter_context(nc.psum_tensor(f"bank{k}", [P, 512], F32)) for k in range(8)]
        vec = nc.vector
        pe = nc.tensor
        act = nc.scalar

        def tile_of(X, t):
            return X[:, ds(t * D, D)]

        x_in, tail_clear, made = dma_sem("x_in"), sem("tail_clear"), sem("constants_made")
        with nc.Block() as block:
            @block.sync
            def _(sp):
                full = a["x"][0:(NT - 1) * P, :].rearrange("(t p) d -> p t d", p=P)
                sp.dma_start(X[:, 0:(NT - 1) * D].rearrange("p (t d) -> p t d", d=D), full).then_inc(x_in, 16)
                sp.wait_ge(tail_clear, 1)
                sp.dma_start(X[0:TAIL, (NT - 1) * D:NT * D], a["x"][(NT - 1) * P:N, :]).then_inc(x_in, 16)
                sp.wait_ge(x_in, 32)

            @block.vector
            def _(dve):
                vec.memset(X[:, (NT - 1) * D:NT * D], 0.0).then_inc(tail_clear, 1)
                vec.memset(ones[:, :], 1.0)
                vec.memset(zeros[:, :], 0.0)
                vec.memset(eps_ln[:, :], LN_EPS)
                vec.memset(eps_norm[:, :], NORM_EPS)
                vec.memset(ACC[:, :], 0.0)

            @block.gpsimd
            def _(pool):
                pool.iota(iota[:, :], pattern=[[1, P]], base=0, channel_multiplier=0,
                          allow_small_or_imprecise_dtypes=True)
                pool.iota(bcol[:, :], pattern=[[1, NB]], base=0, channel_multiplier=0,
                          allow_small_or_imprecise_dtypes=True)
                pool.iota(qcol[:, :], pattern=[[P, QB]], base=0, channel_multiplier=1,
                          allow_small_or_imprecise_dtypes=True)
                pool.memset(ident[:, :], 0.0).then_inc(made, 1)
                pool.memset(tri[:, :], 1.0).then_inc(made, 1)
                pool.memset(hmask[:, :], 1.0).then_inc(made, 1)
                pool.wait_ge(made, 3)
                pool.affine_select(out=ident[:, :], in_=ident[:, :], compare_op=ALU.not_equal, fill=1.0,
                                   base=0, pattern=[[-1, P]], channel_multiplier=1)
                pool.affine_select(out=hmask[:, :], in_=hmask[:, :], compare_op=ALU.is_ge, fill=0.0, base=0,
                                   pattern=[[-KD, KH // H]], channel_multiplier=1).then_inc(made, 1)
                pool.wait_ge(made, 4)
                pool.affine_select(out=hmask[:, :], in_=hmask[:, :], compare_op=ALU.is_ge, fill=0.0, base=KD - 1,
                                   pattern=[[KD, KH // H]], channel_multiplier=-1)
                pool.affine_select(out=tri[:, :], in_=tri[:, :], compare_op=ALU.is_gt, fill=0.0,
                                   base=0, pattern=[[1, P]], channel_multiplier=-1)

        src_i = ACC[:, 0:J].bitcast(I32)
        dst_i = ACC[:, J:2 * J].bitcast(I32)
        typ_i = ACC[:, 2 * J:3 * J].bitcast(I32)
        hi_i = ACC[:, 3 * J:4 * J].bitcast(I32)
        w_f = ACC[:, 4 * J:5 * J]
        hi = [ACC[:, 5 * J:6 * J], ACC[:, 6 * J:7 * J]]
        rec = BIG[:, 0:4 * J].rearrange("p (j f) -> p j f", f=4)
        padded, edges_in, rec_src, fields, rec_out, edge_chain = (
            sem("pad_set"), dma_sem("edges_in"), sem("dst_field"), sem("fields"), dma_sem("rec_out"), sem("edge_chain"))
        with nc.Block() as block:
            @block.gpsimd
            def _(pool):
                for v, fill in ((src_i, NPAD), (dst_i, NPAD), (typ_i, 0), (w_f, 0)):
                    pool.memset(v[96:P, JTAIL - 1:J], fill).then_inc(padded, 1)

            @block.sync
            def _(sp):
                sp.wait_ge(padded, 4)
                for v, n in ((src_i, "src"), (dst_i, "dst"), (typ_i, "edge_type_8"), (w_f, "edge_weight")):
                    e = a[n]
                    for lo, hi_ in ((0, 112), (112, P - 1)):
                        sp.dma_start(v[lo:hi_, :], e[lo * J:hi_ * J].rearrange("(p j) -> p j", j=J)).then_inc(edges_in, 16)
                    sp.dma_start(v[P - 1:P, 0:JTAIL], e[(P - 1) * J:E].rearrange("(p j) -> p j", p=1)).then_inc(edges_in, 16)
                sp.wait_ge(fields, 2)
                sp.dma_start(dram["rec"].rearrange("(p j) f -> p (j f)", p=P), BIG[:, 0:4 * J]).then_inc(rec_out, 16)
                sp.wait_ge(rec_out, 16)

            @block.scalar
            def _(s):
                s.wait_ge(edges_in, 12 * 16)
                act.copy(rec[:, :, 2], w_f).then_inc(fields, 1)

            @block.vector
            def _(dve):
                c = Chain(dve, edge_chain)
                dve.wait_ge(edges_in, 12 * 16)
                vec.tensor_copy(rec[:, :, 0], src_i)
                c.link(vec.tensor_copy(rec[:, :, 1], dst_i))
                vec.scalar_tensor_tensor(rec[:, :, 3], typ_i, float(NPAD), rec[:, :, 1], ALU.mult, ALU.add).then_inc(fields, 1)
                for k, v in enumerate((src_i, dst_i)):
                    c.link(vec.tensor_scalar(hi_i, v, 7, None, ALU.arith_shift_right))
                    c.link(vec.tensor_copy(hi[k], hi_i))

        cnt, cum, tot, base = (small[:, k * 64:k * 64 + NB] for k in range(4))
        mask = ACC[:, 0:J].bitcast(I32)
        scan = ACC[:, J:2 * J]
        scan1 = ACC[:, 2 * J:3 * J]
        pos_f = ACC[:, 3 * J:4 * J]
        maskf = ACC[:, 4 * J:5 * J]
        start = [sb("start0", [P, NB]), sb("start1", [P, NB])]
        end = [sb("end0", [P, NB]), sb("end1", [P, NB])]
        SC = J // RING
        SREST = J - SC * RING
        for key in (0, 1):
            count_chain, counted, bases, placed, staged, sent = (
                sem(f"count_chain{key}"), sem(f"counted{key}"), sem(f"bases{key}"), sem(f"placed{key}"),
                sem(f"staged{key}"), [dma_sem(f"sent{key}_{k}") for k in range(2)])
            slotless = sem(f"stage_free{key}")
            dest = dram["rec_by_src"] if key == 0 else dram["rec_by_dst"]
            with nc.Block() as block:
                @block.vector
                def _(dve):
                    vec.memset(scan1, 1.0)
                    with dve.Fori(0, NB) as b:
                        vec.tensor_scalar(maskf, hi[key], bcol[:, ds(b, 1)], None, ALU.is_equal, ALU.add,
                                          accum_out=cnt[:, ds(b, 1)]).then_inc(count_chain, 1)
                        dve.wait_ge(count_chain, b + 1)
                    dve.nop().then_inc(counted, 1)
                    dve.wait_ge(bases, 1)
                    c = Chain(dve, count_chain, NB)
                    c.link(vec.tensor_copy(tot, bank[0][:, 64:64 + NB]))
                    c.link(vec.tensor_tensor_scan(end[key][:, :], ones[:, 0:NB], tot, 0.0, ALU.mult, ALU.add))
                    c.link(vec.tensor_tensor(start[key][:, :], end[key][:, :], tot, ALU.subtract))
                    c.link(vec.tensor_tensor(base, start[key][:, :], bank[0][:, 0:NB], ALU.add))
                    c.link(vec.tensor_scalar(base, base, -1.0, None, ALU.add))
                    c.link(vec.memset(pos_f, 0.0))
                    c0 = NB + c.n
                    with dve.Fori(0, NB) as b:
                        c = Chain(dve, count_chain, c0 + b * 3)
                        c.link(vec.tensor_scalar(mask, hi[key], bcol[:, ds(b, 1)], None, ALU.is_equal))
                        c.link(vec.tensor_tensor_scan(scan, scan1, mask, base[:, ds(b, 1)], ALU.mult, ALU.add))
                        dve.nop(nofuse=True)
                        c.link(vec.copy_predicated(pos_f, mask, scan))
                    vec.tensor_copy(pos[:, :], pos_f).then_inc(placed, 1)

                @block.tensor
                def _(t):
                    t.wait_ge(counted, 1)
                    t.wait_ge(count_chain, NB)
                    pe.matmul(bank[0][:, 0:NB], tri[:, :], cnt, start=True, stop=True)
                    pe.matmul(bank[0][:, 64:64 + NB], ones[:, :], cnt, start=True, stop=True).then_inc(bases, 1)

                @block.scalar
                def _(s):
                    s.wait_ge(placed, 1)

                    def stage(first, half, n):
                        cols = slice(half * HALF, half * HALF + n)
                        act.copy(idx_st[:, cols], pos[:, ds(first, n)])
                        act.copy(rec_st[:, half * HALF * 4:(half * HALF + n) * 4],
                                 BIG[:, ds(first * 4, n * 4)]).then_inc(staged, 1)

                    with s.Fori(0, SC) as i:
                        for half in range(2):
                            s.wait_ge(slotless, 2 * i + half + 1)
                            stage(i * RING + half * HALF, half, HALF)
                    for half in range(2):
                        n = min(HALF, SREST - half * HALF)
                        if n > 0:
                            s.wait_ge(slotless, 2 * SC + half + 1)
                            stage(SC * RING + half * HALF, half, n)

                @block.gpsimd
                def _(pool):
                    pool.sem_inc(slotless, 2)

                    def scatter(half, n):
                        for k in range(half * HALF, half * HALF + n):
                            pool.indirect_dma_start(
                                dest, bass.IndirectOffsetOnAxis(ap=idx_st[:, k:k + 1], axis=0),
                                rec_st[:, 4 * k:4 * k + 4], None).then_inc(sent[half], 16)

                    with pool.Fori(0, SC) as i:
                        for half in range(2):
                            pool.wait_ge(staged, 2 * i + half + 1)
                            pool.nop(nofuse=True)
                            scatter(half, HALF)
                            other = 1 - half
                            if half:
                                pool.wait_ge(sent[0], (i + 1) * HALF * 16)
                                pool.nop(nofuse=True)
                                pool.sem_inc(slotless, 1)
                                pool.wait_ge(sent[1], (i + 1) * HALF * 16)
                                pool.nop(nofuse=True)
                                pool.sem_inc(slotless, 1)
                    for half in range(2):
                        n = min(HALF, SREST - half * HALF)
                        if n > 0:
                            pool.wait_ge(staged, 2 * SC + half + 1)
                            pool.nop(nofuse=True)
                            scatter(half, n)
                    pool.wait_ge(sent[0], (SC * HALF + min(HALF, SREST)) * 16)
                    pool.nop(nofuse=True)
                    pool.wait_ge(sent[1], (SC * HALF + max(0, SREST - HALF)) * 16)
                    pool.nop(nofuse=True)

        def ints(k):
            return small[:, k * 64:k * 64 + NB].bitcast(I32)

        first_c, last_c, npair, poi, f, qbucket, qchunk, junk = (
            sb(n, [P, max(QB, NB)]) for n in ("first_c", "last_c", "npair", "pairs_before", "fdiff", "qbucket", "qchunk", "junk"))
        qi = sb("qi", [P, QB], I32)
        off_i = sb("off_i", [P, QB], I32)

        def make_pairs(key):
            ch, made_q, got, tr, cp, offs = (sem(f"pair_chain{key}"), sem(f"pair_chunk{key}"), dma_sem(f"pair_rows{key}"),
                                             sem(f"pair_turned{key}"), sem(f"pair_copied{key}"), dma_sem(f"pair_off{key}"))
            local = sem(f"pair_local{key}")
            source = dram["rec_by_src"] if key == 0 else dram["rec_by_dst"]
            chunk_rows = source.rearrange("(c e) f -> c (e f)", e=P)
            prow = T[0]
            b_only = slice(0, NT)
            with nc.Block() as block:
                @block.vector
                def _(dve):
                    c = Chain(dve, ch)
                    s0, e0 = start[key][:, b_only], end[key][:, b_only]
                    si, ei = ints(0)[:, b_only], ints(1)[:, b_only]
                    c.link(vec.tensor_copy(si, s0))
                    c.link(vec.tensor_scalar(npair[:, b_only], e0, -1.0, None, ALU.add))
                    c.link(vec.tensor_copy(ei, npair[:, b_only]))
                    c.link(vec.tensor_scalar(si, si, 7, None, ALU.arith_shift_right))
                    c.link(vec.tensor_scalar(ei, ei, 7, None, ALU.arith_shift_right))
                    c.link(vec.tensor_copy(first_c[:, b_only], si))
                    c.link(vec.tensor_copy(last_c[:, b_only], ei))
                    c.link(vec.tensor_tensor(npair[:, b_only], last_c[:, b_only], first_c[:, b_only], ALU.subtract))
                    c.link(vec.tensor_scalar(npair[:, b_only], npair[:, b_only], 1.0, None, ALU.add))
                    c.link(vec.tensor_tensor(last_c[:, b_only], e0, s0, ALU.is_gt))
                    c.link(vec.tensor_tensor(npair[:, b_only], npair[:, b_only], last_c[:, b_only], ALU.mult))
                    c.link(vec.tensor_tensor_scan(poi[:, b_only], ones[:, b_only], npair[:, b_only], 0.0, ALU.mult, ALU.add))
                    c.link(vec.tensor_tensor(f[:, b_only], first_c[:, b_only], poi[:, b_only], ALU.subtract))
                    c.link(vec.tensor_tensor(f[:, b_only], f[:, b_only], npair[:, b_only], ALU.add))
                    c.link(vec.tensor_tensor(last_c[:, 0:NT - 1], f[:, 1:NT], f[:, 0:NT - 1], ALU.subtract))
                    for k in range(QB):
                        c.link(vec.scalar_tensor_tensor(junk[:, b_only], poi[:, b_only], qcol[:, k:k + 1], ones[:, b_only],
                                                        ALU.is_le, ALU.mult, accum_out=qbucket[:, k:k + 1]))
                        c.link(vec.scalar_tensor_tensor(junk[:, 0:NT - 1], poi[:, 0:NT - 1], qcol[:, k:k + 1],
                                                        last_c[:, 0:NT - 1], ALU.is_le, ALU.mult,
                                                        accum_out=qchunk[:, k:k + 1]))
                    c.link(vec.tensor_tensor(qchunk[:, 0:QB], qchunk[:, 0:QB], qcol[:, :], ALU.add))
                    c.link(vec.tensor_scalar(qchunk[:, 0:QB], qchunk[:, 0:QB], f[:, 0:1], float(J - 1), ALU.add, ALU.min))
                    vec.tensor_copy(qi[:, :], qchunk[:, 0:QB])
                    c.link(vec.tensor_scalar(off_i[:, :], qbucket[:, 0:QB], float(P), None, ALU.mult))
                    c.link(vec.tensor_scalar(qbucket[:, 0:QB], qbucket[:, 0:QB], float(P), None, ALU.mult))
                    dve.nop().then_inc(made_q, 1)
                    key_f = 0 if key == 0 else 1
                    for k in range(QB):
                        dve.wait_ge(got, 16 * (k + 1))
                        pr = prow[:, :].rearrange("q (e f) -> q f e", f=4)
                        vec.tensor_scalar(pr[:, key_f, :], pr[:, key_f, :], qbucket[:, k:k + 1], None,
                                          ALU.subtract).then_inc(local, 1)
                        dve.wait_ge(tr, k + 1)
                        cols = slice(k * P, (k + 1) * P)
                        vec.tensor_copy(pair_lo[:, cols], bank[0][:, 0:P])
                        if key == 0:
                            vec.tensor_copy(pair_idx[:, cols], bank[0][:, P:2 * P]).then_inc(cp, 1)
                        else:
                            vec.tensor_copy(norm[:, cols], bank[0][:, 2 * P:3 * P])
                            vec.tensor_scalar(pair_idx[:, cols], bank[0][:, P:2 * P], float(NPAD - 1), None,
                                              ALU.min).then_inc(cp, 1)

                @block.gpsimd
                def _(pool):
                    pool.wait_ge(made_q, 1)
                    for k in range(QB):
                        if k:
                            pool.wait_ge(tr, k)
                        pool.indirect_dma_start(prow[:, :], None, chunk_rows,
                                                bass.IndirectOffsetOnAxis(ap=qi[:, k:k + 1], axis=0)).then_inc(got, 16)

                @block.tensor
                def _(t):
                    for k in range(QB):
                        t.wait_ge(local, k + 1)
                        if k:
                            t.wait_ge(cp, k)
                        pr = prow[:, :].rearrange("q (e f) -> q f e", f=4)
                        fields_ = (0, 3) if key == 0 else (1, 0, 2)
                        for n, fl in enumerate(fields_):
                            last = pe.transpose(bank[0][:, n * P:(n + 1) * P], pr[:, fl, :], ident[:, :])
                        last.then_inc(tr, 1)

                @block.sync
                def _(sp):
                    sp.wait_ge(made_q, 1)
                    with nc.allow_non_contiguous_dma(reason="one offset of a pair each"):
                        sp.dma_start(dram[f"off{key}"].rearrange("(k q) -> q k", q=P), off_i[:, :]).then_inc(offs, 16)
                    sp.wait_ge(offs, 16)

        recycle()
        make_pairs(1)

        parts = ACC[:, 0:5 * CB * P]
        lo_c = [parts[:, k * CB * P:k * CB * P + CB * P] for k in (0, 1)]
        hi_c = [parts[:, k * CB * P:k * CB * P + CB * P] for k in (2, 3)]
        w_c = parts[:, 4 * CB * P:5 * CB * P]
        int_a = BIG[:, 0:CB * P].bitcast(I32)
        int_b = BIG[:, CB * P:2 * CB * P].bitcast(I32)
        cr_in, cr_tr, cr_cp, dg_ch, onehot, counted2, degs_ready, deg_out_s = (
            dma_sem("chunk_rows_in"), sem("chunk_turned"), sem("chunk_copied"), sem("degree_chain"),
            sem("onehots"), sem("degrees_added"), sem("degrees_ready"), dma_sem("degrees_out"))
        degs = [small[:, k * 64:k * 64 + NB] for k in (0, 1)]
        with nc.Block() as block:
            @block.sync
            def _(sp):
                view = dram["rec"].rearrange("(c e) f -> c (e f)", e=P)
                for k in range(CB):
                    if k:
                        sp.wait_ge(cr_tr, k)
                    n = min(P, J - k * P)
                    sp.dma_start(T[1][0:n, :], view[k * P:k * P + n, :]).then_inc(cr_in, 16)
                sp.wait_ge(degs_ready, 1)
                with nc.allow_non_contiguous_dma(reason="one degree of a node each"):
                    sp.dma_start(dram["tab0"][:, D:D + 1].rearrange("(t p) c -> p t c", p=P), degs[0][:, 0:NT]
                                 .rearrange("p (t c) -> p t c", c=1)).then_inc(deg_out_s, 16)
                    sp.dma_start(dram["deg_in"].rearrange("(t p) -> p t", p=P), degs[1][:, :]).then_inc(deg_out_s, 16)
                sp.wait_ge(deg_out_s, 32)
                sp.dma_start(BIG[:, 0:NB * P], dram["deg_in"].rearrange("(a n) -> a n", a=1)
                             .broadcast_to([P, NB * P])).then_inc(deg_out_s, 16)
                sp.wait_ge(deg_out_s, 48)

            @block.tensor
            def _(t):
                pr = T[1][:, :].rearrange("q (e f) -> q f e", f=4)
                for k in range(CB):
                    n = min(P, J - k * P)
                    t.wait_ge(cr_in, 16 * (k + 1))
                    if k:
                        t.wait_ge(cr_cp, k)
                    for fl in range(3):
                        last = pe.transpose(bank[0][:, fl * P:fl * P + n], pr[0:n, fl, :], ident[0:n, 0:n])
                    last.then_inc(cr_tr, 1)
                for k in (0, 1):
                    pe.matmul(bank[1 + k][:, 0:NB], zeros[:, 0:P], zeros[:, 0:NB], start=True, stop=False, skip_group_check=True)
                with t.Fori(0, J) as c:
                    for k in (0, 1):
                        t.wait_ge(onehot, 2 * c + k + 1)
                        pe.matmul(bank[1 + k][:, 0:NB], sel[2 * k][:, :], sel[2 * k + 1][:, 0:NB],
                                  start=False, stop=False, skip_group_check=True).then_inc(counted2, 1)
                for k in (0, 1):
                    pe.matmul(bank[1 + k][:, 0:NB], zeros[:, 0:P], zeros[:, 0:NB], start=False, stop=True,
                              skip_group_check=True).then_inc(counted2, 1)

            @block.vector
            def _(dve):
                for k in range(CB):
                    n = min(P, J - k * P)
                    dve.wait_ge(cr_tr, k + 1)
                    c0 = slice(k * P, k * P + n)
                    vec.tensor_copy(lo_c[0][:, c0], bank[0][:, 0:n])
                    vec.tensor_copy(lo_c[1][:, c0], bank[0][:, P:P + n])
                    vec.tensor_copy(w_c[:, c0], bank[0][:, 2 * P:2 * P + n]).then_inc(cr_cp, 1)
                dve.wait_ge(cr_cp, CB)
                c = Chain(dve, dg_ch)
                for k in (0, 1):
                    c.link(vec.tensor_copy(int_a[:, 0:J], lo_c[k][:, 0:J]))
                    c.link(vec.tensor_scalar(int_b[:, 0:J], int_a[:, 0:J], 7, None, ALU.arith_shift_right))
                    c.link(vec.tensor_copy(hi_c[k][:, 0:J], int_b[:, 0:J]))
                    c.link(vec.tensor_scalar(int_b[:, 0:J], int_a[:, 0:J], 127, None, ALU.bitwise_and))
                    c.link(vec.tensor_copy(lo_c[k][:, 0:J], int_b[:, 0:J]))
                dve.sem_inc(counted2, 2)
                with dve.Fori(0, J) as c:
                    for k in (0, 1):
                        dve.wait_ge(counted2, 2 * c + k + 1)
                        vec.tensor_scalar(sel[2 * k][:, :], iota[:, :], lo_c[k][:, ds(c, 1)], None, ALU.is_equal)
                        vec.tensor_scalar(sel[2 * k + 1][:, 0:NB], bcol[:, :], hi_c[k][:, ds(c, 1)], w_c[:, ds(c, 1)],
                                          ALU.is_equal, ALU.mult).then_inc(onehot, 1)
                dve.wait_ge(counted2, 2 * J + 4)
                vec.tensor_copy(degs[0], bank[1][:, 0:NB])
                vec.tensor_copy(degs[1], bank[2][:, 0:NB]).then_inc(degs_ready, 1)

        mean = mean_var[:, 0:NT]
        var = mean_var[:, NT:2 * NT]

        def layer_norm_stats(name, rows_of=None):
            st, ag, rt = sem(f"{name}_stats"), sem(f"{name}_aggregate"), sem(f"{name}_root")
            six = TT[:, 0:6 * NT].rearrange("p (t c) -> p t c", c=6)
            with nc.Block() as block:
                @block.vector
                def _(dve):
                    with dve.Fori(0, NT) as t:
                        vec.bn_stats(TT[:, ds(6 * t, 6)], tile_of(X if rows_of is None else rows_of, t)).then_inc(st, 1)
                    dve.wait_ge(st, NT)
                    c = Chain(dve, ag)
                    c.link(vec.tensor_tensor(mean, six[:, :, 1], six[:, :, 4], ALU.subtract))
                    c.link(vec.tensor_tensor(var, six[:, :, 2], six[:, :, 5], ALU.add))
                    c.link(vec.tensor_scalar(mean, mean, 0.5, None, ALU.mult))
                    c.link(vec.tensor_tensor(mean, mean, mean, ALU.mult))
                    c.link(vec.scalar_tensor_tensor(var, var, 1.0 / D, mean, ALU.mult, ALU.add))
                    c.link(vec.tensor_tensor(mean, six[:, :, 1], six[:, :, 4], ALU.add))
                    c.link(vec.tensor_scalar(mean, mean, 0.5, None, ALU.mult))
                    dve.wait_ge(rt, 1)
                    c.link(vec.reciprocal(rstd[:, :], rstd[:, :]))

                @block.scalar
                def _(s):
                    s.wait_ge(ag, 5)
                    act.activation(rstd[:, :], var, ACT.Sqrt, bias=eps_ln[:, 0:1]).then_inc(rt, 1)

        def normalize(out_ap, t):
            return vec.tensor_scalar(out_ap, tile_of(X, t), mean_var[:, ds(t, 1)], rstd[:, ds(t, 1)],
                                     ALU.subtract, ALU.mult)

        def turn(bank_ap, src):
            for h in range(H):
                last = pe.transpose(bank_ap[:, h * P:(h + 1) * P], src[:, h * P:(h + 1) * P], ident[:, :])
            return last

        def product(out_ap, lhs, rhs, cols=None, last=True):
            n = rhs.shape[1] // H
            c0, c1 = cols or (0, n)
            for h in range(H):
                ins = pe.matmul(out_ap, lhs[:, h * P:(h + 1) * P], rhs[:, h * n + c0:h * n + c1],
                                start=h == 0, stop=last and h == H - 1)
            return ins

        def add_row(out_ap, row, last=True):
            return pe.matmul(out_ap, ones[0:1, :], row, start=False, stop=last)

        def load_halves(sp, dst, src, done):
            n = src.shape[1]
            return sp.dma_start(dst.rearrange("p (h n) -> p h n", h=H), src.rearrange("(h p) n -> p h n", p=P)).then_inc(done, 16)

        def bias_row(sp, at, name, done):
            n = a[name].shape[0]
            sp.dma_start(brow[0:1, at:at + n], a[name].rearrange("(a n) -> a n", a=1)).then_inc(done, 16)
            return brow[0:1, at:at + n]


        def tiles(eng, stages):
            lags = max(lag for lag, _ in stages)

            def step(i, par, n):
                for lag, f in stages:
                    b = (par - lag) % 2
                    if not isinstance(i, int):
                        f(i - lag, b, P, n + (first + par - lag - b) // 2)
                    elif 0 <= i - lag < NT:
                        f(i - lag, b, TAIL if i - lag == NT - 1 else P, (i - lag) // 2)

            first = max(2, lags + lags % 2)
            turns = (NT - 1 - first) // 2
            for i in range(first):
                step(i, i % 2, None)
            with eng.Fori(0, turns) as n:
                for par in range(2):
                    step(2 * n + first + par, par, n)
            for i in range(first + 2 * turns, NT + lags):
                step(i, i % 2, None)

        def first_use(u):
            return isinstance(u, int) and u == 0

        def wide(v, n=NT):
            return v[:, 0:n * D].rearrange("p (t d) -> p t d", d=D)

        def per_tile(v):
            return v.rearrange("p (t a) -> p t a", a=1).broadcast_to([P, NT, D])

        def per_feature(v):
            return v.rearrange("p (a d) -> p a d", a=1).broadcast_to([P, NT, D])

        def turned_weights(name, dst, weights):
            w_in, w_tr, w_cp = dma_sem(f"{name}_w_in"), sem(f"{name}_w_turned"), sem(f"{name}_w_copied")
            blocks = [w[o:o + P, :] for w in weights for o in range(0, w.shape[0], P)]
            n_out = len(blocks) * P
            with nc.Block() as block:
                @block.sync
                def _(sp):
                    for k, b in enumerate(blocks):
                        sp.dma_start(TT[:, k * D:(k + 1) * D], b).then_inc(w_in, 16)

                @block.tensor
                def _(t):
                    t.wait_ge(w_in, 16 * len(blocks))
                    for k in range(len(blocks)):
                        turn(bank[k][:, 0:D], TT[:, k * D:(k + 1) * D]).then_inc(w_tr, 1)

                @block.vector
                def _(dve):
                    for k in range(len(blocks)):
                        dve.wait_ge(w_tr, k + 1)
                        vec.tensor_copy(dst.rearrange("p (h o) -> p h o", h=H)[:, :, k * P:(k + 1) * P],
                                        bank[k][:, 0:D].rearrange("p (h o) -> p h o", h=H)).then_inc(w_cp, 1)
                    dve.wait_ge(w_cp, len(blocks))

        recycle()
        layer_norm_stats("ln0")
        wq_t, wkv_t, wproj_t = W[:, 0:H * D], W[:, H * D:3 * H * D], W[:, 3 * H * D:4 * H * D]
        turned_weights("mix0_q", wq_t, [a["L0_mix_Wq"]])
        turned_weights("mix0_kv", wkv_t, [a["L0_mix_Wkv"]])
        turned_weights("mix0_proj", wproj_t, [a["L0_mix_Wproj"]])

        stored = [dma_sem("m0_stored0"), dma_sem("m0_stored1")]
        nrm, turned, turned_sb, kv, low, expk, kpos, v_sb, done = (
            sem(f"m0_{n}") for n in ("normalized", "turned", "turned_sb", "kv", "low", "exp", "k", "v", "done"))

        def vx(b):
            return T[4 + b][:, 0:H * 132]

        with nc.Block() as block:
            @block.vector
            def _(dve):
                def normal(t, b, rows_, u):
                    dve.wait_ge(done, t + 1)
                    dve.nop(nofuse=True)
                    if not first_use(u):
                        dve.wait_ge(stored[b], 16 * u)
                    normalize(T[0][:, b * D:(b + 1) * D], t).then_inc(nrm, 1)

                def keys(t, b, rows_, u):
                    dve.wait_ge(kv, t + 1)
                    vec.tensor_scalar(T[2][:, b * D:(b + 1) * D], bank[2 + b][:, 0:D], 0.0, None, ALU.min).then_inc(low, 1)
                    dve.wait_ge(expk, t + 1)
                    vec.scalar_tensor_tensor(T[3][:, b * D:(b + 1) * D], bank[2 + b][:, 0:D], 0.0,
                                             T[2][:, b * D:(b + 1) * D], ALU.max, ALU.add).then_inc(kpos, 1)

                tiles(dve, [(0, normal), (1, keys)])

            @block.sync
            def _(sp):
                def store(t, b, rows_, u):
                    sp.wait_ge(nrm, t + 1)
                    sp.dma_start(dram["tab0"][ds(t * P, P), 0:D], T[0][:, b * D:(b + 1) * D]).then_inc(stored[b], 16)

                tiles(sp, [(0, store)])
                for b in (0, 1):
                    sp.wait_ge(stored[b], 16 * ((NT + 1 - b) // 2))

            @block.tensor
            def _(t_):
                t_.sem_inc(done, 2)

                def keys(t, b, rows_, u):
                    t_.wait_ge(nrm, t + 1)
                    turn(bank[b][:, 0:D], T[0][:, b * D:(b + 1) * D]).then_inc(turned, 1)
                    t_.wait_ge(turned_sb, t + 1)
                    product(bank[2 + b][:, 0:D], T[1][:, b * D:(b + 1) * D], wkv_t, (0, D))
                    product(bank[4 + b][:, 0:D], T[1][:, b * D:(b + 1) * D], wkv_t, (D, 2 * D)).then_inc(kv, 1)

                def context(t, b, rows_, u):
                    t_.wait_ge(kpos, t + 1)
                    t_.wait_ge(v_sb, t + 1)
                    for h in range(H):
                        last = pe.matmul(bank[6 + h][:, 0:P + 1], T[3][0:rows_, b * D + h * P:b * D + (h + 1) * P],
                                         vx(b)[0:rows_, h * 132:h * 132 + P + 1], start=False, stop=False, skip_group_check=True)
                    last.then_inc(done, 1)

                for h in range(H):
                    pe.matmul(bank[6 + h][:, 0:P + 1], zeros[:, 0:P], zeros[:, 0:P + 1], start=True, stop=False, skip_group_check=True)
                tiles(t_, [(0, keys), (1, context)])
                for h in range(H):
                    pe.matmul(bank[6 + h][:, 0:P + 1], zeros[:, 0:P], zeros[:, 0:P + 1], start=False, stop=True, skip_group_check=True)

            @block.scalar
            def _(s):
                for b in (0, 1):
                    for h in range(H):
                        act.copy(vx(b)[:, h * 132 + P:h * 132 + P + 1], ones[:, 0:1])

                def copy(t, b, rows_, u):
                    s.wait_ge(turned, t + 1)
                    act.copy(T[1][:, b * D:(b + 1) * D], bank[b][:, 0:D]).then_inc(turned_sb, 1)

                def values(t, b, rows_, u):
                    s.wait_ge(kv, t + 1)
                    act.copy(vx(b).rearrange("p (h c) -> p h c", c=132)[:, :, 0:P],
                             bank[4 + b][:, 0:D].rearrange("p (h c) -> p h c", c=P)).then_inc(v_sb, 1)
                    s.wait_ge(low, t + 1)
                    act.activation(T[2][:, b * D:(b + 1) * D], T[2][:, b * D:(b + 1) * D], ACT.Exp).then_inc(expk, 1)

                tiles(s, [(0, copy), (1, values)])

        bd_made = sem("m0_blocks")
        with nc.Block() as block:
            @block.vector
            def _(dve):
                for h in range(H):
                    for j in range(KH // H):
                        vec.tensor_scalar(bdiag[:, h * 132 + KD * j:h * 132 + KD * (j + 1)],
                                          bank[6 + h][:, KD * j:KD * (j + 1)], hmask[:, j:j + 1], None,
                                          ALU.mult).then_inc(bd_made, 1)
                    vec.tensor_scalar(bdiag[:, h * 132 + P:h * 132 + P + KH // H], hmask[:, :], bank[6 + h][:, P:P + 1],
                                      None, ALU.mult).then_inc(bd_made, 1)

        bias_in = dma_sem("m1_bias_in")
        nrm, turned, turned_sb, qs, low, expq, qpos, att, den, scaled, turned2, turned2_sb, proj, done = (
            sem(f"m1_{n}") for n in ("normalized", "turned", "turned_sb", "q", "low", "exp", "q_pos", "attention",
                                     "denominator", "scaled", "turned2", "turned2_sb", "projected", "done"))

        def part(k, b):
            return T[k][:, b * D:(b + 1) * D]

        with nc.Block() as block:
            @block.sync
            def _(sp):
                bias_row(sp, 0, "L0_mix_bproj", bias_in)

            @block.vector
            def _(dve):
                dve.sem_inc(done, 2)

                def normal(t, b, rows_, u):
                    dve.wait_ge(done, t + 1)
                    normalize(part(0, b), t).then_inc(nrm, 1)

                def scale(t, b, rows_, u):
                    dve.wait_ge(att, t + 1)
                    c = Chain(dve, den, 2 * t)
                    av = bank[4 + b][:, 0:H * 132].rearrange("p (h c) -> p h c", c=132)
                    sv = T[6][:, b * 8:b * 8 + 8]
                    c.link(vec.tensor_scalar(sv.rearrange("p (h j) -> p h j", h=H), av[:, :, P:P + KH // H], 1e-06, None, ALU.max))
                    c.link(vec.reciprocal(sv, sv))
                    vec.tensor_tensor(part(4, b).rearrange("p (h j d) -> p h j d", h=H, d=KD),
                                      av[:, :, 0:P].rearrange("p h (j d) -> p h j d", d=KD),
                                      sv.rearrange("p (h j a) -> p h j a", h=H, a=1).broadcast_to([P, H, KH // H, KD]),
                                      ALU.mult).then_inc(scaled, 1)

                def elu(t, b, rows_, u):
                    dve.wait_ge(qs, t + 1)
                    vec.tensor_scalar(part(2, b), bank[2 + b][:, 0:D], 0.0, None, ALU.min).then_inc(low, 1)
                    dve.wait_ge(expq, t + 1)
                    vec.scalar_tensor_tensor(part(3, b), bank[2 + b][:, 0:D], 0.0, part(2, b), ALU.max, ALU.add).then_inc(qpos, 1)

                def add(t, b, rows_, u):
                    dve.wait_ge(proj, t + 1)
                    vec.tensor_tensor(tile_of(X, t), tile_of(X, t), bank[6 + b][:, D:2 * D], ALU.add).then_inc(done, 1)

                tiles(dve, [(0, normal), (1, scale), (0, elu), (1, add)])

            @block.scalar
            def _(s):
                def copy(t, b, rows_, u):
                    s.wait_ge(turned, t + 1)
                    act.copy(part(1, b), bank[b][:, 0:D]).then_inc(turned_sb, 1)

                def copy2(t, b, rows_, u):
                    s.wait_ge(turned2, t + 1)
                    act.copy(part(5, b), bank[6 + b][:, 0:D]).then_inc(turned2_sb, 1)

                def exp(t, b, rows_, u):
                    s.wait_ge(low, t + 1)
                    act.activation(part(2, b), part(2, b), ACT.Exp).then_inc(expq, 1)

                tiles(s, [(0, copy), (1, copy2), (0, exp)])

            @block.tensor
            def _(t_):
                t_.wait_ge(bias_in, 16)

                def attend(t, b, rows_, u):
                    t_.wait_ge(qpos, t + 1)
                    for h in range(H):
                        last = pe.matmul(bank[4 + b][:, h * 132:(h + 1) * 132], part(3, b)[:, h * P:(h + 1) * P],
                                         bdiag[:, h * 132:(h + 1) * 132], start=True, stop=True)
                    last.then_inc(att, 1)

                def turn1(t, b, rows_, u):
                    t_.wait_ge(nrm, t + 1)
                    turn(bank[b][:, 0:D], part(0, b)).then_inc(turned, 1)

                def turn2(t, b, rows_, u):
                    t_.wait_ge(scaled, t + 1)
                    turn(bank[6 + b][:, 0:D], part(4, b)).then_inc(turned2, 1)

                def query(t, b, rows_, u):
                    t_.wait_ge(turned_sb, t + 1)
                    for h in range(H):
                        for c in range(H):
                            last = pe.matmul(bank[2 + b][:, h * P:(h + 1) * P], wq_t[:, c * D + h * P:c * D + (h + 1) * P],
                                             part(1, b)[:, c * P:(c + 1) * P], start=c == 0, stop=c == H - 1)
                    last.then_inc(qs, 1)

                def project(t, b, rows_, u):
                    t_.wait_ge(turned2_sb, t + 1)
                    product(bank[6 + b][:, D:2 * D], part(5, b), wproj_t, last=False)
                    add_row(bank[6 + b][:, D:2 * D], brow[0:1, 0:D]).then_inc(proj, 1)

                tiles(t_, [(1, attend), (0, turn1), (1, turn2), (0, query), (1, project)])

        NPAIR = QR * RING
        assert NPAIR + HALF <= QB * P or QR * RING == QB * P

        landed_sems = [dma_sem(f"landed{k}") for k in range(RING)]
        turn_no = [0]

        def aggregate(name, table, width, off, weighted, norms):
            off_in, cleared, idx_ready, landed, chosen, summed, added, di_ch, rooted = (
                dma_sem(f"{name}_off_in"), sem(f"{name}_cleared"), sem(f"{name}_idx_ready"), landed_sems, sem(f"{name}_chosen"), sem(f"{name}_summed"),
                sem(f"{name}_added"), sem(f"{name}_norm_chain"), sem(f"{name}_rooted"))
            before = turn_no[0] * QR
            turn_no[0] += 1
            idx_at = AR[:, 6400:6400 + RING].bitcast(I32)
            junk = AR[:, 6528:6528 + P]
            n_in = AR[:, 6784:6784 + HALF]
            d_root = AR[:, 6800:6800 + HALF]
            with nc.Block() as block:
                @block.sync
                def _(sp):
                    sp.dma_start(pair_off, off.rearrange("(a n) -> a n", a=1)).then_inc(off_in, 16)

                @block.scalar
                def _(s):
                    def stage(m, half):
                        s.wait_ge(summed, HALF * (m + 1))
                        act.copy(idx_at[:, half * HALF:(half + 1) * HALF],
                                 pair_idx[:, ds(m * HALF, HALF)]).then_inc(idx_ready, 1)

                    stage(0, 0)
                    with s.Fori(0, QR) as i:
                        for half in range(2):
                            m = 2 * i + half
                            if half == 0:
                                stage(m + 1, 1)
                            else:
                                s.wait_ge(summed, HALF * (m + 2))
                                act.copy(idx_at[:, 0:HALF], pair_idx[:, ds((m + 1) * HALF, HALF)]).then_inc(idx_ready, 1)
                            if norms:
                                s.wait_ge(di_ch, m * (HALF + 3) + HALF + 1)
                                act.activation(d_root, n_in, ACT.Sqrt, bias=eps_norm[:, 0:1]).then_inc(rooted, 1)

                @block.gpsimd
                def _(pool):
                    with pool.Fori(0, QR) as i:
                        for half in range(2):
                            pool.wait_ge(idx_ready, 2 * i + half + 1)
                            pool.nop(nofuse=True)
                            for k in range(half * HALF, (half + 1) * HALF):
                                pool.indirect_dma_start(rows[k][:, 0:width], None, table,
                                                        bass.IndirectOffsetOnAxis(ap=idx_at[:, k:k + 1], axis=0)
                                                        ).then_inc(landed[k], 16)

                @block.tensor
                def _(t):
                    t.sem_inc(summed, RING)
                    with t.Fori(0, QR) as i:
                        for half in range(2):
                            t.wait_ge(chosen, 2 * i + half + 1)
                            for k in range(half * HALF, (half + 1) * HALF):
                                t.wait_ge(landed[k], 16 * (i + 1 + before))
                                t.wait_ge(added, i * RING + k + 1)
                                pe.matmul(bank[k % BANKS][:, 0:D], sel[k], rows[k][:, 0:D], start=True, stop=True).then_inc(summed, 1)

                @block.vector
                def _(dve):
                    dve.wait_ge(off_in, 16)
                    vec.memset(ACC[:, :], 0.0).then_inc(cleared, 1)
                    dve.wait_ge(cleared, 1)
                    dve.sem_inc(added, BANKS)
                    regs = [dve.alloc_register(f"{name}_r{k}") for k in range(4)]

                    def offsets(m, quarter):
                        dve.load(regs, pair_off[0:1, ds(m * HALF + 4 * quarter, 4)])
                        return [dve.snap(r, min_val=0, max_val=NT * P) for r in regs]

                    with dve.Fori(0, QR) as i:
                        for half in range(2):
                            m = 2 * i + half
                            dve.wait_ge(idx_ready, m + 1)
                            if norms:
                                for q in range(2):
                                    offs = offsets(m, q)
                                    for j in range(4):
                                        k = q * 4 + j
                                        vec.scalar_tensor_tensor(
                                            junk, iota[:, :], pair_lo[:, ds(m * HALF + k, 1)], BIG[:, ds(offs[j], P)],
                                            ALU.is_equal, ALU.mult, accum_out=n_in[:, k:k + 1]).then_inc(di_ch, 1)
                                        dve.wait_ge(di_ch, m * (HALF + 3) + k + 1)
                                for k in range(HALF):
                                    dve.wait_ge(landed[half * HALF + k], 16 * (i + 1 + before))
                                c = Chain(dve, di_ch, m * (HALF + 3) + HALF)
                                c.link(vec.tensor_tensor(n_in, n_in, ring[:, half * HALF:(half + 1) * HALF, D], ALU.mult))
                                dve.wait_ge(rooted, m + 1)
                                c.link(vec.reciprocal(d_root, d_root))
                                c.link(vec.tensor_tensor(norm[:, ds(m * HALF, HALF)], norm[:, ds(m * HALF, HALF)], d_root, ALU.mult))
                            for k in range(HALF):
                                if weighted:
                                    ins = vec.tensor_scalar(sel[half * HALF + k], iota[:, :], pair_lo[:, ds(m * HALF + k, 1)],
                                                            norm[:, ds(m * HALF + k, 1)], ALU.is_equal, ALU.mult)
                                else:
                                    ins = vec.tensor_scalar(sel[half * HALF + k], iota[:, :], pair_lo[:, ds(m * HALF + k, 1)],
                                                            None, ALU.is_equal)
                            ins.then_inc(chosen, 1)
                            for q in range(2):
                                offs = offsets(m, q)
                                for j in range(4):
                                    k = half * HALF + q * 4 + j
                                    n = i * RING + k
                                    dve.wait_ge(summed, RING + n + 1)
                                    dve.wait_ge(added, BANKS + n)
                                    at = ACC[:, ds(offs[j] * H, D)]
                                    vec.tensor_tensor(at, at, bank[k % BANKS][:, 0:D], ALU.add).then_inc(added, 1)
                    dve.wait_ge(added, BANKS + NPAIR)

        w_g = [W[:, k * H * D:(k + 1) * H * D] for k in range(3)]

        def graph_dense(name, last_layer):
            w_in = dma_sem(f"{name}_weights_in")
            staged, turned, turned_sb, prod, act_out, turned2, turned2_sb, proj, done = (
                sem(f"{name}_{n}") for n in ("staged", "turned", "turned_sb", "product", "relu", "turned2", "turned2_sb",
                                             "projected", "done"))
            stored = [dma_sem(f"{name}_stored{b}") for b in (0, 1)]

            def part(k, b):
                return T[k][:, b * D:(b + 1) * D]

            with nc.Block() as block:
                @block.sync
                def _(sp):
                    names = ("W7", "Wp") if last_layer else ("W6",)
                    for k, n in enumerate(names):
                        load_halves(sp, w_g[k], a[f"L0_gnn_{n}"], w_in)
                        bias_row(sp, k * D, f"L0_gnn_b{n[1:]}", w_in)
                    if not last_layer:
                        def store(t, b, rows_, u):
                            sp.wait_ge(act_out, t + 1)
                            sp.dma_start(dram["tab1"][ds(t * P, P), :], part(2, b)).then_inc(stored[b], 16)

                        tiles(sp, [(0, store)])
                        for b in (0, 1):
                            sp.wait_ge(stored[b], 16 * ((NT + 1 - b) // 2))

                @block.vector
                def _(dve):
                    def load(t, b, rows_, u):
                        dve.wait_ge(done, t + 1)
                        vec.tensor_copy(part(0, b), tile_of(ACC, t)).then_inc(staged, 1)

                    if not last_layer:
                        tiles(dve, [(0, load)])
                    else:
                        dve.sem_inc(done, 2)

                        def add(t, b, rows_, u):
                            dve.wait_ge(proj, t + 1)
                            vec.tensor_tensor(tile_of(X, t), tile_of(X, t), bank[6 + b][:, 0:D], ALU.add).then_inc(done, 1)

                        tiles(dve, [(0, load), (1, add)])

                @block.scalar
                def _(s):
                    def copy(t, b, rows_, u):
                        s.wait_ge(turned, t + 1)
                        act.copy(part(1, b), bank[b][:, 0:D]).then_inc(turned_sb, 1)

                    def relu(t, b, rows_, u):
                        s.wait_ge(prod, t + 1)
                        if not last_layer and not first_use(u):
                            s.wait_ge(stored[b], 16 * u)
                        act.activation(part(2, b), bank[2 + b][:, 0:D], ACT.Relu).then_inc(act_out, 1)
                        if not last_layer:
                            s.wait_ge(act_out, t + 1)
                            s.sem_inc(done, 1)

                    def copy2(t, b, rows_, u):
                        s.wait_ge(turned2, t + 1)
                        act.copy(part(3, b), bank[4 + b][:, 0:D]).then_inc(turned2_sb, 1)

                    if not last_layer:
                        s.sem_inc(done, 2)
                        tiles(s, [(0, copy), (1, relu)])
                    else:
                        tiles(s, [(0, copy), (1, copy2), (0, relu)])

                @block.tensor
                def _(t_):
                    t_.wait_ge(w_in, 64 if last_layer else 32)

                    def turn1(t, b, rows_, u):
                        t_.wait_ge(staged, t + 1)
                        turn(bank[b][:, 0:D], part(0, b)).then_inc(turned, 1)

                    def layer(t, b, rows_, u):
                        t_.wait_ge(turned_sb, t + 1)
                        product(bank[2 + b][:, 0:D], part(1, b), w_g[0], last=False)
                        add_row(bank[2 + b][:, 0:D], brow[0:1, 0:D]).then_inc(prod, 1)

                    def turn2(t, b, rows_, u):
                        t_.wait_ge(act_out, t + 1)
                        turn(bank[4 + b][:, 0:D], part(2, b)).then_inc(turned2, 1)

                    def project(t, b, rows_, u):
                        t_.wait_ge(turned2_sb, t + 1)
                        product(bank[6 + b][:, 0:D], part(3, b), w_g[1], last=False)
                        add_row(bank[6 + b][:, 0:D], brow[0:1, D:2 * D]).then_inc(proj, 1)

                    if last_layer:
                        tiles(t_, [(0, turn1), (1, turn2), (0, layer), (1, project)])
                    else:
                        tiles(t_, [(0, turn1), (0, layer)])

        recycle()
        aggregate("agg0", dram["tab0"], D + 1, dram["off1"], True, True)
        graph_dense("gnn0", False)
        recycle()
        aggregate("agg1", dram["tab1"], D, dram["off1"], True, False)
        graph_dense("gnn1", True)

        recycle()
        layer_norm_stats("ln1")
        NPR = FH // 2
        w_fx, w_lg = W[:, 0:H * INNER], W[:, H * INNER:2 * H * INNER]
        w_xt = W[0:G, 4 * INNER:4 * INNER + FH * D]
        w_slice, w_qk, w_kk, w_vk = (BIG[0:G, 5120 + k * G:5120 + (k + 1) * G] for k in range(4))
        b_xt = BIG[0:G, 5376:5376 + FH]
        temp = BIG[:, 5392:5392 + FH]
        b_fx = BIG[:, 5408:5408 + NPR * G]
        tok_n = BIG[:, 5664:5664 + 2 * NPR]
        w_in = dma_sem("f0_weights_in")
        w_ch, w_tr, w_cp, w_mm = (sem(f"f0_{n}") for n in ("weight_chain", "weight_turned",
                                                                "weight_copied", "weight_product"))
        bs_row = brow[0:1, 0:G]
        bl_row = brow[0:1, 512:512 + INNER]
        with nc.Block() as block:
            @block.sync
            def _(sp):
                load_halves(sp, w_fx, a["L0_ffn_W_fx"], w_in)
                load_halves(sp, TT[:, 0:H * INNER], a["L0_ffn_W_x"], w_in)
                for v, n in ((w_slice, "W_slice"), (w_qk, "W_q"), (w_kk, "W_k"), (w_vk, "W_v")):
                    sp.dma_start(v, a[f"L0_ffn_{n}"]).then_inc(w_in, 16)
                sp.dma_start(temp, a["L0_ffn_temperature"].rearrange("a h b c -> (a b c) h").broadcast_to([P, FH])).then_inc(w_in, 16)
                with nc.allow_non_contiguous_dma(reason="a bias as columns"):
                    sp.dma_start(b_xt, a["L0_ffn_b_x"].rearrange("(h d) -> d h", d=G)).then_inc(w_in, 16)
                for par in range(2):
                    sp.dma_start(b_fx[par * G:(par + 1) * G, :].rearrange("p (k c) -> p k c", c=G),
                                 a["L0_ffn_b_fx"].rearrange("(k two c) -> two k c", two=2, c=G)[par:par + 1, :, :]
                                 .broadcast_to([G, NPR, G])).then_inc(w_in, 16)
                bias_row(sp, 0, "L0_ffn_b_slice", w_in)

            @block.vector
            def _(dve):
                dve.wait_ge(w_in, 16 * 11)
                c = Chain(dve, w_ch)
                c.link(vec.tensor_scalar(temp, temp, 0.1, 5.0, ALU.max, ALU.min))
                c.link(vec.reciprocal(temp, temp))
                for k in range(4):
                    dve.wait_ge(w_tr, k + 1)
                    vec.tensor_copy(w_xt[:, k * 512:(k + 1) * 512], bank[k][0:G, :]).then_inc(w_cp, 1)
                scale = temp.rearrange("p (h a) -> p h a", a=1)
                for h in range(H):
                    dve.wait_ge(w_mm, h + 1)
                    vec.tensor_tensor(w_lg[:, h * INNER:(h + 1) * INNER].rearrange("p (h g) -> p h g", g=G),
                                      bank[4 + h][:, :].rearrange("p (h g) -> p h g", g=G),
                                      scale.broadcast_to([P, FH, G]), ALU.mult)
                dve.wait_ge(w_mm, H + 1)
                row = bl_row.rearrange("p (h g) -> p h g", g=G)
                c.link(vec.tensor_tensor(row, bank[6][0:1, :].rearrange("p (h g) -> p h g", g=G),
                                         bs_row.rearrange("p (a g) -> p a g", a=1).broadcast_to([1, FH, G]), ALU.add))
                c.link(vec.tensor_tensor(row, row, scale[0:1, :, :].broadcast_to([1, FH, G]), ALU.mult))

            @block.tensor
            def _(t):
                t.wait_ge(w_in, 16 * 11)
                for h in range(FH):
                    for c in range(H):
                        at = h * D + c * P
                        last = pe.transpose(bank[at // 512][0:G, at % 512:at % 512 + P],
                                            TT[:, c * INNER + h * G:c * INNER + (h + 1) * G], ident[:, :])
                    if h % 2:
                        last.then_inc(w_tr, 1)
                t.wait_ge(w_cp, 4)
                for c in range(H):
                    for h in range(FH):
                        last = pe.matmul(bank[4 + c][:, h * G:(h + 1) * G], w_xt[:, h * D + c * P:h * D + (c + 1) * P],
                                         w_slice, start=True, stop=True)
                    last.then_inc(w_mm, 1)
                for h in range(FH):
                    last = pe.matmul(bank[6][0:1, h * G:(h + 1) * G], b_xt[:, h:h + 1], w_slice, start=True, stop=True)
                last.then_inc(w_mm, 1)

        (nrm, turned, turned_sb, lg, fx, mx_ch, exped, slw, fx_sb, done) = (
            sem(f"f1_{n}") for n in ("normalized", "turned", "turned_sb", "logits", "features", "softmax_chain", "exp",
                                     "slice_weights", "features_sb", "done"))
        stored = [dma_sem(f"f1_stored{b}") for b in (0, 1)]
        lgb = [T[2], T[3]]
        swb = [T[4], T[5]]
        fxb = [W[:, 4096:4096 + NPR * 132], W[:, 4096 + NPR * 132:4096 + 2 * NPR * 132]]

        def token_at(k):
            return (bank[6][:, k * 129:(k + 1) * 129]) if k < 3 else bank[7][:, 0:129]

        def heads(v):
            return v.rearrange("p (h g) -> p h g", g=G)

        def spread(v, n, g):
            return v.rearrange("p (h a) -> p h a", a=1).broadcast_to([n, v.shape[1], g])

        with nc.Block() as block:
            @block.sync
            def _(sp):
                def store(t, b, rows_, u):
                    sp.wait_ge(slw, t + 1)
                    sp.dma_start(dram["sw"][ds(t * P, P), :], swb[b]).then_inc(stored[b], 16)

                tiles(sp, [(0, store)])
                for b in (0, 1):
                    sp.wait_ge(stored[b], 16 * ((NT + 1 - b) // 2))

            @block.vector
            def _(dve):
                def normal(t, b, rows_, u):
                    dve.wait_ge(done, t + 1)
                    normalize(T[0][:, b * D:(b + 1) * D], t).then_inc(nrm, 1)

                def top(t, b, rows_, u):
                    dve.wait_ge(lg, t + 1)
                    c = Chain(dve, mx_ch, 4 * t)
                    m = T[6][:, b * 16:b * 16 + FH]
                    c.link(vec.tensor_reduce(m, heads(bank[2 + b][:, :]), AX, ALU.max))
                    vec.tensor_tensor(heads(lgb[b]), heads(bank[2 + b][:, :]), spread(m, P, G), ALU.subtract).then_inc(mx_ch, 1)

                def share(t, b, rows_, u):
                    dve.wait_ge(exped, t + 1)
                    if not first_use(u):
                        dve.wait_ge(stored[b], 16 * u)
                    c = Chain(dve, mx_ch, 4 * t + 2)
                    m = T[6][:, b * 16 + 8:b * 16 + 8 + FH]
                    c.link(vec.tensor_reduce(m, heads(lgb[b]), AX, ALU.add))
                    c.link(vec.reciprocal(m, m))
                    vec.tensor_tensor(heads(swb[b]), heads(lgb[b]), spread(m, P, G), ALU.mult).then_inc(slw, 1)

                tiles(dve, [(0, normal), (0, top), (0, share)])

            @block.scalar
            def _(s):
                for b in (0, 1):
                    for k in range(NPR):
                        act.copy(fxb[b][:, k * 132 + P:k * 132 + P + 1], ones[:, 0:1])

                def copy(t, b, rows_, u):
                    s.wait_ge(turned, t + 1)
                    act.copy(T[1][:, b * D:(b + 1) * D], bank[b][:, 0:D]).then_inc(turned_sb, 1)

                def exp(t, b, rows_, u):
                    s.wait_ge(mx_ch, 4 * t + 2)
                    act.activation(lgb[b], lgb[b], ACT.Exp).then_inc(exped, 1)

                def features(t, b, rows_, u):
                    s.wait_ge(fx, t + 1)
                    act.copy(fxb[b].rearrange("p (k c) -> p k c", c=132)[:, :, 0:P],
                             bank[4 + b][:, :].rearrange("p (k c) -> p k c", c=P)).then_inc(fx_sb, 1)

                tiles(s, [(0, copy), (0, exp), (0, features)])

            @block.tensor
            def _(t_):
                t_.sem_inc(done, 2)

                def turn1(t, b, rows_, u):
                    t_.wait_ge(nrm, t + 1)
                    turn(bank[b][:, 0:D], T[0][:, b * D:(b + 1) * D]).then_inc(turned, 1)

                def logits(t, b, rows_, u):
                    t_.wait_ge(turned_sb, t + 1)
                    product(bank[2 + b][:, :], T[1][:, b * D:(b + 1) * D], w_lg, last=False)
                    add_row(bank[2 + b][:, :], bl_row).then_inc(lg, 1)
                    product(bank[4 + b][:, :], T[1][:, b * D:(b + 1) * D], w_fx).then_inc(fx, 1)

                def tokens(t, b, rows_, u):
                    t_.wait_ge(slw, t + 1)
                    t_.wait_ge(fx_sb, t + 1)
                    for k in range(NPR):
                        last = pe.matmul(token_at(k), swb[b][0:rows_, k * P:(k + 1) * P], fxb[b][0:rows_, k * 132:k * 132 + 129],
                                         start=False, stop=False, skip_group_check=True)
                    last.then_inc(done, 1)

                pe.matmul(bank[6][:, 0:387], zeros[:, 0:P], W[:, 0:387], start=True, stop=False, skip_group_check=True)
                pe.matmul(bank[7][:, 0:129], zeros[:, 0:P], W[:, 0:129], start=True, stop=False, skip_group_check=True)
                tiles(t_, [(0, turn1), (0, logits), (1, tokens)])
                pe.matmul(bank[6][:, 0:387], zeros[:, 0:P], W[:, 0:387], start=False, stop=True, skip_group_check=True)
                pe.matmul(bank[7][:, 0:129], zeros[:, 0:P], W[:, 0:129], start=False, stop=True, skip_group_check=True)

        tok = BIG[:, 0:NPR * G]
        tok_t, q_t, k_t, v_t, prob = (BIG[0:G, 512 * (k + 1):512 * (k + 2)] for k in range(5))
        prob_t = BIG[0:G, 512 * 6:512 * 7]
        w_out = W[0:G, 0:FH * D]
        vw = TT[0:G, 0:FH * D]
        rows_out = TT[0:G, FH * D:2 * FH * D]
        mm_rows = W[:, 2048:2048 + NPR * D]
        a_in = dma_sem("fa_weights_in")
        a_ch, a_pe, a_ex, a_out = (sem(f"fa_{n}") for n in ("vector", "tensor", "exp", "packed"))
        SCALE = float(G) ** -0.5
        TOK_STEPS = NPR + 2 + 4 * NPR
        red = BIG[0:G, 5700:5700 + FH]
        with nc.Block() as block:
            @block.sync
            def _(sp):
                sp.dma_start(w_out.rearrange("c (h d) -> c h d", d=D), a["L0_ffn_W_out"].rearrange("(h c) d -> c h d", c=G)).then_inc(a_in, 16)
                bias_row(sp, 0, "L0_ffn_b_out", a_in)
                sp.wait_ge(a_out, 1)
                for par in range(2):
                    sp.dma_start(mm_rows[par * G:(par + 1) * G, :].rearrange("g (k d) -> g k d", d=D),
                                 rows_out.rearrange("g (k two d) -> g two k d", two=2, d=D)[:, par, :, :]).then_inc(a_in, 16)
                sp.wait_ge(a_in, 64)

            @block.vector
            def _(dve):
                c = Chain(dve, a_ch)
                wsum = tok_n[:, 0:NPR]
                rec_w = tok_n[:, NPR:2 * NPR]
                for k in range(NPR):
                    c.link(vec.tensor_copy(wsum[:, k:k + 1], token_at(k)[:, P:P + 1]))
                c.link(vec.tensor_scalar(rec_w, wsum, 1e-05, None, ALU.add))
                c.link(vec.reciprocal(rec_w, rec_w))
                for k in range(NPR):
                    c.link(vec.tensor_scalar(b_fx[:, k * G:(k + 1) * G], b_fx[:, k * G:(k + 1) * G], wsum[:, k:k + 1], None, ALU.mult))
                    for par in range(2):
                        r = slice(par * G, (par + 1) * G)
                        c.link(vec.tensor_tensor(tok[r, k * G:(k + 1) * G], token_at(k)[r, par * G:(par + 1) * G],
                                                 b_fx[r, k * G:(k + 1) * G], ALU.add))
                    c.link(vec.tensor_scalar(tok[:, k * G:(k + 1) * G], tok[:, k * G:(k + 1) * G], rec_w[:, k:k + 1], None, ALU.mult))
                assert c.n == TOK_STEPS
                dve.wait_ge(a_pe, 1)
                c.link(vec.tensor_copy(tok_t, bank[0][0:G, :]))
                for n, v in enumerate((q_t, k_t, v_t)):
                    dve.wait_ge(a_pe, 2 + n)
                    c.link(vec.tensor_copy(v, bank[1 + n][0:G, :]))
                dve.wait_ge(a_pe, 5)
                c.link(vec.tensor_reduce(red, heads(bank[4][0:G, :]), AX, ALU.max))
                c.link(vec.tensor_tensor(heads(prob), heads(bank[4][0:G, :]), spread(red, G, G), ALU.subtract))
                dve.wait_ge(a_ex, 1)
                c.link(vec.tensor_reduce(red, heads(prob), AX, ALU.add))
                c.link(vec.reciprocal(red, red))
                c.link(vec.tensor_tensor(heads(prob), heads(prob), spread(red, G, G), ALU.mult))
                dve.wait_ge(a_pe, 6)
                c.link(vec.tensor_copy(prob_t, bank[5][0:G, :]))
                for n in range(4):
                    dve.wait_ge(a_pe, 7 + n)
                    c.link(vec.tensor_copy(vw[:, n * 512:(n + 1) * 512], bank[n][0:G, :]))
                for n in range(4):
                    dve.wait_ge(a_pe, 11 + n)
                    c.link(vec.tensor_copy(rows_out[:, n * 512:(n + 1) * 512], bank[4 + n][0:G, :]))
                dve.nop().then_inc(a_out, 1)

            @block.scalar
            def _(s):
                s.wait_ge(a_ch, TOK_STEPS + 6)
                act.activation(prob, prob, ACT.Exp, scale=SCALE).then_inc(a_ex, 1)

            @block.tensor
            def _(t):
                t.wait_ge(a_ch, TOK_STEPS)
                for k in range(NPR):
                    last = pe.transpose(bank[0][0:G, k * P:(k + 1) * P], tok[:, k * G:(k + 1) * G], ident[:, :])
                last.then_inc(a_pe, 1)
                t.wait_ge(a_ch, TOK_STEPS + 1)
                for n, w in enumerate((w_qk, w_kk, w_vk)):
                    pe.matmul(bank[1 + n][0:G, :], w, tok_t, start=True, stop=True).then_inc(a_pe, 1)
                t.wait_ge(a_ch, TOK_STEPS + 4)
                for h in range(FH):
                    r = slice(h * G, (h + 1) * G)
                    last = pe.matmul(bank[4][0:G, r], q_t[:, r], k_t[:, r], start=True, stop=True)
                last.then_inc(a_pe, 1)
                t.wait_ge(a_ch, TOK_STEPS + 9)
                for h in range(FH):
                    r = slice(h * G, (h + 1) * G)
                    last = pe.transpose(bank[5][0:G, r], prob[:, r], ident[0:G, 0:G])
                last.then_inc(a_pe, 1)
                t.wait_ge(a_in, 32)
                for h in range(FH):
                    last = pe.matmul(bank[h // 2][0:G, (h % 2) * D:(h % 2 + 1) * D], v_t[:, h * G:(h + 1) * G],
                                     w_out[:, h * D:(h + 1) * D], start=True, stop=True)
                    if h % 2:
                        last.then_inc(a_pe, 1)
                t.wait_ge(a_ch, TOK_STEPS + 14)
                for h in range(FH):
                    last = pe.matmul(bank[4 + h // 2][0:G, (h % 2) * D:(h % 2 + 1) * D], prob_t[:, h * G:(h + 1) * G],
                                     vw[:, h * D:(h + 1) * D], start=True, stop=True)
                    if h % 2:
                        last.then_inc(a_pe, 1)

        turned, turned_sb, prod, done = (sem(f"f2_{n}") for n in ("turned", "turned_sb", "product", "done"))
        loaded = [dma_sem(f"f2_loaded{b}") for b in (0, 1)]
        with nc.Block() as block:
            @block.sync
            def _(sp):
                def load(t, b, rows_, u):
                    sp.wait_ge(done, t + 1)
                    sp.dma_start(T[b], dram["sw"][ds(t * P, P), :]).then_inc(loaded[b], 16)

                tiles(sp, [(0, load)])

            @block.scalar
            def _(s):
                def copy(t, b, rows_, u):
                    s.wait_ge(turned, t + 1)
                    act.copy(T[2 + b], bank[b][:, :]).then_inc(turned_sb, 1)

                tiles(s, [(0, copy)])

            @block.vector
            def _(dve):
                dve.sem_inc(done, 2)

                def add(t, b, rows_, u):
                    dve.wait_ge(prod, t + 1)
                    vec.tensor_tensor(tile_of(X, t), tile_of(X, t), bank[2 + b][:, 0:D], ALU.add).then_inc(done, 1)

                tiles(dve, [(0, add)])

            @block.tensor
            def _(t_):
                def turn1(t, b, rows_, u):
                    t_.wait_ge(loaded[b], 16 * (u + 1))
                    for k in range(NPR):
                        last = pe.transpose(bank[b][:, k * P:(k + 1) * P], T[b][:, k * P:(k + 1) * P], ident[:, :])
                    last.then_inc(turned, 1)

                def back(t, b, rows_, u):
                    t_.wait_ge(turned_sb, t + 1)
                    for k in range(NPR):
                        pe.matmul(bank[2 + b][:, 0:D], T[2 + b][:, k * P:(k + 1) * P], mm_rows[:, k * D:(k + 1) * D],
                                  start=k == 0, stop=False)
                    add_row(bank[2 + b][:, 0:D], brow[0:1, 0:D]).then_inc(prod, 1)

                tiles(t_, [(0, turn1), (1, back)])

        recycle()
        layer_norm_stats("ln2")
        RW = R * D
        w_rel = W[:, 0:H * RW]
        w_qkv = W[:, H * RW:H * RW + H * 3 * HID]
        g_pre = small[:, 0:H]
        assert H * RW + H * 3 * HID <= 6144
        w_in, ss_in = dma_sem("g0_weights_in"), sem("g0_weights_scaled")
        nrm, turned, turned_sb, done, squares, mov_a, mov_v, prods, qkv_ready = (
            sem(f"g0_{n}") for n in ("normalized", "turned", "turned_sb", "done", "squares", "moved_by_act",
                                     "moved_by_vec", "products", "qkv"))
        stored = [dma_sem(f"g0_stored{b}") for b in (0, 1)]
        xt_sb = [BIG[:, b * RW:(b + 1) * RW] for b in (0, 1)]
        qkv_sb = [T[2][:, 0:3 * HID], T[3][:, 0:3 * HID]]
        tab2_rows = dram["tab2"].rearrange("(r n) d -> n r d", r=R)
        with nc.Block() as block:
            @block.sync
            def _(sp):
                for r in range(R):
                    sp.dma_start(w_rel.rearrange("p (h r o) -> p h r o", h=H, r=R)[:, :, r, :],
                                 a["L1_gnn_weight"][r, :, :].rearrange("(h p) o -> p h o", p=P)).then_inc(w_in, 16)
                load_halves(sp, w_qkv, a["L1_mix_w_qkv"], w_in)
                with nc.allow_non_contiguous_dma(reason="gains as columns"):
                    sp.dma_start(g_pre, a["L1_mix_g_pre"].rearrange("(h p) -> p h", p=P)).then_inc(w_in, 16)

                def store(t, b, rows_, u):
                    sp.wait_ge(mov_a, t + 1)
                    sp.wait_ge(mov_v, t + 1)
                    sp.dma_start(tab2_rows[ds(t * P, P), :, :], xt_sb[b].rearrange("p (r d) -> p r d", r=R)).then_inc(stored[b], 16)
                    sp.dma_start(dram["qkv"][ds(t * P, P), :], qkv_sb[b]).then_inc(stored[b], 16)

                tiles(sp, [(0, store)])
                for b in (0, 1):
                    sp.wait_ge(stored[b], 32 * ((NT + 1 - b) // 2))

            @block.vector
            def _(dve):
                dve.wait_ge(w_in, 16 * (R + 2))
                for h in range(H):
                    vec.tensor_scalar(w_qkv[:, h * 3 * HID:(h + 1) * 3 * HID], w_qkv[:, h * 3 * HID:(h + 1) * 3 * HID],
                                      g_pre[:, h:h + 1], float(D) ** 0.5, ALU.mult, ALU.mult).then_inc(ss_in, 1)
                dve.sem_inc(done, 2)

                def normal(t, b, rows_, u):
                    dve.wait_ge(done, t + 1)
                    normalize(T[0][:, b * D:(b + 1) * D], t).then_inc(nrm, 1)

                def move(t, b, rows_, u):
                    if not first_use(u):
                        dve.wait_ge(stored[b], 32 * u)
                    for k in (1, 3):
                        dve.wait_ge(prods, 4 * t + k + 1)
                        ins = vec.tensor_copy(xt_sb[b][:, k * 512:(k + 1) * 512], bank[2 + k][:, :])
                    ins.then_inc(mov_v, 1)
                    dve.wait_ge(mov_v, t + 1)
                    dve.wait_ge(mov_a, t + 1)
                    dve.wait_ge(squares, t + 1)
                    dve.sem_inc(done, 1)

                tiles(dve, [(0, normal), (1, move)])

            @block.scalar
            def _(s):
                def copy(t, b, rows_, u):
                    s.wait_ge(turned, t + 1)
                    act.copy(T[1][:, b * D:(b + 1) * D], bank[b][:, 0:D]).then_inc(turned_sb, 1)
                    s.wait_ge(nrm, t + 1)
                    if not first_use(t):
                        s.wait_ge(squares, t)
                    s.nop(nofuse=True)
                    act.activation(T[4][:, 0:D], T[0][:, b * D:(b + 1) * D], ACT.Square,
                                   accum_out=sumsq[:, ds(t, 1)]).then_inc(squares, 1)

                def move(t, b, rows_, u):
                    if not first_use(u):
                        s.wait_ge(stored[b], 32 * u)
                    for k in (0, 2):
                        s.wait_ge(prods, 4 * t + k + 1)
                        act.copy(xt_sb[b][:, k * 512:(k + 1) * 512], bank[2 + k][:, :])
                    s.wait_ge(qkv_ready, t + 1)
                    act.copy(qkv_sb[b], bank[6 + b][:, 0:3 * HID]).then_inc(mov_a, 1)

                tiles(s, [(0, copy), (1, move)])

            @block.tensor
            def _(t_):
                t_.wait_ge(w_in, 16 * (R + 2))
                t_.wait_ge(ss_in, H)

                def turn1(t, b, rows_, u):
                    t_.wait_ge(nrm, t + 1)
                    turn(bank[b][:, 0:D], T[0][:, b * D:(b + 1) * D]).then_inc(turned, 1)

                def rels(t, b, rows_, u):
                    t_.wait_ge(turned_sb, t + 1)
                    lhs = T[1][:, b * D:(b + 1) * D]
                    if not (isinstance(t, int) and t == 0):
                        t_.wait_ge(mov_a, t)
                        t_.wait_ge(mov_v, t)
                    for k in range(4):
                        product(bank[2 + k][:, :], lhs, w_rel, (k * 512, (k + 1) * 512)).then_inc(prods, 1)
                    product(bank[6 + b][:, 0:3 * HID], lhs, w_qkv).then_inc(qkv_ready, 1)

                tiles(t_, [(0, turn1), (1, rels)])

        recycle()
        inv_n = small[:, 64:64 + NT]
        kmax = T[4][:, 0:P]
        krow = T[5][:, 0:P]
        mem_k, mem_v = T[6][0:MEM, 0:P], T[7][0:MEM, 0:132]
        mem_kt = small[:, 128:128 + MEM]
        col = [small[:, 136 + k:137 + k] for k in range(4)]
        w_om, cw = W[:, 0:D], W[:, D:2 * D]
        g_out = W[:, 2 * D:3 * D]
        diag = W[:, 3 * D:3 * D + P]
        m_in, m_ch, m_rt, m_pe, km_ch = (dma_sem("h0_weights_in"), sem("h0_chain"), sem("h0_root"), sem("h0_tensor"),
                                         sem("h0_maxima"))
        loaded = [dma_sem(f"h0_loaded{b}") for b in (0, 1)]
        with nc.Block() as block:
            @block.sync
            def _(sp):
                sp.dma_start(w_om, a["L1_mix_w_out"]).then_inc(m_in, 16)
                bias_row(sp, 0, "L1_mix_b_out", m_in)
                sp.dma_start(g_out, a["L1_mix_g_out"].rearrange("(a d) -> a d", a=1).broadcast_to([P, D])).then_inc(m_in, 16)
                sp.dma_start(mem_kt, a["L1_mix_mem_kv"][0, :, :, :].rearrange("h d m -> (h d) m")).then_inc(m_in, 16)
                with nc.allow_non_contiguous_dma(reason="memories as rows"):
                    sp.dma_start(mem_k, a["L1_mix_mem_kv"][0, :, :, :].rearrange("h d m -> m (h d)")).then_inc(m_in, 16)
                    sp.dma_start(mem_v[:, 0:P], a["L1_mix_mem_kv"][1, :, :, :].rearrange("h d m -> m (h d)")).then_inc(m_in, 16)

                def load(t, b, rows_, u):
                    if not first_use(u):
                        sp.wait_ge(km_ch, t - 1)
                    sp.dma_start(T[b][:, 0:HID], dram["qkv"][ds(t * P, P), HID:2 * HID]).then_inc(loaded[b], 16)

                tiles(sp, [(0, load)])

            @block.scalar
            def _(s):
                act.activation(inv_n, sumsq[:, :], ACT.Sqrt).then_inc(m_rt, 1)

            @block.vector
            def _(dve):
                c = Chain(dve, m_ch)
                c.link(vec.memset(kmax, -3.0e38))
                dve.wait_ge(m_rt, 1)
                c.link(vec.tensor_scalar(inv_n, inv_n, 1e-12, None, ALU.max))
                c.link(vec.reciprocal(inv_n, inv_n))

                def largest(t, b, rows_, u):
                    dve.wait_ge(loaded[b], 16 * (u + 1))
                    if not (isinstance(t, int) and t == 0):
                        dve.wait_ge(km_ch, t)
                    vec.scalar_tensor_tensor(kmax[0:rows_, :], T[b][0:rows_, 0:HID], inv_n[0:rows_, ds(t, 1)], kmax[0:rows_, :],
                                             ALU.mult, ALU.max).then_inc(km_ch, 1)

                tiles(dve, [(0, largest)])
                dve.wait_ge(m_in, 16 * 6)
                c.link(vec.tensor_reduce(col[0], mem_kt, AX, ALU.max))
                dve.wait_ge(m_pe, 1)
                c.link(vec.tensor_reduce(col[1], bank[0][:, 0:P], AX, ALU.max))
                c.link(vec.tensor_tensor(col[0], col[0], col[1], ALU.max))
                c.link(vec.tensor_scalar(diag, ident[:, :], col[0], None, ALU.mult))
                dve.wait_ge(m_pe, 2)
                c.link(vec.tensor_copy(krow, bank[1][:, 0:P]))

            @block.tensor
            def _(t):
                t.wait_ge(km_ch, NT)
                pe.transpose(bank[0][:, 0:P], kmax, ident[:, :]).then_inc(m_pe, 1)
                t.wait_ge(m_ch, 7)
                pe.matmul(bank[1][:, 0:P], ones[:, :], diag, start=True, stop=True).then_inc(m_pe, 1)

        kd, ke, vs_, done, mm_ch, mm_ex = (sem(f"h1_{n}") for n in ("lowered", "exp", "values", "done", "memory", "memory_exp"))
        loaded = [dma_sem(f"h1_loaded{b}") for b in (0, 1)]
        vb = [T[2][:, 0:132], T[3][:, 0:132]]
        with nc.Block() as block:
            @block.sync
            def _(sp):
                def load(t, b, rows_, u):
                    sp.wait_ge(done, t + 1)
                    sp.dma_start(T[b][:, 0:2 * HID], dram["qkv"][ds(t * P, P), HID:3 * HID]).then_inc(loaded[b], 16)

                tiles(sp, [(0, load)])

            @block.vector
            def _(dve):
                vec.memset(mem_v[:, P:P + 1], 1.0)
                vec.tensor_tensor(mem_k, mem_k, krow[0:MEM, :], ALU.subtract).then_inc(mm_ch, 1)

                def lower(t, b, rows_, u):
                    dve.wait_ge(loaded[b], 16 * (u + 1))
                    vec.scalar_tensor_tensor(T[b][:, 256:256 + HID], T[b][:, 0:HID], inv_n[:, ds(t, 1)], krow,
                                             ALU.mult, ALU.subtract).then_inc(kd, 1)
                    vec.tensor_scalar(vb[b][:, 0:HID], T[b][:, HID:2 * HID], inv_n[:, ds(t, 1)], None, ALU.mult).then_inc(vs_, 1)

                tiles(dve, [(0, lower)])

            @block.scalar
            def _(s):
                for b in (0, 1):
                    act.copy(vb[b][:, P:P + 1], ones[:, 0:1])
                s.wait_ge(mm_ch, 1)
                act.activation(mem_k, mem_k, ACT.Exp).then_inc(mm_ex, 1)

                def exp(t, b, rows_, u):
                    s.wait_ge(kd, t + 1)
                    act.activation(T[b][:, 256:256 + HID], T[b][:, 256:256 + HID], ACT.Exp).then_inc(ke, 1)

                tiles(s, [(0, exp)])

            @block.tensor
            def _(t_):
                t_.sem_inc(done, 2)
                t_.wait_ge(mm_ex, 1)
                pe.matmul(bank[2][:, 0:P + 1], mem_k, mem_v[:, 0:P + 1], start=True, stop=False, skip_group_check=True)

                def context(t, b, rows_, u):
                    t_.wait_ge(ke, t + 1)
                    t_.wait_ge(vs_, t + 1)
                    pe.matmul(bank[2][:, 0:P + 1], T[b][0:rows_, 256:256 + HID], vb[b][0:rows_, 0:P + 1],
                              start=False, stop=False, skip_group_check=True).then_inc(done, 1)

                tiles(t_, [(0, context)])
                pe.matmul(bank[2][:, 0:P + 1], zeros[:, 0:P], zeros[:, 0:P + 1], start=False, stop=True, skip_group_check=True)

        n_ch, n_pe = sem("h2_chain"), sem("h2_tensor")
        with nc.Block() as block:
            @block.vector
            def _(dve):
                c = Chain(dve, n_ch)
                c.link(vec.tensor_copy(col[2], bank[2][:, P:P + 1]))
                c.link(vec.reciprocal(col[2], col[2]))
                for j in range(MH):
                    c.link(vec.tensor_scalar(diag[:, j * MD:(j + 1) * MD], bank[2][:, j * MD:(j + 1) * MD], hmask[:, j:j + 1],
                                             col[2], ALU.mult, ALU.mult))
                dve.wait_ge(n_pe, 1)
                c.link(vec.tensor_copy(bdiag[:, 0:P], bank[3][:, 0:P]))
                dve.wait_ge(n_pe, 2)
                c.link(vec.tensor_copy(cw, bank[4][:, 0:D]))

            @block.tensor
            def _(t):
                t.wait_ge(n_ch, 2 + MH)
                pe.transpose(bank[3][:, 0:P], diag, ident[:, :]).then_inc(n_pe, 1)
                t.wait_ge(n_ch, 3 + MH)
                pe.matmul(bank[4][:, 0:D], bdiag[:, 0:P], w_om, start=True, stop=True).then_inc(n_pe, 1)

        recycle()
        qch, qex, qn, qt, qts, outp, ysb, done = (sem(f"h3_{n}") for n in ("chain", "exp", "softmaxed", "turned", "turned_sb",
                                                                         "out", "stored", "done"))
        loaded = [dma_sem(f"h3_loaded{b}") for b in (0, 1)]
        QSCALE = float(MD) ** -0.5

        def mheads(v):
            return v.rearrange("p (h d) -> p h d", d=MD)

        def mspread(v):
            return v.rearrange("p (h a) -> p h a", a=1).broadcast_to([P, MH, MD])

        with nc.Block() as block:
            @block.sync
            def _(sp):
                def load(t, b, rows_, u):
                    sp.wait_ge(done, t + 1)
                    sp.dma_start(T[b][:, 0:HID], dram["qkv"][ds(t * P, P), 0:HID]).then_inc(loaded[b], 16)

                tiles(sp, [(0, load)])

            @block.vector
            def _(dve):
                def low(t, b, rows_, u):
                    dve.wait_ge(loaded[b], 16 * (u + 1))
                    c = Chain(dve, qch, 5 * t)
                    q, m = T[b][:, 0:HID], T[b][:, 384:384 + MH]
                    c.link(vec.tensor_scalar(q, q, inv_n[:, ds(t, 1)], None, ALU.mult))
                    c.link(vec.tensor_reduce(m, mheads(q), AX, ALU.max))
                    vec.tensor_tensor(mheads(q), mheads(q), mspread(m), ALU.subtract).then_inc(qch, 1)

                def share(t, b, rows_, u):
                    dve.wait_ge(qex, t + 1)
                    c = Chain(dve, qch, 5 * t + 3)
                    q, m = T[b][:, 0:HID], T[b][:, 384:384 + MH]
                    c.link(vec.tensor_reduce(m, mheads(q), AX, ALU.add))
                    c.link(vec.reciprocal(m, m))
                    vec.scalar_tensor_tensor(mheads(T[2 + b][:, 0:HID]), mheads(q), QSCALE, mspread(m), ALU.mult, ALU.mult).then_inc(qn, 1)

                tiles(dve, [(0, low), (0, share)])

            @block.scalar
            def _(s):
                def exp(t, b, rows_, u):
                    s.wait_ge(qch, 5 * t + 3)
                    act.activation(T[b][:, 0:HID], T[b][:, 0:HID], ACT.Exp).then_inc(qex, 1)

                def copy(t, b, rows_, u):
                    s.wait_ge(qt, t + 1)
                    act.copy(T[4 + b][:, 0:HID], bank[b][:, 0:HID]).then_inc(qts, 1)

                def keep(t, b, rows_, u):
                    s.wait_ge(outp, t + 1)
                    act.copy(tile_of(ACC, t), bank[2 + b][:, 0:D]).then_inc(ysb, 1)
                    s.wait_ge(ysb, t + 1)
                    s.nop(nofuse=True)
                    act.activation(T[6][:, b * D:(b + 1) * D], tile_of(ACC, t), ACT.Square, accum_out=sumsq[:, ds(t, 1)]).then_inc(done, 1)
                    s.wait_ge(done, t + 3)

                s.sem_inc(done, 2)
                tiles(s, [(0, exp), (0, copy), (0, keep)])

            @block.tensor
            def _(t_):
                t_.wait_ge(m_in, 32)

                def turn1(t, b, rows_, u):
                    t_.wait_ge(qn, t + 1)
                    pe.transpose(bank[b][:, 0:HID], T[2 + b][:, 0:HID], ident[:, :]).then_inc(qt, 1)

                def out_rows(t, b, rows_, u):
                    t_.wait_ge(qts, t + 1)
                    pe.matmul(bank[2 + b][:, 0:D], T[4 + b][:, 0:HID], cw, start=True, stop=False)
                    add_row(bank[2 + b][:, 0:D], brow[0:1, 0:D]).then_inc(outp, 1)

                tiles(t_, [(0, turn1), (0, out_rows)])

        r_ch, r_rt = sem("h4_chain"), sem("h4_root")
        with nc.Block() as block:
            @block.scalar
            def _(s):
                act.activation(inv_n, sumsq[:, :], ACT.Sqrt).then_inc(r_rt, 1)

            @block.vector
            def _(dve):
                c = Chain(dve, r_ch)
                dve.wait_ge(r_rt, 1)
                c.link(vec.tensor_scalar(inv_n, inv_n, 1e-12, None, ALU.max))
                c.link(vec.reciprocal(inv_n, inv_n))
                c.link(vec.tensor_scalar(inv_n, inv_n, float(D) ** 0.5, None, ALU.mult))
                y, x = wide(ACC[:, :]), wide(X[:, :])
                c.link(vec.tensor_tensor(y, y, per_tile(inv_n), ALU.mult))
                c.link(vec.tensor_tensor(y, y, per_feature(g_out), ALU.mult))
                c.link(vec.tensor_tensor(mean, mean, rstd[:, :], ALU.mult))
                c.link(vec.tensor_tensor(y, y, x, ALU.add))
                c.link(vec.tensor_tensor(x, x, per_tile(rstd[:, :]), ALU.mult))
                c.link(vec.tensor_tensor(y, y, x, ALU.add))
                c.link(vec.tensor_tensor(x, y, per_tile(mean), ALU.subtract))

        recycle()
        make_pairs(0)
        recycle()
        aggregate("agg2", dram["tab2"], D, dram["off0"], False, False)
        gb_in, gb_ch = dma_sem("g2_bias_in"), sem("g2_chain")
        with nc.Block() as block:
            @block.sync
            def _(sp):
                sp.dma_start(W[:, 0:D], a["L1_gnn_bias"].rearrange("(a d) -> a d", a=1).broadcast_to([P, D])).then_inc(gb_in, 16)

            @block.vector
            def _(dve):
                c = Chain(dve, gb_ch)
                dve.wait_ge(gb_in, 16)
                y, x = wide(ACC[:, :]), wide(X[:, :])
                c.link(vec.tensor_tensor(y, y, per_feature(W[:, 0:D]), ALU.add))
                c.link(vec.scalar_tensor_tensor(X[:, :], ACC[:, 0:NT * D], 0.0, X[:, :], ALU.max, ALU.add))

        recycle()
        layer_norm_stats("ln3")
        wr, br = small[:, 0:H * EX], brow[0:1, 2 * D:2 * D + EX]
        mean_row = brow[0:1, 0:D]
        mean_t = small[:, 32:32 + H]
        def rr(k):
            return brow[0:1, 2 * D + 16 * k:2 * D + 16 * k + EX]

        lrow, erow, wrow, top_v, oh0, oh1, dense, iorow = (rr(k) for k in range(1, 9))
        s1 = brow[0:1, 2 * D + 160:2 * D + 168]
        top_i = brow[0:1, 2 * D + 176:2 * D + 184].bitcast(mybir.dt.uint32)
        pick = brow[0:1, 2 * D + 192:2 * D + 196]
        picks = small[:, 40:44]
        dense_t, oh_t = small[0:EX, 44:45], small[0:EX, 45:47]
        b1_all, b2_all = T[0][0:EX, :], T[1][0:EX, 0:D]
        b1_col = small[:, 48:48 + 2 * (FF // P)]
        e_idx = small[:, 64:64 + 12].bitcast(I32)
        e_f = small[:, 80:92]
        pcol = small[:, 96:97]
        FC = FF // P
        w1 = [W[:, e * H * FF:(e + 1) * H * FF] for e in (0, 1)]
        w2 = [W[:, 2 * H * FF + e * FC * D:2 * H * FF + (e + 1) * FC * D] for e in (0, 1)]
        b2_row = brow[0:1, 3 * D:4 * D]
        CAP = math.ceil(N * 1.25 / EX) / N
        i_in, i_ch, i_pe, i_ex, i_w, i_p = (dma_sem("i0_in"), sem("i0_chain"), sem("i0_tensor"), sem("i0_exp"),
                                            dma_sem("i0_weights"), sem("i0_constants"))
        norm_t, summed_t = sem("i0_normalized"), sem("i0_summed")
        with nc.Block() as block:
            @block.sync
            def _(sp):
                for h in range(H):
                    sp.dma_start(wr[:, h * EX:(h + 1) * EX], a["L1_ffn_Wr"][h * P:(h + 1) * P, :]).then_inc(i_in, 16)
                sp.dma_start(br, a["L1_ffn_br"].rearrange("(a n) -> a n", a=1)).then_inc(i_in, 16)
                sp.dma_start(b1_all, a["L1_ffn_b1"]).then_inc(i_in, 16)
                sp.dma_start(b2_all, a["L1_ffn_b2"]).then_inc(i_in, 16)

            @block.vector
            def _(dve):
                dve.wait_ge(i_in, 80)

                def normal(t, b, rows_, u):
                    if not first_use(u):
                        dve.wait_ge(summed_t, t - 1)
                    normalize(T[2][:, b * D:(b + 1) * D], t).then_inc(norm_t, 1)

                tiles(dve, [(0, normal)])
                c = Chain(dve, i_ch)
                dve.wait_ge(i_pe, 1)
                c.link(vec.tensor_scalar(mean_row, bank[0][0:1, 0:D], 1.0 / N, None, ALU.mult))
                dve.wait_ge(i_pe, 2)
                c.link(vec.tensor_copy(mean_t, bank[1][:, 0:H]))
                dve.wait_ge(i_pe, 3)
                c.link(vec.tensor_tensor(lrow, bank[2][0:1, 0:EX], br, ALU.add))

                def softmax(dst, src, n, turn_):
                    c.link(vec.tensor_reduce(s1[:, 0:1], src, AX, ALU.max))
                    c.link(vec.tensor_scalar(dst, src, s1[:, 0:1], None, ALU.subtract))
                    dve.nop().then_inc(i_p, 1)
                    dve.wait_ge(i_ex, turn_)
                    c.link(vec.tensor_reduce(s1[:, 0:1], dst, AX, ALU.add))
                    c.link(vec.reciprocal(s1[:, 1:2], s1[:, 0:1]))
                    c.link(vec.tensor_scalar(dst, dst, s1[:, 1:2], None, ALU.mult))

                softmax(erow, lrow, EX, 1)
                c.link(vec.tensor_scalar(lrow, erow, CAP, None, ALU.min))
                softmax(wrow, lrow, EX, 2)
                dve.nop(nofuse=True)
                c.link(vec.max(top_v, wrow))
                c.link(vec.max_index(top_i, top_v, wrow))
                c.link(vec.tensor_copy(pick[:, 0:2], top_i[:, 0:2]))
                softmax(pick[:, 2:4], top_v[:, 0:2], 2, 3)
                c.link(vec.tensor_scalar(oh0, iota[0:1, 0:EX], pick[:, 0:1], None, ALU.is_equal))
                c.link(vec.tensor_scalar(oh1, iota[0:1, 0:EX], pick[:, 1:2], None, ALU.is_equal))
                c.link(vec.tensor_scalar(dense, oh0, pick[:, 2:3], None, ALU.mult))
                c.link(vec.scalar_tensor_tensor(dense, oh1, pick[:, 3:4], dense, ALU.mult, ALU.add))
                dve.nop().then_inc(i_p, 1)
                dve.wait_ge(i_pe, 4)
                c.link(vec.tensor_copy(picks, bank[3][:, 0:4]))
                c.link(vec.tensor_copy(dense_t, bank[4][0:EX, 0:1]))
                c.link(vec.tensor_copy(oh_t, bank[4][0:EX, 1:3]))
                dve.nop().then_inc(i_p, 1)
                for e in (0, 1):
                    for h in range(H):
                        c.link(vec.tensor_scalar(e_f[:, e * 6 + h:e * 6 + h + 1], picks[:, e:e + 1], float(D), float(h * P), ALU.mult, ALU.add))
                    for k in range(FC):
                        c.link(vec.tensor_scalar(e_f[:, e * 6 + 2 + k:e * 6 + 3 + k], picks[:, e:e + 1], float(FF), float(k * P), ALU.mult, ALU.add))
                c.link(vec.tensor_scalar(e_f, e_f, qcol[:, 0:1], None, ALU.add))
                vec.tensor_copy(e_idx, e_f).then_inc(i_p, 1)
                dve.wait_ge(i_pe, 5)
                c.link(vec.tensor_copy(b1_col, bank[5][:, 0:2 * FC]))
                c.link(vec.tensor_copy(b2_row, bank[6][0:1, 0:D]))
                dve.wait_ge(i_w, 16 * 12)
                for e in (0, 1):
                    c.link(vec.tensor_scalar(w2[e], w2[e], picks[:, 2 + e:3 + e], None, ALU.mult))

            @block.scalar
            def _(s):
                for k, v in enumerate((erow, wrow, pick[:, 2:4])):
                    s.wait_ge(i_p, k + 1)
                    act.activation(v, v, ACT.Exp).then_inc(i_ex, 1)

            @block.gpsimd
            def _(pool):
                pool.wait_ge(i_p, 6)
                w1_rows = a["L1_ffn_W1"].rearrange("e c f -> (e c) f")
                w2_rows = a["L1_ffn_W2"].rearrange("e f d -> (e f) d")
                for e in (0, 1):
                    for k in range(H + FC):
                        dst = w1[e][:, k * FF:(k + 1) * FF] if k < H else w2[e][:, (k - H) * D:(k - H + 1) * D]
                        pool.indirect_dma_start(dst, None, w1_rows if k < H else w2_rows,
                                                bass.IndirectOffsetOnAxis(ap=e_idx[:, e * 6 + k:e * 6 + k + 1], axis=0)).then_inc(i_w, 16)
                pool.wait_ge(i_w, 16 * 12)

            @block.tensor
            def _(t_):
                def column_sum(t, b, rows_, u):
                    t_.wait_ge(norm_t, t + 1)
                    pe.matmul(bank[0][0:1, 0:D], ones[0:rows_, 0:1], T[2][0:rows_, b * D:(b + 1) * D],
                              start=False, stop=False, skip_group_check=True).then_inc(summed_t, 1)

                pe.matmul(bank[0][0:1, 0:D], zeros[:, 0:1], W[:, 0:D], start=True, stop=False, skip_group_check=True)
                tiles(t_, [(0, column_sum)])
                pe.matmul(bank[0][0:1, 0:D], zeros[:, 0:1], W[:, 0:D], start=False, stop=True, skip_group_check=True).then_inc(i_pe, 1)
                t_.wait_ge(i_ch, 1)
                for h in range(H):
                    last = pe.matmul(bank[1][:, h:h + 1], mean_row[:, h * P:(h + 1) * P], ones[0:1, 0:1], start=True, stop=True)
                last.then_inc(i_pe, 1)
                t_.wait_ge(i_ch, 2)
                for h in range(H):
                    last = pe.matmul(bank[2][0:1, 0:EX], mean_t[:, h:h + 1], wr[:, h * EX:(h + 1) * EX], start=h == 0, stop=h == H - 1)
                last.then_inc(i_pe, 1)
                t_.wait_ge(i_p, 4)
                pe.matmul(bank[3][:, 0:4], ones[0:1, :], pick, start=True, stop=True)
                for k, v in enumerate((dense, oh0, oh1)):
                    last = pe.matmul(bank[4][0:EX, k:k + 1], v, ones[0:1, 0:1], start=True, stop=True)
                last.then_inc(i_pe, 1)
                t_.wait_ge(i_p, 5)
                for e in (0, 1):
                    for k in range(FC):
                        pe.matmul(bank[5][:, e * FC + k:e * FC + k + 1], b1_all[:, k * P:(k + 1) * P], oh_t[:, e:e + 1], start=True, stop=True)
                pe.matmul(bank[6][0:1, 0:D], dense_t, b2_all, start=True, stop=True).then_inc(i_pe, 1)

        nrm, turned, turned_sb, hid, act_out, prod, done, ready = (
            sem(f"i1_{n}") for n in ("normalized", "turned", "turned_sb", "hidden", "gelu", "product", "done", "ready"))
        hsb = [[T[2], T[3]], [T[4], T[5]]]
        with nc.Block() as block:
            @block.vector
            def _(dve):
                dve.sem_inc(done, 2)

                def normal(t, b, rows_, u):
                    dve.wait_ge(done, t + 1)
                    normalize(T[0][:, b * D:(b + 1) * D], t).then_inc(nrm, 1)

                def add(t, b, rows_, u):
                    dve.wait_ge(prod, t + 1)
                    vec.tensor_tensor(tile_of(ACC, t), T[0][:, b * D:(b + 1) * D], bank[6 + b][:, 0:D], ALU.add).then_inc(done, 1)

                tiles(dve, [(0, normal), (1, add)])

            @block.scalar
            def _(s):
                def copy(t, b, rows_, u):
                    s.wait_ge(turned, t + 1)
                    act.copy(T[1][:, b * D:(b + 1) * D], bank[b][:, 0:D]).then_inc(turned_sb, 1)

                def gelu(t, b, rows_, u):
                    for e in (0, 1):
                        s.wait_ge(hid, 2 * t + e + 1)
                        for k in range(FC):
                            ins = act.activation(hsb[e][b][:, k * P:(k + 1) * P], bank[2 + 2 * e + b][:, k * P:(k + 1) * P],
                                                 ACT.Gelu, bias=b1_col[:, e * FC + k:e * FC + k + 1])
                        ins.then_inc(act_out, 1)

                tiles(s, [(0, copy), (0, gelu)])

            @block.tensor
            def _(t_):
                def turn1(t, b, rows_, u):
                    t_.wait_ge(nrm, t + 1)
                    turn(bank[b][:, 0:D], T[0][:, b * D:(b + 1) * D]).then_inc(turned, 1)

                def hidden(t, b, rows_, u):
                    t_.wait_ge(turned_sb, t + 1)
                    for e in (0, 1):
                        for k in range(FC):
                            for h in range(H):
                                last = pe.matmul(bank[2 + 2 * e + b][:, k * P:(k + 1) * P], w1[e][:, h * FF + k * P:h * FF + (k + 1) * P],
                                                 T[1][:, b * D + h * P:b * D + (h + 1) * P], start=h == 0, stop=h == H - 1)
                        last.then_inc(hid, 1)

                def outputs(t, b, rows_, u):
                    for e in (0, 1):
                        t_.wait_ge(act_out, 2 * t + e + 1)
                        for k in range(FC):
                            pe.matmul(bank[6 + b][:, 0:D], hsb[e][b][:, k * P:(k + 1) * P], w2[e][:, k * D:(k + 1) * D],
                                      start=e == 0 and k == 0, stop=False)
                    add_row(bank[6 + b][:, 0:D], b2_row).then_inc(prod, 1)

                tiles(t_, [(0, turn1), (0, hidden), (1, outputs)])

        recycle()
        z_in, z_ch = dma_sem("z_in"), sem("z_chain")
        layer_norm_stats("ln4", ACC)
        with nc.Block() as block:
            @block.sync
            def _(sp):
                for k, n in enumerate(("gamma", "beta")):
                    sp.dma_start(W[:, k * D:(k + 1) * D], a[f"L1_ffn_{n}"].rearrange("(a d) -> a d", a=1).broadcast_to([P, D])).then_inc(z_in, 16)

            @block.vector
            def _(dve):
                c = Chain(dve, z_ch)
                dve.wait_ge(z_in, 32)
                y, x = wide(ACC[:, :]), wide(X[:, :])
                c.link(vec.tensor_tensor(y, y, per_tile(mean), ALU.subtract))
                c.link(vec.tensor_tensor(y, y, per_tile(rstd[:, :]), ALU.mult))
                c.link(vec.tensor_tensor(y, y, per_feature(W[:, 0:D]), ALU.mult))
                c.link(vec.tensor_tensor(x, x, per_feature(W[:, D:2 * D]), ALU.add))
                c.link(vec.tensor_tensor(x, x, y, ALU.add))

        stored = sem("stored")
        with nc.Block() as block:
            @block.sync
            def _(sp):
                full = out[0:(NT - 1) * P, :].rearrange("(t p) d -> p t d", p=P)
                sp.dma_start(full, X[:, 0:(NT - 1) * D].rearrange("p (t d) -> p t d", d=D)).then_inc(stored, 16)
                sp.dma_start(out[(NT - 1) * P:N, :], X[0:TAIL, (NT - 1) * D:NT * D]).then_inc(stored, 16)
                sp.wait_ge(stored, 32)


_SCRATCH_KIND = "Internal"


def kernel(**inputs):
    import numpy as np
    import concourse.bacc as bacc
    from concourse.bass_utils import run_bass_kernel_spmd

    nc = bacc.Bacc("TRN2", target_bir_lowering=False, num_devices=1)
    arrays, a = {}, {}
    for name, value in inputs.items():
        v = np.ascontiguousarray(value)
        arrays[f"in_{name}"] = v
        a[name] = nc.dram_tensor(f"in_{name}", v.shape, mybir.dt.from_np(v.dtype), kind="ExternalInput").ap()
    N, D = inputs["x"].shape
    E = inputs["src"].shape[0]
    R = inputs["L1_gnn_weight"].shape[0]
    NT = -(-N // P)
    J = -(-E // P)
    QB = -(-(J + NT - 1) // P)
    NPAD = NT * P
    INNER = inputs["L0_ffn_W_fx"].shape[1]
    scratch = {
        "rec": ([P * J, 4], F32), "rec_by_src": ([P * J, 4], F32), "rec_by_dst": ([P * J, 4], F32),
        "off0": ([QB * P], I32), "off1": ([QB * P], I32), "deg_in": ([(NT + 1) * P], F32),
        "tab0": ([NPAD, D + 1], F32), "tab1": ([NPAD, D], F32), "tab2": ([R * NPAD, D], F32),
        "sw": ([NPAD, INNER], F32), "qkv": ([NPAD, 3 * P], F32), "route": ([1, 64], F32),
    }
    dram = {n: nc.dram_tensor(n, s, d, kind=_SCRATCH_KIND).ap() for n, (s, d) in scratch.items()}
    out = nc.dram_tensor("out", [N, D], F32, kind="ExternalOutput").ap()
    gps_layers(nc, a, dram, out)
    r = run_bass_kernel_spmd(nc, [arrays], core_ids=[0])
    return r.results[0]["out"]
```

```python
import math
from contextlib import ExitStack

import concourse.bass as bass
from concourse import mybir

F32 = mybir.dt.float32
I32 = mybir.dt.int32
ALU = mybir.AluOpType
ACT = mybir.ActivationFunctionType
AX = mybir.AxisListType.X
P = 128
ds = bass.ds

LN_EPS = 1e-05
NORM_EPS = 1e-12
RING = 16
HALF = RING // 2
GROUP = 8
GROUPS = 3
SLOTS = GROUP * GROUPS


class Chain:

    def __init__(self, eng, sem, base=0):
        self.eng, self.sem, self.base, self.n = eng, sem, base, 0

    def link(self, ins):
        self.n += 1
        ins.then_inc(self.sem, 1)
        self.eng.wait_ge(self.sem, self.base + self.n)


def each(eng, n, unroll, body):
    if n >= unroll:
        with eng.Fori(0, n // unroll) as i:
            for d in range(unroll):
                body(i * unroll + d)
    for k in range(n - n % unroll, n):
        body(k)


def gps_layers(nc, a, dram, out):
    N, D = a["x"].shape
    E = a["src"].shape[0]
    H = D // P
    NT = -(-N // P)
    NPAD = NT * P
    TAIL = N - (NT - 1) * P
    J = -(-E // P)
    JTAIL = E - (P - 1) * J
    CB = -(-J // P)
    QR = -(-(J + NT - 1) // SLOTS)
    QB = -(-QR * SLOTS // P)
    NB = NT + 1
    TW = D + 4
    R = a["L1_gnn_weight"].shape[0]
    INNER = a["L0_ffn_W_fx"].shape[1]
    G = a["L0_ffn_W_slice"].shape[1]
    FH = INNER // G
    HID = a["L1_mix_w_out"].shape[0]
    MEM = a["L1_mix_mem_kv"].shape[3]
    MH = a["L1_mix_mem_kv"].shape[1]
    MD = HID // MH
    EX = a["L1_ffn_Wr"].shape[1]
    FF = a["L1_ffn_W1"].shape[2]
    KH = 8
    KD = D // KH
    assert D == 256 and G == 64 and HID == P and 0 < JTAIL <= J

    ctx = ExitStack()
    with ctx:
        def sb(name, shape, dt=F32):
            return ctx.enter_context(nc.sbuf_tensor(name, shape, dt))

        def dma_sem(name):
            return ctx.enter_context(nc.semaphore(name))

        in_use = []

        def sem(name):
            held = nc.semaphore(name)
            in_use.append((held, held.__enter__()))
            return in_use[-1][1]

        def recycle():
            with nc.Block() as block:
                @block.sync
                def _(sp):
                    for _, s in in_use:
                        sp.sem_clear(s)

            while in_use:
                in_use.pop()[0].__exit__(None, None, None)

        X = sb("X", [P, NT * D])
        ACC = sb("ACC", [P, NB * D])
        BIG = sb("BIG", [P, max(4 * J, NB * P, 6144)])
        pair_idx = sb("pair_idx", [P, QB * P], I32)
        pair_lo = sb("pair_lo", [P, QB * P])
        norm = sb("norm", [P, QB * P])
        AR = sb("AR", [P, 6144 + 8 * 512])
        W = AR[:, 0:6144]
        TT = AR[:, 6144:6144 + 8 * 512]
        T = [TT[:, k * 512:(k + 1) * 512] for k in range(8)]
        ring = AR[:, 0:SLOTS * TW].rearrange("p (k c) -> p k c", k=SLOTS)
        rows = [AR[:, k * TW:(k + 1) * TW] for k in range(SLOTS)]
        sel = [AR[:, SLOTS * TW + k * P:SLOTS * TW + (k + 1) * P] for k in range(SLOTS)]
        AFTER = SLOTS * (TW + P)
        pos = AR[:, 0:J].bitcast(I32)
        idx_st = AR[:, J:J + RING].bitcast(I32)
        rec_st = AR[:, J + RING:J + 5 * RING]
        brow = sb("brow", [1, 2048])
        pair_off = brow[:, 0:QB * P].bitcast(I32)
        iota = sb("iota", [P, P])
        ident = sb("ident", [P, P])
        tri = sb("tri", [P, P])
        ones = sb("ones", [P, P])
        zeros = sb("zeros", [P, 132])
        bcol = sb("bcol", [P, NB])
        qcol = sb("qcol", [P, QB])
        eps_ln = sb("eps_ln", [P, 1])
        eps_norm = sb("eps_norm", [P, 1])
        mean_var = sb("mean_var", [P, NT * 2])
        rstd = sb("rstd", [P, NT])
        hmask = sb("hmask", [P, KH // H])
        bdiag = sb("bdiag", [P, H * 132])
        sumsq = sb("sumsq", [P, NT])
        small = sb("small", [P, 256])
        bank = [ctx.enter_context(nc.psum_tensor(f"bank{k}", [P, 512], F32)) for k in range(8)]
        vec = nc.vector
        pe = nc.tensor
        act = nc.scalar

        def tile_of(X, t):
            return X[:, ds(t * D, D)]

        x_in, tail_clear, made = dma_sem("x_in"), sem("tail_clear"), sem("constants_made")
        with nc.Block() as block:
            @block.sync
            def _(sp):
                full = a["x"][0:(NT - 1) * P, :].rearrange("(t p) d -> p t d", p=P)
                sp.dma_start(X[:, 0:(NT - 1) * D].rearrange("p (t d) -> p t d", d=D), full).then_inc(x_in, 16)
                sp.wait_ge(tail_clear, 1)
                sp.dma_start(X[0:TAIL, (NT - 1) * D:NT * D], a["x"][(NT - 1) * P:N, :]).then_inc(x_in, 16)
                sp.wait_ge(x_in, 32)

            @block.vector
            def _(dve):
                vec.memset(X[:, (NT - 1) * D:NT * D], 0.0).then_inc(tail_clear, 1)
                vec.memset(ones[:, :], 1.0)
                vec.memset(zeros[:, :], 0.0)
                vec.memset(eps_ln[:, :], LN_EPS)
                vec.memset(eps_norm[:, :], NORM_EPS)
                vec.memset(ACC[:, :], 0.0)

            @block.gpsimd
            def _(pool):
                pool.iota(iota[:, :], pattern=[[1, P]], base=0, channel_multiplier=0,
                          allow_small_or_imprecise_dtypes=True)
                pool.iota(bcol[:, :], pattern=[[1, NB]], base=0, channel_multiplier=0,
                          allow_small_or_imprecise_dtypes=True)
                pool.iota(qcol[:, :], pattern=[[P, QB]], base=0, channel_multiplier=1,
                          allow_small_or_imprecise_dtypes=True)
                pool.memset(ident[:, :], 0.0).then_inc(made, 1)
                pool.memset(tri[:, :], 1.0).then_inc(made, 1)
                pool.memset(hmask[:, :], 1.0).then_inc(made, 1)
                pool.wait_ge(made, 3)
                pool.affine_select(out=ident[:, :], in_=ident[:, :], compare_op=ALU.not_equal, fill=1.0,
                                   base=0, pattern=[[-1, P]], channel_multiplier=1)
                pool.affine_select(out=hmask[:, :], in_=hmask[:, :], compare_op=ALU.is_ge, fill=0.0, base=0,
                                   pattern=[[-KD, KH // H]], channel_multiplier=1).then_inc(made, 1)
                pool.wait_ge(made, 4)
                pool.affine_select(out=hmask[:, :], in_=hmask[:, :], compare_op=ALU.is_ge, fill=0.0, base=KD - 1,
                                   pattern=[[KD, KH // H]], channel_multiplier=-1)
                pool.affine_select(out=tri[:, :], in_=tri[:, :], compare_op=ALU.is_gt, fill=0.0,
                                   base=0, pattern=[[1, P]], channel_multiplier=-1)

        src_i = ACC[:, 0:J].bitcast(I32)
        dst_i = ACC[:, J:2 * J].bitcast(I32)
        typ_i = ACC[:, 2 * J:3 * J].bitcast(I32)
        hi_i = ACC[:, 3 * J:4 * J].bitcast(I32)
        w_f = ACC[:, 4 * J:5 * J]
        hi = [TT[:, 1024:1024 + J], ACC[:, 6 * J:7 * J]]
        rec = BIG[:, 0:4 * J].rearrange("p (j f) -> p j f", f=4)
        padded, edges_in, rec_src, fields, rec_out, edge_chain = (
            sem("pad_set"), dma_sem("edges_in"), sem("dst_field"), sem("fields"), dma_sem("rec_out"), sem("edge_chain"))
        with nc.Block() as block:
            @block.gpsimd
            def _(pool):
                for v, fill in ((src_i, NPAD), (dst_i, NPAD), (typ_i, 0), (w_f, 0)):
                    pool.memset(v[96:P, JTAIL - 1:J], fill).then_inc(padded, 1)

            @block.sync
            def _(sp):
                sp.wait_ge(padded, 4)
                for v, n in ((src_i, "src"), (dst_i, "dst"), (typ_i, "edge_type_8"), (w_f, "edge_weight")):
                    e = a[n]
                    for lo, hi_ in ((0, 112), (112, P - 1)):
                        sp.dma_start(v[lo:hi_, :], e[lo * J:hi_ * J].rearrange("(p j) -> p j", j=J)).then_inc(edges_in, 16)
                    sp.dma_start(v[P - 1:P, 0:JTAIL], e[(P - 1) * J:E].rearrange("(p j) -> p j", p=1)).then_inc(edges_in, 16)
                sp.wait_ge(fields, 2)
                sp.dma_start(dram["rec"].rearrange("(p j) f -> p (j f)", p=P), BIG[:, 0:4 * J]).then_inc(rec_out, 16)
                sp.wait_ge(rec_out, 16)

            @block.scalar
            def _(s):
                s.wait_ge(edges_in, 12 * 16)
                act.copy(rec[:, :, 2], w_f).then_inc(fields, 1)

            @block.vector
            def _(dve):
                c = Chain(dve, edge_chain)
                dve.wait_ge(edges_in, 12 * 16)
                vec.tensor_copy(rec[:, :, 0], src_i)
                c.link(vec.tensor_copy(rec[:, :, 1], dst_i))
                vec.scalar_tensor_tensor(rec[:, :, 3], typ_i, float(NPAD), rec[:, :, 1], ALU.mult, ALU.add).then_inc(fields, 1)
                for k, v in enumerate((src_i, dst_i)):
                    c.link(vec.tensor_scalar(hi_i, v, 7, None, ALU.arith_shift_right))
                    c.link(vec.tensor_copy(hi[k], hi_i))

        cnt, tot, base = (small[:, k * 64:k * 64 + NB] for k in range(3))
        mask = ACC[:, 0:J].bitcast(I32)
        scan = ACC[:, J:2 * J]
        scan1 = ACC[:, 2 * J:3 * J]
        maskf = ACC[:, 3 * J:4 * J]
        pos_f = [ACC[:, 7 * J:8 * J], ACC[:, 4 * J:5 * J]]
        start = [sb("start0", [P, NB]), sb("start1", [P, NB])]
        end = [sb("end0", [P, NB]), sb("end1", [P, NB])]

        class Rank:

            def __init__(self, key, sums):
                self.key, self.sums = key, sums
                self.chain, self.counted, self.bases = (sem(f"rank_chain{key}"), sem(f"counted{key}"), sem(f"bases{key}"))

            def on_vector(self, dve):
                key, chain, sums, places = self.key, self.chain, self.sums, pos_f[self.key]
                vec.memset(scan1, 1.0)

                def count(b):
                    vec.tensor_scalar(maskf, hi[key], bcol[:, ds(b, 1)], None, ALU.is_equal, ALU.add,
                                      accum_out=cnt[:, ds(b, 1)]).then_inc(chain, 1)
                    dve.wait_ge(chain, b + 1)

                each(dve, NB, 5, count)
                dve.nop().then_inc(self.counted, 1)
                dve.wait_ge(self.bases, 1)
                c = Chain(dve, chain, NB)
                c.link(vec.tensor_copy(tot, sums[:, 64:64 + NB]))
                c.link(vec.tensor_tensor_scan(end[key][:, :], ones[:, 0:NB], tot, 0.0, ALU.mult, ALU.add))
                c.link(vec.tensor_tensor(start[key][:, :], end[key][:, :], tot, ALU.subtract))
                c.link(vec.tensor_tensor(base, start[key][:, :], sums[:, 0:NB], ALU.add))
                c.link(vec.tensor_scalar(base, base, -1.0, None, ALU.add))
                c.link(vec.memset(places, 0.0))
                c0 = NB + c.n

                def place(b):
                    c = Chain(dve, chain, c0 + b * 3)
                    c.link(vec.tensor_scalar(mask, hi[key], bcol[:, ds(b, 1)], None, ALU.is_equal))
                    c.link(vec.tensor_tensor_scan(scan, scan1, mask, base[:, ds(b, 1)], ALU.mult, ALU.add))
                    dve.nop(nofuse=True)
                    c.link(vec.copy_predicated(places, mask, scan))

                each(dve, NB, 5, place)

            def on_tensor(self, t):
                t.wait_ge(self.counted, 1)
                t.wait_ge(self.chain, NB)
                pe.matmul(self.sums[:, 0:NB], tri[:, :], cnt, start=True, stop=True)
                pe.matmul(self.sums[:, 64:64 + NB], ones[:, :], cnt, start=True, stop=True).then_inc(self.bases, 1)

        STAGES, STAGED = 3, 8
        TURN = STAGES * STAGED
        TURNS = J // TURN
        PLACED = 5
        placed_rec = ACC[:, 0:PLACED * J].rearrange("p (j f) -> p j f", f=PLACED)
        place_field = ACC[:, 0:PLACED * J].bitcast(I32).rearrange("p (j f) -> p j f", f=PLACED)[:, :, 4]
        stage_buf = sb("stage_buf", [P, TURN * PLACED])
        stage_int = stage_buf[:, :].bitcast(I32)
        stage_loaded, records_put = ([dma_sem(f"{n}{g}") for g in range(STAGES)] for n in ("stage_loaded", "records_put"))
        turns_put = [0]

        def put_records(pool, until):
            table = dram["placed_rec"]

            def load(g, T_, n=STAGED):
                pool.nop(nofuse=True)
                pool.dma_start(stage_buf[:, g * STAGED * PLACED:(g * STAGED + n) * PLACED],
                               table[:, ds((T_ * TURN + g * STAGED) * PLACED, n * PLACED)]).then_inc(stage_loaded[g], 16)

            def put_stage(g, T_, n=STAGED):
                pool.wait_ge(stage_loaded[g], (T_ + 1) * 16)
                pool.nop(nofuse=True)
                for k in range(g * STAGED, g * STAGED + n):
                    pool.indirect_dma_start(
                        dram["rec_by_src"],
                        bass.IndirectOffsetOnAxis(ap=stage_int[:, k * PLACED + 4:k * PLACED + 5], axis=0),
                        stage_buf[:, k * PLACED:k * PLACED + 4], None).then_inc(records_put[g], 16)

            def turn_of(T_, more=True):
                for g in range(STAGES):
                    put_stage(g, T_)
                    if g == 0:
                        if not (isinstance(T_, int) and T_ == 0):
                            pool.wait_ge(records_put[2], T_ * STAGED * 16)
                            load(2, T_)
                    elif more:
                        pool.wait_ge(records_put[g - 1], (T_ + 1) * STAGED * 16)
                        load(g - 1, T_ + 1)

            T0 = turns_put[0]
            last = until > TURNS
            stop = min(until, TURNS - 1)
            turns_put[0] = max(stop, 1)
            if T0 == 0:
                for g in range(STAGES):
                    load(g, 0)
                turn_of(0, TURNS > 1)
                T0 = 1
            if stop > T0:
                with pool.Fori(0, stop - T0) as i:
                    turn_of(i + T0)
            if last:
                if TURNS > 1:
                    turn_of(TURNS - 1, False)
                left = J - TURNS * TURN
                for g in range(-(-left // STAGED)):
                    n = min(STAGED, left - g * STAGED)
                    pool.wait_ge(records_put[g], TURNS * STAGED * 16)
                    load(g, TURNS, n)
                    put_stage(g, TURNS, n)
                for g in range(STAGES):
                    n = TURNS * STAGED + max(0, min(STAGED, left - g * STAGED))
                    pool.wait_ge(records_put[g], n * 16)
                    pool.nop(nofuse=True)

        parts = ACC[:, 0:5 * CB * P]
        lo_c = [parts[:, k * CB * P:k * CB * P + CB * P] for k in (0, 1)]
        hi_c = [parts[:, k * CB * P:k * CB * P + CB * P] for k in (2, 3)]
        w_c = parts[:, 4 * CB * P:5 * CB * P]
        int_a = ACC[:, 5 * CB * P:6 * CB * P].bitcast(I32)
        int_b = ACC[:, 6 * CB * P:7 * CB * P].bitcast(I32)
        degs = [small[:, 192:192 + NB], sb("deg_in_cols", [P, NB])[:, :]]
        by_dst, by_src = Rank(1, bank[3]), Rank(0, bank[4])
        placed, staged, slotless, src_placed, table_made = (
            sem("placed"), sem("staged"), sem("stage_free"), sem("src_placed"), sem("table_made"))
        sent, table_out = [dma_sem(f"sent{k}") for k in range(2)], dma_sem("table_out")
        cr_in, cr_tr, cr_cp, dg_ch, onehot, counted2, degs_ready, deg_out_s = (
            dma_sem("chunk_rows_in"), sem("chunk_turned"), sem("chunk_copied"), sem("degree_chain"),
            sem("onehots"), sem("degrees_added"), sem("degrees_ready"), dma_sem("degrees_out"))
        SC = J // RING
        SREST = J - SC * RING
        BATCH = 7
        BATCHES = J // BATCH
        BATCH_AT = J + 6 * RING
        assert BATCH_AT + 4 * BATCH * (P + NB) <= 7168

        def batch_of(par, k, n):
            at = BATCH_AT + (2 * par + k) * BATCH * (P + NB)
            mid = at + BATCH * P
            return (AR[:, at:at + n * P].rearrange("p (c s) -> p c s", s=P),
                    AR[:, mid:mid + n * NB].rearrange("p (c s) -> p c s", s=NB))

        with nc.Block() as block:
            @block.vector
            def _(dve):
                by_dst.on_vector(dve)
                vec.tensor_copy(pos[:, :], pos_f[1]).then_inc(placed, 1)
                dve.wait_ge(placed, 1)
                for k in range(CB):
                    n = min(P, J - k * P)
                    dve.wait_ge(cr_tr, k + 1)
                    c0 = slice(k * P, k * P + n)
                    vec.tensor_copy(lo_c[0][:, c0], bank[0][:, 0:n])
                    vec.tensor_copy(lo_c[1][:, c0], bank[0][:, P:P + n])
                    vec.tensor_copy(w_c[:, c0], bank[0][:, 2 * P:2 * P + n]).then_inc(cr_cp, 1)
                dve.wait_ge(cr_cp, CB)
                c = Chain(dve, dg_ch)
                for k in (0, 1):
                    c.link(vec.tensor_copy(int_a[:, 0:J], lo_c[k][:, 0:J]))
                    c.link(vec.tensor_scalar(int_b[:, 0:J], int_a[:, 0:J], 7, None, ALU.arith_shift_right))
                    c.link(vec.tensor_copy(hi_c[k][:, 0:J], int_b[:, 0:J]))
                    c.link(vec.tensor_scalar(int_b[:, 0:J], int_a[:, 0:J], 127, None, ALU.bitwise_and))
                    c.link(vec.tensor_copy(lo_c[k][:, 0:J], int_b[:, 0:J]))
                dve.sem_inc(counted2, 4)

                def onehots(m, par, n):
                    def over(v, size):
                        return v.rearrange("p (c a) -> p c a", a=1).broadcast_to([P, n, size])

                    def along(v):
                        return v.rearrange("p (a s) -> p a s", a=1).broadcast_to([P, n, v.shape[1]])

                    for k in (0, 1):
                        dve.wait_ge(counted2, 2 * m + k + 1)
                        lo_h, hi_h = batch_of(par, k, n)
                        cols = ds(m * BATCH, n)
                        c = Chain(dve, dg_ch, 10 + 2 * m + k)
                        vec.tensor_tensor(lo_h, along(iota[:, :]), over(lo_c[k][:, cols], P), ALU.is_equal)
                        c.link(vec.tensor_tensor(hi_h, along(bcol[:, :]), over(hi_c[k][:, cols], NB), ALU.is_equal))
                        vec.tensor_tensor(hi_h, hi_h, over(w_c[:, cols], NB), ALU.mult).then_inc(onehot, 1)

                with dve.Fori(0, BATCHES // 2) as i:
                    for par in (0, 1):
                        onehots(i * 2 + par, par, BATCH)
                for m in range(BATCHES - BATCHES % 2, BATCHES + 1):
                    n = min(BATCH, J - m * BATCH)
                    if n > 0:
                        onehots(m, m % 2, n)
                dve.wait_ge(counted2, 2 * -(-J // BATCH) + 2 + 4)
                vec.tensor_copy(degs[0], bank[1][:, 0:NB])
                vec.tensor_copy(degs[1], bank[2][:, 0:NB]).then_inc(degs_ready, 1)
                by_src.on_vector(dve)
                vec.tensor_copy(place_field, pos_f[0]).then_inc(table_made, 1)
                vec.tensor_copy(placed_rec[:, :, 0:4], rec).then_inc(table_made, 1)

            @block.tensor
            def _(t):
                by_dst.on_tensor(t)
                pr = T[1][:, :].rearrange("q (e f) -> q f e", f=4)
                for k in range(CB):
                    n = min(P, J - k * P)
                    t.wait_ge(cr_in, 16 * (k + 1))
                    if k:
                        t.wait_ge(cr_cp, k)
                    for fl in range(3):
                        last = pe.transpose(bank[0][:, fl * P:fl * P + n], pr[0:n, fl, :], ident[0:n, 0:n])
                    last.then_inc(cr_tr, 1)
                for k in (0, 1):
                    pe.matmul(bank[1 + k][:, 0:NB], zeros[:, 0:P], zeros[:, 0:NB], start=True, stop=False, skip_group_check=True)

                def add(m, par, n):
                    for k in (0, 1):
                        t.wait_ge(onehot, 2 * m + k + 1)
                        lo_h, hi_h = batch_of(par, k, n)
                        for c in range(n):
                            last = pe.matmul(bank[1 + k][:, 0:NB], lo_h[:, c, :], hi_h[:, c, :],
                                             start=False, stop=False, skip_group_check=True)
                        last.then_inc(counted2, 1)

                with t.Fori(0, BATCHES // 2) as i:
                    for par in (0, 1):
                        add(i * 2 + par, par, BATCH)
                for m in range(BATCHES - BATCHES % 2, BATCHES + 1):
                    n = min(BATCH, J - m * BATCH)
                    if n > 0:
                        add(m, m % 2, n)
                for k in (0, 1):
                    pe.matmul(bank[1 + k][:, 0:NB], zeros[:, 0:P], zeros[:, 0:NB], start=False, stop=True,
                              skip_group_check=True).then_inc(counted2, 1)
                by_src.on_tensor(t)

            @block.scalar
            def _(s):
                s.wait_ge(placed, 1)

                def stage(first, half, n):
                    cols = slice(half * HALF, half * HALF + n)
                    act.copy(idx_st[:, cols], pos[:, ds(first, n)])
                    act.copy(rec_st[:, half * HALF * 4:(half * HALF + n) * 4],
                             BIG[:, ds(first * 4, n * 4)]).then_inc(staged, 1)

                with s.Fori(0, SC) as i:
                    for half in range(2):
                        s.wait_ge(slotless, 2 * i + half + 1)
                        stage(i * RING + half * HALF, half, HALF)
                for half in range(2):
                    n = min(HALF, SREST - half * HALF)
                    if n > 0:
                        s.wait_ge(slotless, 2 * SC + half + 1)
                        stage(SC * RING + half * HALF, half, n)

            @block.gpsimd
            def _(pool):
                pool.sem_inc(slotless, 2)

                def scatter(half, n):
                    for k in range(half * HALF, half * HALF + n):
                        pool.indirect_dma_start(
                            dram["rec_by_dst"], bass.IndirectOffsetOnAxis(ap=idx_st[:, k:k + 1], axis=0),
                            rec_st[:, 4 * k:4 * k + 4], None).then_inc(sent[half], 16)

                with pool.Fori(0, SC) as i:
                    for half in range(2):
                        pool.wait_ge(staged, 2 * i + half + 1)
                        pool.nop(nofuse=True)
                        scatter(half, HALF)
                    for half in range(2):
                        pool.wait_ge(sent[half], (i + 1) * HALF * 16)
                        pool.nop(nofuse=True)
                        pool.sem_inc(slotless, 1)
                for half in range(2):
                    n = min(HALF, SREST - half * HALF)
                    if n > 0:
                        pool.wait_ge(staged, 2 * SC + half + 1)
                        pool.nop(nofuse=True)
                        scatter(half, n)
                pool.wait_ge(sent[0], (SC * HALF + min(HALF, SREST)) * 16)
                pool.nop(nofuse=True)
                pool.wait_ge(sent[1], (SC * HALF + max(0, SREST - HALF)) * 16)
                pool.nop(nofuse=True)

            @block.sync
            def _(sp):
                view = dram["rec"].rearrange("(c e) f -> c (e f)", e=P)
                for k in range(CB):
                    if k:
                        sp.wait_ge(cr_tr, k)
                    n = min(P, J - k * P)
                    sp.dma_start(T[1][0:n, :], view[k * P:k * P + n, :]).then_inc(cr_in, 16)
                sp.wait_ge(degs_ready, 1)
                with nc.allow_non_contiguous_dma(reason="one degree of a node each"):
                    sp.dma_start(dram["tab0"][:, D:D + 1].rearrange("(t p) c -> p t c", p=P), degs[0][:, 0:NT]
                                 .rearrange("p (t c) -> p t c", c=1)).then_inc(deg_out_s, 16)
                    sp.dma_start(dram["deg_in"].rearrange("(t p) -> p t", p=P), degs[1]).then_inc(deg_out_s, 16)
                sp.wait_ge(table_made, 2)
                sp.dma_start(dram["placed_rec"], ACC[:, 0:PLACED * J]).then_inc(table_out, 16)
                sp.wait_ge(deg_out_s, 32)
                sp.wait_ge(table_out, 16)

        def ints(k):
            return small[:, k * 64:k * 64 + NB].bitcast(I32)

        first_c, last_c, npair, poi, f, qbucket, qchunk, junk = (
            sb(n, [P, max(QB, NB)]) for n in ("first_c", "last_c", "npair", "pairs_before", "fdiff", "qbucket", "qchunk", "junk"))
        qi = sb("qi", [P, QB], I32)
        off_i = sb("off_i", [P, QB], I32)

        def make_pairs(key):
            ch, made_q, got, tr, cp, offs = (sem(f"pair_chain{key}"), sem(f"pair_chunk{key}"), dma_sem(f"pair_rows{key}"),
                                             sem(f"pair_turned{key}"), sem(f"pair_copied{key}"), dma_sem(f"pair_off{key}"))
            local = sem(f"pair_local{key}")
            source = dram["rec_by_src"] if key == 0 else dram["rec_by_dst"]
            chunk_rows = source.rearrange("(c e) f -> c (e f)", e=P)
            prow = T[0]
            b_only = slice(0, NT)
            with nc.Block() as block:
                @block.vector
                def _(dve):
                    c = Chain(dve, ch)
                    s0, e0 = start[key][:, b_only], end[key][:, b_only]
                    si, ei = ints(0)[:, b_only], ints(1)[:, b_only]
                    c.link(vec.tensor_copy(si, s0))
                    c.link(vec.tensor_scalar(npair[:, b_only], e0, -1.0, None, ALU.add))
                    c.link(vec.tensor_copy(ei, npair[:, b_only]))
                    c.link(vec.tensor_scalar(si, si, 7, None, ALU.arith_shift_right))
                    c.link(vec.tensor_scalar(ei, ei, 7, None, ALU.arith_shift_right))
                    c.link(vec.tensor_copy(first_c[:, b_only], si))
                    c.link(vec.tensor_copy(last_c[:, b_only], ei))
                    c.link(vec.tensor_tensor(npair[:, b_only], last_c[:, b_only], first_c[:, b_only], ALU.subtract))
                    c.link(vec.tensor_scalar(npair[:, b_only], npair[:, b_only], 1.0, None, ALU.add))
                    c.link(vec.tensor_tensor(last_c[:, b_only], e0, s0, ALU.is_gt))
                    c.link(vec.tensor_tensor(npair[:, b_only], npair[:, b_only], last_c[:, b_only], ALU.mult))
                    c.link(vec.tensor_tensor_scan(poi[:, b_only], ones[:, b_only], npair[:, b_only], 0.0, ALU.mult, ALU.add))
                    c.link(vec.tensor_tensor(f[:, b_only], first_c[:, b_only], poi[:, b_only], ALU.subtract))
                    c.link(vec.tensor_tensor(f[:, b_only], f[:, b_only], npair[:, b_only], ALU.add))
                    c.link(vec.tensor_tensor(last_c[:, 0:NT - 1], f[:, 1:NT], f[:, 0:NT - 1], ALU.subtract))
                    for k in range(QB):
                        c.link(vec.scalar_tensor_tensor(junk[:, b_only], poi[:, b_only], qcol[:, k:k + 1], ones[:, b_only],
                                                        ALU.is_le, ALU.mult, accum_out=qbucket[:, k:k + 1]))
                        c.link(vec.scalar_tensor_tensor(junk[:, 0:NT - 1], poi[:, 0:NT - 1], qcol[:, k:k + 1],
                                                        last_c[:, 0:NT - 1], ALU.is_le, ALU.mult,
                                                        accum_out=qchunk[:, k:k + 1]))
                    c.link(vec.tensor_tensor(qchunk[:, 0:QB], qchunk[:, 0:QB], qcol[:, :], ALU.add))
                    c.link(vec.tensor_scalar(qchunk[:, 0:QB], qchunk[:, 0:QB], f[:, 0:1], float(J - 1), ALU.add, ALU.min))
                    vec.tensor_copy(qi[:, :], qchunk[:, 0:QB])
                    c.link(vec.tensor_scalar(off_i[:, :], qbucket[:, 0:QB], float(P), None, ALU.mult))
                    c.link(vec.tensor_scalar(qbucket[:, 0:QB], qbucket[:, 0:QB], float(P), None, ALU.mult))
                    dve.nop().then_inc(made_q, 1)
                    key_f = 0 if key == 0 else 1
                    for k in range(QB):
                        dve.wait_ge(got, 16 * (k + 1))
                        pr = prow[:, :].rearrange("q (e f) -> q f e", f=4)
                        vec.tensor_scalar(pr[:, key_f, :], pr[:, key_f, :], qbucket[:, k:k + 1], None,
                                          ALU.subtract).then_inc(local, 1)
                        dve.wait_ge(tr, k + 1)
                        cols = slice(k * P, (k + 1) * P)
                        vec.tensor_copy(pair_lo[:, cols], bank[0][:, 0:P])
                        if key == 0:
                            vec.tensor_copy(pair_idx[:, cols], bank[0][:, P:2 * P]).then_inc(cp, 1)
                        else:
                            vec.tensor_copy(norm[:, cols], bank[0][:, 2 * P:3 * P])
                            vec.tensor_scalar(pair_idx[:, cols], bank[0][:, P:2 * P], float(NPAD - 1), None,
                                              ALU.min).then_inc(cp, 1)

                @block.gpsimd
                def _(pool):
                    pool.wait_ge(made_q, 1)
                    for k in range(QB):
                        if k:
                            pool.wait_ge(tr, k)
                        pool.indirect_dma_start(prow[:, :], None, chunk_rows,
                                                bass.IndirectOffsetOnAxis(ap=qi[:, k:k + 1], axis=0)).then_inc(got, 16)

                @block.tensor
                def _(t):
                    for k in range(QB):
                        t.wait_ge(local, k + 1)
                        if k:
                            t.wait_ge(cp, k)
                        pr = prow[:, :].rearrange("q (e f) -> q f e", f=4)
                        fields_ = (0, 3) if key == 0 else (1, 0, 2)
                        for n, fl in enumerate(fields_):
                            last = pe.transpose(bank[0][:, n * P:(n + 1) * P], pr[:, fl, :], ident[:, :])
                        last.then_inc(tr, 1)

                @block.sync
                def _(sp):
                    if key == 1:
                        sp.dma_start(BIG[:, 0:NB * P], dram["deg_in"].rearrange("(a n) -> a n", a=1)
                                     .broadcast_to([P, NB * P])).then_inc(offs, 16)
                    sp.wait_ge(made_q, 1)
                    with nc.allow_non_contiguous_dma(reason="one offset of a pair each"):
                        sp.dma_start(dram[f"off{key}"].rearrange("(k q) -> q k", q=P), off_i[:, :]).then_inc(offs, 16)
                    sp.wait_ge(offs, 32 if key == 1 else 16)

        recycle()
        make_pairs(1)

        mean = mean_var[:, 0:NT]
        var = mean_var[:, NT:2 * NT]

        def layer_norm_stats(name, rows_of=None):
            st, ag, rt = sem(f"{name}_stats"), sem(f"{name}_aggregate"), sem(f"{name}_root")
            six = TT[:, 0:6 * NT].rearrange("p (t c) -> p t c", c=6)
            with nc.Block() as block:
                @block.vector
                def _(dve):
                    each(dve, NT, 8, lambda t: vec.bn_stats(
                        TT[:, ds(6 * t, 6)], tile_of(X if rows_of is None else rows_of, t)).then_inc(st, 1))
                    dve.wait_ge(st, NT)
                    c = Chain(dve, ag)
                    c.link(vec.tensor_tensor(mean, six[:, :, 1], six[:, :, 4], ALU.subtract))
                    c.link(vec.tensor_tensor(var, six[:, :, 2], six[:, :, 5], ALU.add))
                    c.link(vec.tensor_scalar(mean, mean, 0.5, None, ALU.mult))
                    c.link(vec.tensor_tensor(mean, mean, mean, ALU.mult))
                    c.link(vec.scalar_tensor_tensor(var, var, 1.0 / D, mean, ALU.mult, ALU.add))
                    c.link(vec.tensor_tensor(mean, six[:, :, 1], six[:, :, 4], ALU.add))
                    c.link(vec.tensor_scalar(mean, mean, 0.5, None, ALU.mult))
                    dve.wait_ge(rt, 1)
                    c.link(vec.reciprocal(rstd[:, :], rstd[:, :]))

                @block.scalar
                def _(s):
                    s.wait_ge(ag, 5)
                    act.activation(rstd[:, :], var, ACT.Sqrt, bias=eps_ln[:, 0:1]).then_inc(rt, 1)

        def normalize(out_ap, t):
            return vec.tensor_scalar(out_ap, tile_of(X, t), mean_var[:, ds(t, 1)], rstd[:, ds(t, 1)],
                                     ALU.subtract, ALU.mult)

        def turn(bank_ap, src):
            for h in range(H):
                last = pe.transpose(bank_ap[:, h * P:(h + 1) * P], src[:, h * P:(h + 1) * P], ident[:, :])
            return last

        def product(out_ap, lhs, rhs, cols=None, last=True):
            n = rhs.shape[1] // H
            c0, c1 = cols or (0, n)
            for h in range(H):
                ins = pe.matmul(out_ap, lhs[:, h * P:(h + 1) * P], rhs[:, h * n + c0:h * n + c1],
                                start=h == 0, stop=last and h == H - 1)
            return ins

        def add_row(out_ap, row, last=True):
            return pe.matmul(out_ap, ones[0:1, :], row, start=False, stop=last)

        def load_halves(sp, dst, src, done):
            n = src.shape[1]
            return sp.dma_start(dst.rearrange("p (h n) -> p h n", h=H), src.rearrange("(h p) n -> p h n", p=P)).then_inc(done, 16)

        def bias_row(sp, at, name, done):
            n = a[name].shape[0]
            sp.dma_start(brow[0:1, at:at + n], a[name].rearrange("(a n) -> a n", a=1)).then_inc(done, 16)
            return brow[0:1, at:at + n]


        def tiles(eng, stages):
            lags = max(lag for lag, _ in stages)

            def step(i, par, n):
                for lag, f in stages:
                    b = (par - lag) % 2
                    if not isinstance(i, int):
                        f(i - lag, b, P, n + (first + par - lag - b) // 2)
                    elif 0 <= i - lag < NT:
                        f(i - lag, b, TAIL if i - lag == NT - 1 else P, (i - lag) // 2)

            first = max(2, lags + lags % 2)
            turns = (NT - 1 - first) // 2
            for i in range(first):
                step(i, i % 2, None)
            with eng.Fori(0, turns) as n:
                for par in range(2):
                    step(2 * n + first + par, par, n)
            for i in range(first + 2 * turns, NT + lags):
                step(i, i % 2, None)

        def first_use(u):
            return isinstance(u, int) and u == 0

        def wide(v, n=NT):
            return v[:, 0:n * D].rearrange("p (t d) -> p t d", d=D)

        def per_tile(v):
            return v.rearrange("p (t a) -> p t a", a=1).broadcast_to([P, NT, D])

        def per_feature(v):
            return v.rearrange("p (a d) -> p a d", a=1).broadcast_to([P, NT, D])

        def turned_weights(name, dst, weights):
            w_in, w_tr, w_cp = dma_sem(f"{name}_w_in"), sem(f"{name}_w_turned"), sem(f"{name}_w_copied")
            blocks = [w[o:o + P, :] for w in weights for o in range(0, w.shape[0], P)]
            n_out = len(blocks) * P
            with nc.Block() as block:
                @block.sync
                def _(sp):
                    for k, b in enumerate(blocks):
                        sp.dma_start(TT[:, k * D:(k + 1) * D], b).then_inc(w_in, 16)

                @block.tensor
                def _(t):
                    t.wait_ge(w_in, 16 * len(blocks))
                    for k in range(len(blocks)):
                        turn(bank[k][:, 0:D], TT[:, k * D:(k + 1) * D]).then_inc(w_tr, 1)

                @block.vector
                def _(dve):
                    for k in range(len(blocks)):
                        dve.wait_ge(w_tr, k + 1)
                        vec.tensor_copy(dst.rearrange("p (h o) -> p h o", h=H)[:, :, k * P:(k + 1) * P],
                                        bank[k][:, 0:D].rearrange("p (h o) -> p h o", h=H)).then_inc(w_cp, 1)
                    dve.wait_ge(w_cp, len(blocks))

        recycle()
        layer_norm_stats("ln0")
        wq_t, wkv_t, wproj_t = W[:, 0:H * D], W[:, H * D:3 * H * D], W[:, 3 * H * D:4 * H * D]
        turned_weights("mix0_q", wq_t, [a["L0_mix_Wq"]])
        turned_weights("mix0_kv", wkv_t, [a["L0_mix_Wkv"]])
        turned_weights("mix0_proj", wproj_t, [a["L0_mix_Wproj"]])

        stored = [dma_sem("m0_stored0"), dma_sem("m0_stored1")]
        nrm, turned, turned_sb, kv, low, expk, kpos, v_sb, done = (
            sem(f"m0_{n}") for n in ("normalized", "turned", "turned_sb", "kv", "low", "exp", "k", "v", "done"))

        def vx(b):
            return T[4 + b][:, 0:H * 132]

        with nc.Block() as block:
            @block.gpsimd
            def _(pool):
                put_records(pool, TURNS * 7 // 65)

            @block.vector
            def _(dve):
                def normal(t, b, rows_, u):
                    dve.wait_ge(done, t + 1)
                    dve.nop(nofuse=True)
                    if not first_use(u):
                        dve.wait_ge(stored[b], 16 * u)
                    normalize(T[0][:, b * D:(b + 1) * D], t).then_inc(nrm, 1)

                def keys(t, b, rows_, u):
                    dve.wait_ge(kv, t + 1)
                    vec.tensor_scalar(T[2][:, b * D:(b + 1) * D], bank[2 + b][:, 0:D], 0.0, None, ALU.min).then_inc(low, 1)
                    dve.wait_ge(expk, t + 1)
                    vec.scalar_tensor_tensor(T[3][:, b * D:(b + 1) * D], bank[2 + b][:, 0:D], 0.0,
                                             T[2][:, b * D:(b + 1) * D], ALU.max, ALU.add).then_inc(kpos, 1)

                tiles(dve, [(0, normal), (1, keys)])

            @block.sync
            def _(sp):
                def store(t, b, rows_, u):
                    sp.wait_ge(nrm, t + 1)
                    sp.dma_start(dram["tab0"][ds(t * P, P), 0:D], T[0][:, b * D:(b + 1) * D]).then_inc(stored[b], 16)

                tiles(sp, [(0, store)])
                for b in (0, 1):
                    sp.wait_ge(stored[b], 16 * ((NT + 1 - b) // 2))

            @block.tensor
            def _(t_):
                t_.sem_inc(done, 2)

                def keys(t, b, rows_, u):
                    t_.wait_ge(nrm, t + 1)
                    turn(bank[b][:, 0:D], T[0][:, b * D:(b + 1) * D]).then_inc(turned, 1)
                    t_.wait_ge(turned_sb, t + 1)
                    product(bank[2 + b][:, 0:D], T[1][:, b * D:(b + 1) * D], wkv_t, (0, D))
                    product(bank[4 + b][:, 0:D], T[1][:, b * D:(b + 1) * D], wkv_t, (D, 2 * D)).then_inc(kv, 1)

                def context(t, b, rows_, u):
                    t_.wait_ge(kpos, t + 1)
                    t_.wait_ge(v_sb, t + 1)
                    for h in range(H):
                        last = pe.matmul(bank[6 + h][:, 0:P + 1], T[3][0:rows_, b * D + h * P:b * D + (h + 1) * P],
                                         vx(b)[0:rows_, h * 132:h * 132 + P + 1], start=False, stop=False, skip_group_check=True)
                    last.then_inc(done, 1)

                for h in range(H):
                    pe.matmul(bank[6 + h][:, 0:P + 1], zeros[:, 0:P], zeros[:, 0:P + 1], start=True, stop=False, skip_group_check=True)
                tiles(t_, [(0, keys), (1, context)])
                for h in range(H):
                    pe.matmul(bank[6 + h][:, 0:P + 1], zeros[:, 0:P], zeros[:, 0:P + 1], start=False, stop=True, skip_group_check=True)

            @block.scalar
            def _(s):
                for b in (0, 1):
                    for h in range(H):
                        act.copy(vx(b)[:, h * 132 + P:h * 132 + P + 1], ones[:, 0:1])

                def copy(t, b, rows_, u):
                    s.wait_ge(turned, t + 1)
                    act.copy(T[1][:, b * D:(b + 1) * D], bank[b][:, 0:D]).then_inc(turned_sb, 1)

                def values(t, b, rows_, u):
                    s.wait_ge(kv, t + 1)
                    act.copy(vx(b).rearrange("p (h c) -> p h c", c=132)[:, :, 0:P],
                             bank[4 + b][:, 0:D].rearrange("p (h c) -> p h c", c=P)).then_inc(v_sb, 1)
                    s.wait_ge(low, t + 1)
                    act.activation(T[2][:, b * D:(b + 1) * D], T[2][:, b * D:(b + 1) * D], ACT.Exp).then_inc(expk, 1)

                tiles(s, [(0, copy), (1, values)])

        bd_made = sem("m0_blocks")
        with nc.Block() as block:
            @block.vector
            def _(dve):
                for h in range(H):
                    for j in range(KH // H):
                        vec.tensor_scalar(bdiag[:, h * 132 + KD * j:h * 132 + KD * (j + 1)],
                                          bank[6 + h][:, KD * j:KD * (j + 1)], hmask[:, j:j + 1], None,
                                          ALU.mult).then_inc(bd_made, 1)
                    vec.tensor_scalar(bdiag[:, h * 132 + P:h * 132 + P + KH // H], hmask[:, :], bank[6 + h][:, P:P + 1],
                                      None, ALU.mult).then_inc(bd_made, 1)

        bias_in = dma_sem("m1_bias_in")
        nrm, turned, turned_sb, qs, low, expq, qpos, att, den, scaled, turned2, turned2_sb, proj, done = (
            sem(f"m1_{n}") for n in ("normalized", "turned", "turned_sb", "q", "low", "exp", "q_pos", "attention",
                                     "denominator", "scaled", "turned2", "turned2_sb", "projected", "done"))

        def part(k, b):
            return T[k][:, b * D:(b + 1) * D]

        with nc.Block() as block:
            @block.gpsimd
            def _(pool):
                put_records(pool, TURNS * 16 // 65)

            @block.sync
            def _(sp):
                bias_row(sp, 0, "L0_mix_bproj", bias_in)

            @block.vector
            def _(dve):
                dve.sem_inc(done, 2)

                def normal(t, b, rows_, u):
                    dve.wait_ge(done, t + 1)
                    normalize(part(0, b), t).then_inc(nrm, 1)

                def scale(t, b, rows_, u):
                    dve.wait_ge(att, t + 1)
                    c = Chain(dve, den, 2 * t)
                    av = bank[4 + b][:, 0:H * 132].rearrange("p (h c) -> p h c", c=132)
                    sv = T[6][:, b * 8:b * 8 + 8]
                    c.link(vec.tensor_scalar(sv.rearrange("p (h j) -> p h j", h=H), av[:, :, P:P + KH // H], 1e-06, None, ALU.max))
                    c.link(vec.reciprocal(sv, sv))
                    vec.tensor_tensor(part(4, b).rearrange("p (h j d) -> p h j d", h=H, d=KD),
                                      av[:, :, 0:P].rearrange("p h (j d) -> p h j d", d=KD),
                                      sv.rearrange("p (h j a) -> p h j a", h=H, a=1).broadcast_to([P, H, KH // H, KD]),
                                      ALU.mult).then_inc(scaled, 1)

                def elu(t, b, rows_, u):
                    dve.wait_ge(qs, t + 1)
                    vec.tensor_scalar(part(2, b), bank[2 + b][:, 0:D], 0.0, None, ALU.min).then_inc(low, 1)
                    dve.wait_ge(expq, t + 1)
                    vec.scalar_tensor_tensor(part(3, b), bank[2 + b][:, 0:D], 0.0, part(2, b), ALU.max, ALU.add).then_inc(qpos, 1)

                def add(t, b, rows_, u):
                    dve.wait_ge(proj, t + 1)
                    vec.tensor_tensor(tile_of(X, t), tile_of(X, t), bank[6 + b][:, D:2 * D], ALU.add).then_inc(done, 1)

                tiles(dve, [(0, normal), (1, scale), (0, elu), (1, add)])

            @block.scalar
            def _(s):
                def copy(t, b, rows_, u):
                    s.wait_ge(turned, t + 1)
                    act.copy(part(1, b), bank[b][:, 0:D]).then_inc(turned_sb, 1)

                def copy2(t, b, rows_, u):
                    s.wait_ge(turned2, t + 1)
                    act.copy(part(5, b), bank[6 + b][:, 0:D]).then_inc(turned2_sb, 1)

                def exp(t, b, rows_, u):
                    s.wait_ge(low, t + 1)
                    act.activation(part(2, b), part(2, b), ACT.Exp).then_inc(expq, 1)

                tiles(s, [(0, copy), (1, copy2), (0, exp)])

            @block.tensor
            def _(t_):
                t_.wait_ge(bias_in, 16)

                def attend(t, b, rows_, u):
                    t_.wait_ge(qpos, t + 1)
                    for h in range(H):
                        last = pe.matmul(bank[4 + b][:, h * 132:(h + 1) * 132], part(3, b)[:, h * P:(h + 1) * P],
                                         bdiag[:, h * 132:(h + 1) * 132], start=True, stop=True)
                    last.then_inc(att, 1)

                def turn1(t, b, rows_, u):
                    t_.wait_ge(nrm, t + 1)
                    turn(bank[b][:, 0:D], part(0, b)).then_inc(turned, 1)

                def turn2(t, b, rows_, u):
                    t_.wait_ge(scaled, t + 1)
                    turn(bank[6 + b][:, 0:D], part(4, b)).then_inc(turned2, 1)

                def query(t, b, rows_, u):
                    t_.wait_ge(turned_sb, t + 1)
                    for h in range(H):
                        for c in range(H):
                            last = pe.matmul(bank[2 + b][:, h * P:(h + 1) * P], wq_t[:, c * D + h * P:c * D + (h + 1) * P],
                                             part(1, b)[:, c * P:(c + 1) * P], start=c == 0, stop=c == H - 1)
                    last.then_inc(qs, 1)

                def project(t, b, rows_, u):
                    t_.wait_ge(turned2_sb, t + 1)
                    product(bank[6 + b][:, D:2 * D], part(5, b), wproj_t, last=False)
                    add_row(bank[6 + b][:, D:2 * D], brow[0:1, 0:D]).then_inc(proj, 1)

                tiles(t_, [(1, attend), (0, turn1), (1, turn2), (0, query), (1, project)])

        NPAIR = QR * SLOTS
        landed = [dma_sem(f"landed{g}") for g in range(GROUPS)]
        turn_no = [0]

        def aggregate(name, table, width, off, weighted, norms):
            off_in, cleared, idx_ready, chosen, summed, added, di_ch, rooted = (
                dma_sem(f"{name}_off_in"), sem(f"{name}_cleared"), sem(f"{name}_idx_ready"), sem(f"{name}_chosen"),
                sem(f"{name}_summed"), sem(f"{name}_added"), sem(f"{name}_norm_chain"), sem(f"{name}_rooted"))
            before = turn_no[0] * QR
            turn_no[0] += 1
            idx_at = AR[:, AFTER:AFTER + SLOTS].bitcast(I32)
            n_in = AR[:, AFTER + 192:AFTER + 192 + GROUP]
            d_root = AR[:, AFTER + 208:AFTER + 208 + GROUP]
            STEPS = GROUP + 3

            with nc.Block() as block:
                @block.sync
                def _(sp):
                    sp.dma_start(pair_off, off.rearrange("(a n) -> a n", a=1)).then_inc(off_in, 16)

                @block.scalar
                def _(s):
                    def stage(m, g):
                        s.wait_ge(summed, GROUP * (m + 1))
                        act.copy(idx_at[:, g * GROUP:(g + 1) * GROUP],
                                 pair_idx[:, ds(m * GROUP, GROUP)]).then_inc(idx_ready, 1)

                    def turn_of_ring(i, last=False):
                        for g in range(GROUPS):
                            m = GROUPS * i + g
                            if norms:
                                s.wait_ge(di_ch, m * STEPS + GROUP + 1)
                                act.activation(d_root, n_in, ACT.Sqrt, bias=eps_norm[:, 0:1]).then_inc(rooted, 1)
                            if not (last and g):
                                stage(m + 2, (g + 2) % GROUPS)

                    stage(0, 0)
                    stage(1, 1)
                    with s.Fori(0, QR - 1) as i:
                        turn_of_ring(i)
                    turn_of_ring(QR - 1, True)

                @block.gpsimd
                def _(pool):
                    with pool.Fori(0, QR) as i:
                        for g in range(GROUPS):
                            pool.wait_ge(idx_ready, GROUPS * i + g + 1)
                            pool.nop(nofuse=True)
                            for k in range(g * GROUP, (g + 1) * GROUP):
                                pool.indirect_dma_start(rows[k][:, 0:width], None, table,
                                                        bass.IndirectOffsetOnAxis(ap=idx_at[:, k:k + 1], axis=0)
                                                        ).then_inc(landed[g], 16)

                @block.tensor
                def _(t):
                    t.sem_inc(summed, SLOTS)
                    with t.Fori(0, QR) as i:
                        for g in range(GROUPS):
                            t.wait_ge(chosen, GROUPS * i + g + 1)
                            t.wait_ge(landed[g], 16 * GROUP * (i + 1 + before))
                            for j in range(GROUP):
                                k = g * GROUP + j
                                t.wait_ge(added, i * SLOTS + k + 1)
                                pe.matmul(bank[j][:, 0:D], sel[k], rows[k][:, 0:D], start=True, stop=True).then_inc(summed, 1)

                @block.vector
                def _(dve):
                    dve.wait_ge(off_in, 16)
                    vec.memset(ACC[:, :], 0.0).then_inc(cleared, 1)
                    dve.wait_ge(cleared, 1)
                    dve.sem_inc(added, GROUP)
                    add_regs, pick_regs = ([dve.alloc_register(f"{name}_{n}{k}") for k in range(GROUP)] for n in ("a", "p"))

                    def offsets(m, regs):
                        dve.nop(nofuse=True)
                        dve.load(regs, pair_off[0:1, ds(m * GROUP, GROUP)])
                        return [dve.snap(r, min_val=0, max_val=NT * P) for r in regs]

                    def pick(m, g, k, offs):
                        vec.scalar_tensor_tensor(
                            sel[g * GROUP + k], iota[:, :], pair_lo[:, ds(m * GROUP + k, 1)], BIG[:, ds(offs[k], P)],
                            ALU.is_equal, ALU.mult, accum_out=n_in[:, k:k + 1]).then_inc(di_ch, 1)

                    def degrees(i, m, g):
                        dve.wait_ge(di_ch, m * STEPS + GROUP)
                        dve.wait_ge(landed[g], 16 * GROUP * (i + 1 + before))
                        c = Chain(dve, di_ch, m * STEPS + GROUP)
                        c.link(vec.tensor_tensor(n_in, n_in, ring[:, g * GROUP:(g + 1) * GROUP, D], ALU.mult))

                    def edge_norms(m):
                        dve.wait_ge(rooted, m + 1)
                        c = Chain(dve, di_ch, m * STEPS + GROUP + 1)
                        c.link(vec.reciprocal(d_root, d_root))
                        nm = norm[:, ds(m * GROUP, GROUP)]
                        c.link(vec.tensor_tensor(nm, nm, d_root, ALU.mult))

                    def select(m, g, k):
                        lo = pair_lo[:, ds(m * GROUP + k, 1)]
                        if weighted:
                            ins = vec.tensor_scalar(sel[g * GROUP + k], iota[:, :], lo,
                                                    norm[:, ds(m * GROUP + k, 1)], ALU.is_equal, ALU.mult)
                        else:
                            ins = vec.tensor_scalar(sel[g * GROUP + k], iota[:, :], lo, None, ALU.is_equal)
                        if k == GROUP - 1:
                            ins.then_inc(chosen, 1)

                    def add(i, g, k, offs):
                        n = i * SLOTS + g * GROUP + k
                        dve.wait_ge(summed, SLOTS + n + 1)
                        dve.wait_ge(added, GROUP + n)
                        at = ACC[:, ds(offs[k] * H, D)]
                        vec.tensor_tensor(at, at, bank[k][:, 0:D], ALU.add).then_inc(added, 1)

                    EARLY = GROUP // 2 if norms else 0

                    def turn_of_ring(i, last=False):
                        for g in range(GROUPS):
                            m, g1 = GROUPS * i + g, (g + 1) % GROUPS
                            offs = offsets(m, add_regs)
                            if last and g == GROUPS - 1:
                                for k in range(GROUP):
                                    add(i, g, k, offs)
                                continue
                            if norms:
                                picks = offsets(m + 1, pick_regs)
                                for k in range(GROUP):
                                    pick(m + 1, g1, k, picks)
                                    if k % 2 and k // 2 < EARLY - 1:
                                        add(i, g, k // 2, offs)
                                degrees(i + (g + 1) // GROUPS, m + 1, g1)
                                add(i, g, EARLY - 1, offs)
                                edge_norms(m + 1)
                            for k in range(GROUP):
                                select(m + 1, g1, k)
                                if k % 2:
                                    add(i, g, EARLY + k // 2, offs)
                            for k in range(EARLY + GROUP // 2, GROUP):
                                add(i, g, k, offs)

                    if norms:
                        picks = offsets(0, pick_regs)
                        for k in range(GROUP):
                            pick(0, 0, k, picks)
                        degrees(0, 0, 0)
                        edge_norms(0)
                    for k in range(GROUP):
                        select(0, 0, k)
                    with dve.Fori(0, QR - 1) as i:
                        turn_of_ring(i)
                    turn_of_ring(QR - 1, True)
                    dve.wait_ge(added, GROUP + NPAIR)

        w_g = [W[:, k * H * D:(k + 1) * H * D] for k in range(3)]

        def graph_dense(name, last_layer):
            w_in = dma_sem(f"{name}_weights_in")
            staged, turned, turned_sb, prod, act_out, turned2, turned2_sb, proj, done = (
                sem(f"{name}_{n}") for n in ("staged", "turned", "turned_sb", "product", "relu", "turned2", "turned2_sb",
                                             "projected", "done"))
            stored = [dma_sem(f"{name}_stored{b}") for b in (0, 1)]

            def part(k, b):
                return T[k][:, b * D:(b + 1) * D]

            with nc.Block() as block:
                @block.gpsimd
                def _(pool):
                    put_records(pool, TURNS * (34 if last_layer else 22) // 65)

                @block.sync
                def _(sp):
                    names = ("W7", "Wp") if last_layer else ("W6",)
                    for k, n in enumerate(names):
                        load_halves(sp, w_g[k], a[f"L0_gnn_{n}"], w_in)
                        bias_row(sp, k * D, f"L0_gnn_b{n[1:]}", w_in)
                    if not last_layer:
                        def store(t, b, rows_, u):
                            sp.wait_ge(act_out, t + 1)
                            sp.dma_start(dram["tab1"][ds(t * P, P), :], part(2, b)).then_inc(stored[b], 16)

                        tiles(sp, [(0, store)])
                        for b in (0, 1):
                            sp.wait_ge(stored[b], 16 * ((NT + 1 - b) // 2))

                @block.vector
                def _(dve):
                    def load(t, b, rows_, u):
                        dve.wait_ge(done, t + 1)
                        vec.tensor_copy(part(0, b), tile_of(ACC, t)).then_inc(staged, 1)

                    if not last_layer:
                        tiles(dve, [(0, load)])
                    else:
                        dve.sem_inc(done, 2)

                        def add(t, b, rows_, u):
                            dve.wait_ge(proj, t + 1)
                            vec.tensor_tensor(tile_of(X, t), tile_of(X, t), bank[6 + b][:, 0:D], ALU.add).then_inc(done, 1)

                        tiles(dve, [(0, load), (1, add)])

                @block.scalar
                def _(s):
                    def copy(t, b, rows_, u):
                        s.wait_ge(turned, t + 1)
                        act.copy(part(1, b), bank[b][:, 0:D]).then_inc(turned_sb, 1)

                    def relu(t, b, rows_, u):
                        s.wait_ge(prod, t + 1)
                        if not last_layer and not first_use(u):
                            s.wait_ge(stored[b], 16 * u)
                        act.activation(part(2, b), bank[2 + b][:, 0:D], ACT.Relu).then_inc(act_out, 1)
                        if not last_layer:
                            s.wait_ge(act_out, t + 1)
                            s.sem_inc(done, 1)

                    def copy2(t, b, rows_, u):
                        s.wait_ge(turned2, t + 1)
                        act.copy(part(3, b), bank[4 + b][:, 0:D]).then_inc(turned2_sb, 1)

                    if not last_layer:
                        s.sem_inc(done, 2)
                        tiles(s, [(0, copy), (1, relu)])
                    else:
                        tiles(s, [(0, copy), (1, copy2), (0, relu)])

                @block.tensor
                def _(t_):
                    t_.wait_ge(w_in, 64 if last_layer else 32)

                    def turn1(t, b, rows_, u):
                        t_.wait_ge(staged, t + 1)
                        turn(bank[b][:, 0:D], part(0, b)).then_inc(turned, 1)

                    def layer(t, b, rows_, u):
                        t_.wait_ge(turned_sb, t + 1)
                        product(bank[2 + b][:, 0:D], part(1, b), w_g[0], last=False)
                        add_row(bank[2 + b][:, 0:D], brow[0:1, 0:D]).then_inc(prod, 1)

                    def turn2(t, b, rows_, u):
                        t_.wait_ge(act_out, t + 1)
                        turn(bank[4 + b][:, 0:D], part(2, b)).then_inc(turned2, 1)

                    def project(t, b, rows_, u):
                        t_.wait_ge(turned2_sb, t + 1)
                        product(bank[6 + b][:, 0:D], part(3, b), w_g[1], last=False)
                        add_row(bank[6 + b][:, 0:D], brow[0:1, D:2 * D]).then_inc(proj, 1)

                    if last_layer:
                        tiles(t_, [(0, turn1), (1, turn2), (0, layer), (1, project)])
                    else:
                        tiles(t_, [(0, turn1), (0, layer)])

        recycle()
        aggregate("agg0", dram["tab0"], D + 1, dram["off1"], True, True)
        graph_dense("gnn0", False)
        recycle()
        aggregate("agg1", dram["tab1"], D, dram["off1"], True, False)
        graph_dense("gnn1", True)

        recycle()
        layer_norm_stats("ln1")
        NPR = FH // 2
        w_fx, w_lg = W[:, 0:H * INNER], W[:, H * INNER:2 * H * INNER]
        w_xt = W[0:G, 4 * INNER:4 * INNER + FH * D]
        w_slice, w_qk, w_kk, w_vk = (BIG[0:G, 5120 + k * G:5120 + (k + 1) * G] for k in range(4))
        b_xt = BIG[0:G, 5376:5376 + FH]
        temp = BIG[:, 5392:5392 + FH]
        b_fx = BIG[:, 5408:5408 + NPR * G]
        tok_n = BIG[:, 5664:5664 + 2 * NPR]
        w_in = dma_sem("f0_weights_in")
        w_ch, w_tr, w_cp, w_mm = (sem(f"f0_{n}") for n in ("weight_chain", "weight_turned",
                                                                "weight_copied", "weight_product"))
        bs_row = brow[0:1, 0:G]
        bl_row = brow[0:1, 512:512 + INNER]
        with nc.Block() as block:
            @block.sync
            def _(sp):
                load_halves(sp, w_fx, a["L0_ffn_W_fx"], w_in)
                load_halves(sp, TT[:, 0:H * INNER], a["L0_ffn_W_x"], w_in)
                for v, n in ((w_slice, "W_slice"), (w_qk, "W_q"), (w_kk, "W_k"), (w_vk, "W_v")):
                    sp.dma_start(v, a[f"L0_ffn_{n}"]).then_inc(w_in, 16)
                sp.dma_start(temp, a["L0_ffn_temperature"].rearrange("a h b c -> (a b c) h").broadcast_to([P, FH])).then_inc(w_in, 16)
                with nc.allow_non_contiguous_dma(reason="a bias as columns"):
                    sp.dma_start(b_xt, a["L0_ffn_b_x"].rearrange("(h d) -> d h", d=G)).then_inc(w_in, 16)
                for par in range(2):
                    sp.dma_start(b_fx[par * G:(par + 1) * G, :].rearrange("p (k c) -> p k c", c=G),
                                 a["L0_ffn_b_fx"].rearrange("(k two c) -> two k c", two=2, c=G)[par:par + 1, :, :]
                                 .broadcast_to([G, NPR, G])).then_inc(w_in, 16)
                bias_row(sp, 0, "L0_ffn_b_slice", w_in)

            @block.vector
            def _(dve):
                dve.wait_ge(w_in, 16 * 11)
                c = Chain(dve, w_ch)
                c.link(vec.tensor_scalar(temp, temp, 0.1, 5.0, ALU.max, ALU.min))
                c.link(vec.reciprocal(temp, temp))
                for k in range(4):
                    dve.wait_ge(w_tr, k + 1)
                    vec.tensor_copy(w_xt[:, k * 512:(k + 1) * 512], bank[k][0:G, :]).then_inc(w_cp, 1)
                scale = temp.rearrange("p (h a) -> p h a", a=1)
                for h in range(H):
                    dve.wait_ge(w_mm, h + 1)
                    vec.tensor_tensor(w_lg[:, h * INNER:(h + 1) * INNER].rearrange("p (h g) -> p h g", g=G),
                                      bank[4 + h][:, :].rearrange("p (h g) -> p h g", g=G),
                                      scale.broadcast_to([P, FH, G]), ALU.mult)
                dve.wait_ge(w_mm, H + 1)
                row = bl_row.rearrange("p (h g) -> p h g", g=G)
                c.link(vec.tensor_tensor(row, bank[6][0:1, :].rearrange("p (h g) -> p h g", g=G),
                                         bs_row.rearrange("p (a g) -> p a g", a=1).broadcast_to([1, FH, G]), ALU.add))
                c.link(vec.tensor_tensor(row, row, scale[0:1, :, :].broadcast_to([1, FH, G]), ALU.mult))

            @block.tensor
            def _(t):
                t.wait_ge(w_in, 16 * 11)
                for h in range(FH):
                    for c in range(H):
                        at = h * D + c * P
                        last = pe.transpose(bank[at // 512][0:G, at % 512:at % 512 + P],
                                            TT[:, c * INNER + h * G:c * INNER + (h + 1) * G], ident[:, :])
                    if h % 2:
                        last.then_inc(w_tr, 1)
                t.wait_ge(w_cp, 4)
                for c in range(H):
                    for h in range(FH):
                        last = pe.matmul(bank[4 + c][:, h * G:(h + 1) * G], w_xt[:, h * D + c * P:h * D + (c + 1) * P],
                                         w_slice, start=True, stop=True)
                    last.then_inc(w_mm, 1)
                for h in range(FH):
                    last = pe.matmul(bank[6][0:1, h * G:(h + 1) * G], b_xt[:, h:h + 1], w_slice, start=True, stop=True)
                last.then_inc(w_mm, 1)

        (nrm, turned, turned_sb, lg, fx, mx_ch, exped, slw, fx_sb, done) = (
            sem(f"f1_{n}") for n in ("normalized", "turned", "turned_sb", "logits", "features", "softmax_chain", "exp",
                                     "slice_weights", "features_sb", "done"))
        stored = [dma_sem(f"f1_stored{b}") for b in (0, 1)]
        lgb = [T[2], T[3]]
        swb = [T[4], T[5]]
        fxb = [W[:, 4096:4096 + NPR * 132], W[:, 4096 + NPR * 132:4096 + 2 * NPR * 132]]

        def token_at(k):
            return (bank[6][:, k * 129:(k + 1) * 129]) if k < 3 else bank[7][:, 0:129]

        def heads(v):
            return v.rearrange("p (h g) -> p h g", g=G)

        def spread(v, n, g):
            return v.rearrange("p (h a) -> p h a", a=1).broadcast_to([n, v.shape[1], g])

        with nc.Block() as block:
            @block.gpsimd
            def _(pool):
                put_records(pool, TURNS * 46 // 65)

            @block.sync
            def _(sp):
                def store(t, b, rows_, u):
                    sp.wait_ge(slw, t + 1)
                    sp.dma_start(dram["sw"][ds(t * P, P), :], swb[b]).then_inc(stored[b], 16)

                tiles(sp, [(0, store)])
                for b in (0, 1):
                    sp.wait_ge(stored[b], 16 * ((NT + 1 - b) // 2))

            @block.vector
            def _(dve):
                def normal(t, b, rows_, u):
                    dve.wait_ge(done, t + 1)
                    normalize(T[0][:, b * D:(b + 1) * D], t).then_inc(nrm, 1)

                def top(t, b, rows_, u):
                    dve.wait_ge(lg, t + 1)
                    c = Chain(dve, mx_ch, 4 * t)
                    m = T[6][:, b * 16:b * 16 + FH]
                    c.link(vec.tensor_reduce(m, heads(bank[2 + b][:, :]), AX, ALU.max))
                    vec.tensor_tensor(heads(lgb[b]), heads(bank[2 + b][:, :]), spread(m, P, G), ALU.subtract).then_inc(mx_ch, 1)

                def share(t, b, rows_, u):
                    dve.wait_ge(exped, t + 1)
                    if not first_use(u):
                        dve.wait_ge(stored[b], 16 * u)
                    c = Chain(dve, mx_ch, 4 * t + 2)
                    m = T[6][:, b * 16 + 8:b * 16 + 8 + FH]
                    c.link(vec.tensor_reduce(m, heads(lgb[b]), AX, ALU.add))
                    c.link(vec.reciprocal(m, m))
                    vec.tensor_tensor(heads(swb[b]), heads(lgb[b]), spread(m, P, G), ALU.mult).then_inc(slw, 1)

                tiles(dve, [(0, normal), (1, top), (1, share)])

            @block.scalar
            def _(s):
                for b in (0, 1):
                    for k in range(NPR):
                        act.copy(fxb[b][:, k * 132 + P:k * 132 + P + 1], ones[:, 0:1])

                def copy(t, b, rows_, u):
                    s.wait_ge(turned, t + 1)
                    act.copy(T[1][:, b * D:(b + 1) * D], bank[b][:, 0:D]).then_inc(turned_sb, 1)

                def exp(t, b, rows_, u):
                    s.wait_ge(mx_ch, 4 * t + 2)
                    act.activation(lgb[b], lgb[b], ACT.Exp).then_inc(exped, 1)

                def features(t, b, rows_, u):
                    s.wait_ge(fx, t + 1)
                    act.copy(fxb[b].rearrange("p (k c) -> p k c", c=132)[:, :, 0:P],
                             bank[4 + b][:, :].rearrange("p (k c) -> p k c", c=P)).then_inc(fx_sb, 1)

                tiles(s, [(1, exp), (1, features), (0, copy)])

            @block.tensor
            def _(t_):
                t_.sem_inc(done, 2)

                def turn1(t, b, rows_, u):
                    t_.wait_ge(nrm, t + 1)
                    turn(bank[b][:, 0:D], T[0][:, b * D:(b + 1) * D]).then_inc(turned, 1)

                def logits(t, b, rows_, u):
                    t_.wait_ge(turned_sb, t + 1)
                    product(bank[2 + b][:, :], T[1][:, b * D:(b + 1) * D], w_lg, last=False)
                    add_row(bank[2 + b][:, :], bl_row).then_inc(lg, 1)
                    product(bank[4 + b][:, :], T[1][:, b * D:(b + 1) * D], w_fx).then_inc(fx, 1)

                def tokens(t, b, rows_, u):
                    t_.wait_ge(slw, t + 1)
                    t_.wait_ge(fx_sb, t + 1)
                    for k in range(NPR):
                        last = pe.matmul(token_at(k), swb[b][0:rows_, k * P:(k + 1) * P], fxb[b][0:rows_, k * 132:k * 132 + 129],
                                         start=False, stop=False, skip_group_check=True)
                    last.then_inc(done, 1)

                pe.matmul(bank[6][:, 0:387], zeros[:, 0:P], W[:, 0:387], start=True, stop=False, skip_group_check=True)
                pe.matmul(bank[7][:, 0:129], zeros[:, 0:P], W[:, 0:129], start=True, stop=False, skip_group_check=True)
                tiles(t_, [(0, turn1), (1, tokens), (0, logits)])
                pe.matmul(bank[6][:, 0:387], zeros[:, 0:P], W[:, 0:387], start=False, stop=True, skip_group_check=True)
                pe.matmul(bank[7][:, 0:129], zeros[:, 0:P], W[:, 0:129], start=False, stop=True, skip_group_check=True)

        tok = BIG[:, 0:NPR * G]
        tok_t, q_t, k_t, v_t, prob = (BIG[0:G, 512 * (k + 1):512 * (k + 2)] for k in range(5))
        prob_t = BIG[0:G, 512 * 6:512 * 7]
        w_out = W[0:G, 0:FH * D]
        vw = TT[0:G, 0:FH * D]
        rows_out = TT[0:G, FH * D:2 * FH * D]
        mm_rows = W[:, 2048:2048 + NPR * D]
        a_in = dma_sem("fa_weights_in")
        a_ch, a_pe, a_ex, a_out = (sem(f"fa_{n}") for n in ("vector", "tensor", "exp", "packed"))
        SCALE = float(G) ** -0.5
        TOK_STEPS = NPR + 2 + 4 * NPR
        red = BIG[0:G, 5700:5700 + FH]
        with nc.Block() as block:
            @block.sync
            def _(sp):
                sp.dma_start(w_out.rearrange("c (h d) -> c h d", d=D), a["L0_ffn_W_out"].rearrange("(h c) d -> c h d", c=G)).then_inc(a_in, 16)
                bias_row(sp, 0, "L0_ffn_b_out", a_in)
                sp.wait_ge(a_out, 1)
                for par in range(2):
                    sp.dma_start(mm_rows[par * G:(par + 1) * G, :].rearrange("g (k d) -> g k d", d=D),
                                 rows_out.rearrange("g (k two d) -> g two k d", two=2, d=D)[:, par, :, :]).then_inc(a_in, 16)
                sp.wait_ge(a_in, 64)

            @block.vector
            def _(dve):
                c = Chain(dve, a_ch)
                wsum = tok_n[:, 0:NPR]
                rec_w = tok_n[:, NPR:2 * NPR]
                for k in range(NPR):
                    c.link(vec.tensor_copy(wsum[:, k:k + 1], token_at(k)[:, P:P + 1]))
                c.link(vec.tensor_scalar(rec_w, wsum, 1e-05, None, ALU.add))
                c.link(vec.reciprocal(rec_w, rec_w))
                for k in range(NPR):
                    c.link(vec.tensor_scalar(b_fx[:, k * G:(k + 1) * G], b_fx[:, k * G:(k + 1) * G], wsum[:, k:k + 1], None, ALU.mult))
                    for par in range(2):
                        r = slice(par * G, (par + 1) * G)
                        c.link(vec.tensor_tensor(tok[r, k * G:(k + 1) * G], token_at(k)[r, par * G:(par + 1) * G],
                                                 b_fx[r, k * G:(k + 1) * G], ALU.add))
                    c.link(vec.tensor_scalar(tok[:, k * G:(k + 1) * G], tok[:, k * G:(k + 1) * G], rec_w[:, k:k + 1], None, ALU.mult))
                assert c.n == TOK_STEPS
                dve.wait_ge(a_pe, 1)
                c.link(vec.tensor_copy(tok_t, bank[0][0:G, :]))
                for n, v in enumerate((q_t, k_t, v_t)):
                    dve.wait_ge(a_pe, 2 + n)
                    c.link(vec.tensor_copy(v, bank[1 + n][0:G, :]))
                dve.wait_ge(a_pe, 5)
                c.link(vec.tensor_reduce(red, heads(bank[4][0:G, :]), AX, ALU.max))
                c.link(vec.tensor_tensor(heads(prob), heads(bank[4][0:G, :]), spread(red, G, G), ALU.subtract))
                dve.wait_ge(a_ex, 1)
                c.link(vec.tensor_reduce(red, heads(prob), AX, ALU.add))
                c.link(vec.reciprocal(red, red))
                c.link(vec.tensor_tensor(heads(prob), heads(prob), spread(red, G, G), ALU.mult))
                dve.wait_ge(a_pe, 6)
                c.link(vec.tensor_copy(prob_t, bank[5][0:G, :]))
                for n in range(4):
                    dve.wait_ge(a_pe, 7 + n)
                    c.link(vec.tensor_copy(vw[:, n * 512:(n + 1) * 512], bank[n][0:G, :]))
                for n in range(4):
                    dve.wait_ge(a_pe, 11 + n)
                    c.link(vec.tensor_copy(rows_out[:, n * 512:(n + 1) * 512], bank[4 + n][0:G, :]))
                dve.nop().then_inc(a_out, 1)

            @block.scalar
            def _(s):
                s.wait_ge(a_ch, TOK_STEPS + 6)
                act.activation(prob, prob, ACT.Exp, scale=SCALE).then_inc(a_ex, 1)

            @block.tensor
            def _(t):
                t.wait_ge(a_ch, TOK_STEPS)
                for k in range(NPR):
                    last = pe.transpose(bank[0][0:G, k * P:(k + 1) * P], tok[:, k * G:(k + 1) * G], ident[:, :])
                last.then_inc(a_pe, 1)
                t.wait_ge(a_ch, TOK_STEPS + 1)
                for n, w in enumerate((w_qk, w_kk, w_vk)):
                    pe.matmul(bank[1 + n][0:G, :], w, tok_t, start=True, stop=True).then_inc(a_pe, 1)
                t.wait_ge(a_ch, TOK_STEPS + 4)
                for h in range(FH):
                    r = slice(h * G, (h + 1) * G)
                    last = pe.matmul(bank[4][0:G, r], q_t[:, r], k_t[:, r], start=True, stop=True)
                last.then_inc(a_pe, 1)
                t.wait_ge(a_ch, TOK_STEPS + 9)
                for h in range(FH):
                    r = slice(h * G, (h + 1) * G)
                    last = pe.transpose(bank[5][0:G, r], prob[:, r], ident[0:G, 0:G])
                last.then_inc(a_pe, 1)
                t.wait_ge(a_in, 32)
                for h in range(FH):
                    last = pe.matmul(bank[h // 2][0:G, (h % 2) * D:(h % 2 + 1) * D], v_t[:, h * G:(h + 1) * G],
                                     w_out[:, h * D:(h + 1) * D], start=True, stop=True)
                    if h % 2:
                        last.then_inc(a_pe, 1)
                t.wait_ge(a_ch, TOK_STEPS + 14)
                for h in range(FH):
                    last = pe.matmul(bank[4 + h // 2][0:G, (h % 2) * D:(h % 2 + 1) * D], prob_t[:, h * G:(h + 1) * G],
                                     vw[:, h * D:(h + 1) * D], start=True, stop=True)
                    if h % 2:
                        last.then_inc(a_pe, 1)

        turned, turned_sb, prod, done = (sem(f"f2_{n}") for n in ("turned", "turned_sb", "product", "done"))
        loaded = [dma_sem(f"f2_loaded{b}") for b in (0, 1)]
        with nc.Block() as block:
            @block.gpsimd
            def _(pool):
                put_records(pool, TURNS * 50 // 65)

            @block.sync
            def _(sp):
                def load(t, b, rows_, u):
                    if not first_use(u):
                        sp.wait_ge(turned, t - 1)
                    sp.dma_start(T[b], dram["sw"][ds(t * P, P), :]).then_inc(loaded[b], 16)

                tiles(sp, [(0, load)])

            @block.scalar
            def _(s):
                def copy(t, b, rows_, u):
                    s.wait_ge(turned, t + 1)
                    if not first_use(u):
                        s.wait_ge(prod, t - 1)
                    act.copy(T[2 + b], bank[b][:, :]).then_inc(turned_sb, 1)

                tiles(s, [(0, copy)])

            @block.vector
            def _(dve):
                dve.sem_inc(done, 2)

                def add(t, b, rows_, u):
                    dve.wait_ge(prod, t + 1)
                    vec.tensor_tensor(tile_of(X, t), tile_of(X, t), bank[2 + b][:, 0:D], ALU.add).then_inc(done, 1)

                tiles(dve, [(0, add)])

            @block.tensor
            def _(t_):
                def turn1(t, b, rows_, u):
                    t_.wait_ge(loaded[b], 16 * (u + 1))
                    for k in range(NPR):
                        last = pe.transpose(bank[b][:, k * P:(k + 1) * P], T[b][:, k * P:(k + 1) * P], ident[:, :])
                    last.then_inc(turned, 1)

                def back(t, b, rows_, u):
                    t_.wait_ge(turned_sb, t + 1)
                    t_.wait_ge(done, t + 1)
                    for k in range(NPR):
                        pe.matmul(bank[2 + b][:, 0:D], T[2 + b][:, k * P:(k + 1) * P], mm_rows[:, k * D:(k + 1) * D],
                                  start=k == 0, stop=False)
                    add_row(bank[2 + b][:, 0:D], brow[0:1, 0:D]).then_inc(prod, 1)

                tiles(t_, [(0, turn1), (1, back)])

        recycle()
        layer_norm_stats("ln2")
        RW = R * D
        w_rel = W[:, 0:H * RW]
        w_qkv = W[:, H * RW:H * RW + H * 3 * HID]
        g_pre = small[:, 0:H]
        assert H * RW + H * 3 * HID <= 6144
        w_in, ss_in = dma_sem("g0_weights_in"), sem("g0_weights_scaled")
        nrm, turned, turned_sb, done, squares, mov_a, mov_v, prods, qkv_ready = (
            sem(f"g0_{n}") for n in ("normalized", "turned", "turned_sb", "done", "squares", "moved_by_act",
                                     "moved_by_vec", "products", "qkv"))
        stored = [dma_sem(f"g0_stored{b}") for b in (0, 1)]
        xt_sb = [BIG[:, b * RW:(b + 1) * RW] for b in (0, 1)]
        qkv_sb = [T[2][:, 0:3 * HID], T[3][:, 0:3 * HID]]
        tab2_rows = dram["tab2"].rearrange("(r n) d -> n r d", r=R)
        with nc.Block() as block:
            @block.gpsimd
            def _(pool):
                put_records(pool, TURNS + 1)

            @block.sync
            def _(sp):
                for r in range(R):
                    sp.dma_start(w_rel.rearrange("p (h r o) -> p h r o", h=H, r=R)[:, :, r, :],
                                 a["L1_gnn_weight"][r, :, :].rearrange("(h p) o -> p h o", p=P)).then_inc(w_in, 16)
                load_halves(sp, w_qkv, a["L1_mix_w_qkv"], w_in)
                with nc.allow_non_contiguous_dma(reason="gains as columns"):
                    sp.dma_start(g_pre, a["L1_mix_g_pre"].rearrange("(h p) -> p h", p=P)).then_inc(w_in, 16)

                def store(t, b, rows_, u):
                    sp.wait_ge(mov_a, 3 * t + 3)
                    sp.wait_ge(mov_v, 2 * t + 2)
                    sp.dma_start(tab2_rows[ds(t * P, P), :, :], xt_sb[b].rearrange("p (r d) -> p r d", r=R)).then_inc(stored[b], 16)
                    sp.dma_start(dram["qkv"][ds(t * P, P), :], qkv_sb[b]).then_inc(stored[b], 16)

                tiles(sp, [(0, store)])
                for b in (0, 1):
                    sp.wait_ge(stored[b], 32 * ((NT + 1 - b) // 2))

            @block.vector
            def _(dve):
                dve.wait_ge(w_in, 16 * (R + 2))
                for h in range(H):
                    vec.tensor_scalar(w_qkv[:, h * 3 * HID:(h + 1) * 3 * HID], w_qkv[:, h * 3 * HID:(h + 1) * 3 * HID],
                                      g_pre[:, h:h + 1], float(D) ** 0.5, ALU.mult, ALU.mult).then_inc(ss_in, 1)
                dve.sem_inc(done, 2)

                def normal(t, b, rows_, u):
                    dve.wait_ge(done, t + 1)
                    normalize(T[0][:, b * D:(b + 1) * D], t).then_inc(nrm, 1)

                def move(t, b, rows_, u):
                    if not first_use(u):
                        dve.wait_ge(stored[b], 32 * u)
                    for k in (1, 3):
                        dve.wait_ge(prods, 4 * t + k + 1)
                        vec.tensor_copy(xt_sb[b][:, k * 512:(k + 1) * 512], bank[2 + k][:, :]).then_inc(mov_v, 1)
                    dve.wait_ge(mov_v, 2 * t + 2)
                    dve.wait_ge(mov_a, 3 * t + 3)
                    dve.wait_ge(squares, t + 1)
                    dve.sem_inc(done, 1)

                tiles(dve, [(0, normal), (1, move)])

            @block.scalar
            def _(s):
                def copy(t, b, rows_, u):
                    s.wait_ge(turned, t + 1)
                    act.copy(T[1][:, b * D:(b + 1) * D], bank[b][:, 0:D]).then_inc(turned_sb, 1)
                    s.wait_ge(nrm, t + 1)
                    if not first_use(t):
                        s.wait_ge(squares, t)
                    s.nop(nofuse=True)
                    act.activation(T[4][:, 0:D], T[0][:, b * D:(b + 1) * D], ACT.Square,
                                   accum_out=sumsq[:, ds(t, 1)]).then_inc(squares, 1)

                def move(t, b, rows_, u):
                    if not first_use(u):
                        s.wait_ge(stored[b], 32 * u)
                    for k in (0, 2):
                        s.wait_ge(prods, 4 * t + k + 1)
                        act.copy(xt_sb[b][:, k * 512:(k + 1) * 512], bank[2 + k][:, :]).then_inc(mov_a, 1)
                    s.wait_ge(qkv_ready, t + 1)
                    act.copy(qkv_sb[b], bank[6 + b][:, 0:3 * HID]).then_inc(mov_a, 1)

                tiles(s, [(0, copy), (1, move)])

            @block.tensor
            def _(t_):
                t_.wait_ge(w_in, 16 * (R + 2))
                t_.wait_ge(ss_in, H)

                def turn1(t, b, rows_, u):
                    t_.wait_ge(nrm, t + 1)
                    turn(bank[b][:, 0:D], T[0][:, b * D:(b + 1) * D]).then_inc(turned, 1)

                def rels(t, b, rows_, u):
                    t_.wait_ge(turned_sb, t + 1)
                    lhs = T[1][:, b * D:(b + 1) * D]
                    for k in range(4):
                        if not (isinstance(t, int) and t == 0):
                            moved, before_ = ((mov_a, 3 * t - 3), (mov_v, 2 * t - 2))[k % 2]
                            t_.wait_ge(moved, before_ + k // 2 + 1)
                        product(bank[2 + k][:, :], lhs, w_rel, (k * 512, (k + 1) * 512)).then_inc(prods, 1)
                    product(bank[6 + b][:, 0:3 * HID], lhs, w_qkv).then_inc(qkv_ready, 1)

                tiles(t_, [(0, turn1), (1, rels)])

        recycle()
        inv_n = small[:, 64:64 + NT]
        kmax = T[4][:, 0:P]
        krow = T[5][:, 0:P]
        mem_k, mem_v = T[6][0:MEM, 0:P], T[7][0:MEM, 0:132]
        mem_kt = small[:, 128:128 + MEM]
        col = [small[:, 136 + k:137 + k] for k in range(4)]
        w_om, cw = W[:, 0:D], W[:, D:2 * D]
        g_out = W[:, 2 * D:3 * D]
        diag = W[:, 3 * D:3 * D + P]
        m_in, m_ch, m_rt, m_pe, km_ch = (dma_sem("h0_weights_in"), sem("h0_chain"), sem("h0_root"), sem("h0_tensor"),
                                         sem("h0_maxima"))
        loaded = [dma_sem(f"h0_loaded{b}") for b in (0, 1)]
        with nc.Block() as block:
            @block.sync
            def _(sp):
                sp.dma_start(w_om, a["L1_mix_w_out"]).then_inc(m_in, 16)
                bias_row(sp, 0, "L1_mix_b_out", m_in)
                sp.dma_start(g_out, a["L1_mix_g_out"].rearrange("(a d) -> a d", a=1).broadcast_to([P, D])).then_inc(m_in, 16)
                sp.dma_start(mem_kt, a["L1_mix_mem_kv"][0, :, :, :].rearrange("h d m -> (h d) m")).then_inc(m_in, 16)
                with nc.allow_non_contiguous_dma(reason="memories as rows"):
                    sp.dma_start(mem_k, a["L1_mix_mem_kv"][0, :, :, :].rearrange("h d m -> m (h d)")).then_inc(m_in, 16)
                    sp.dma_start(mem_v[:, 0:P], a["L1_mix_mem_kv"][1, :, :, :].rearrange("h d m -> m (h d)")).then_inc(m_in, 16)

                def load(t, b, rows_, u):
                    if not first_use(u):
                        sp.wait_ge(km_ch, t - 1)
                    sp.dma_start(T[b][:, 0:HID], dram["qkv"][ds(t * P, P), HID:2 * HID]).then_inc(loaded[b], 16)

                tiles(sp, [(0, load)])

            @block.scalar
            def _(s):
                act.activation(inv_n, sumsq[:, :], ACT.Sqrt).then_inc(m_rt, 1)

            @block.vector
            def _(dve):
                c = Chain(dve, m_ch)
                c.link(vec.memset(kmax, -3.0e38))
                dve.wait_ge(m_rt, 1)
                c.link(vec.tensor_scalar(inv_n, inv_n, 1e-12, None, ALU.max))
                c.link(vec.reciprocal(inv_n, inv_n))

                def largest(t, b, rows_, u):
                    dve.wait_ge(loaded[b], 16 * (u + 1))
                    if not (isinstance(t, int) and t == 0):
                        dve.wait_ge(km_ch, t)
                    vec.scalar_tensor_tensor(kmax[0:rows_, :], T[b][0:rows_, 0:HID], inv_n[0:rows_, ds(t, 1)], kmax[0:rows_, :],
                                             ALU.mult, ALU.max).then_inc(km_ch, 1)

                tiles(dve, [(0, largest)])
                dve.wait_ge(m_in, 16 * 6)
                c.link(vec.tensor_reduce(col[0], mem_kt, AX, ALU.max))
                dve.wait_ge(m_pe, 1)
                c.link(vec.tensor_reduce(col[1], bank[0][:, 0:P], AX, ALU.max))
                c.link(vec.tensor_tensor(col[0], col[0], col[1], ALU.max))
                c.link(vec.tensor_scalar(diag, ident[:, :], col[0], None, ALU.mult))
                dve.wait_ge(m_pe, 2)
                c.link(vec.tensor_copy(krow, bank[1][:, 0:P]))

            @block.tensor
            def _(t):
                t.wait_ge(km_ch, NT)
                pe.transpose(bank[0][:, 0:P], kmax, ident[:, :]).then_inc(m_pe, 1)
                t.wait_ge(m_ch, 7)
                pe.matmul(bank[1][:, 0:P], ones[:, :], diag, start=True, stop=True).then_inc(m_pe, 1)

        kd, ke, vs_, done, mm_ch, mm_ex = (sem(f"h1_{n}") for n in ("lowered", "exp", "values", "done", "memory", "memory_exp"))
        loaded = [dma_sem(f"h1_loaded{b}") for b in (0, 1)]
        vb = [T[2][:, 0:132], T[3][:, 0:132]]
        with nc.Block() as block:
            @block.sync
            def _(sp):
                def load(t, b, rows_, u):
                    sp.wait_ge(done, t + 1)
                    sp.dma_start(T[b][:, 0:2 * HID], dram["qkv"][ds(t * P, P), HID:3 * HID]).then_inc(loaded[b], 16)

                tiles(sp, [(0, load)])

            @block.vector
            def _(dve):
                vec.memset(mem_v[:, P:P + 1], 1.0)
                vec.tensor_tensor(mem_k, mem_k, krow[0:MEM, :], ALU.subtract).then_inc(mm_ch, 1)

                def lower(t, b, rows_, u):
                    dve.wait_ge(loaded[b], 16 * (u + 1))
                    vec.scalar_tensor_tensor(T[b][:, 256:256 + HID], T[b][:, 0:HID], inv_n[:, ds(t, 1)], krow,
                                             ALU.mult, ALU.subtract).then_inc(kd, 1)
                    vec.tensor_scalar(vb[b][:, 0:HID], T[b][:, HID:2 * HID], inv_n[:, ds(t, 1)], None, ALU.mult).then_inc(vs_, 1)

                tiles(dve, [(0, lower)])

            @block.scalar
            def _(s):
                for b in (0, 1):
                    act.copy(vb[b][:, P:P + 1], ones[:, 0:1])
                s.wait_ge(mm_ch, 1)
                act.activation(mem_k, mem_k, ACT.Exp).then_inc(mm_ex, 1)

                def exp(t, b, rows_, u):
                    s.wait_ge(kd, t + 1)
                    act.activation(T[b][:, 256:256 + HID], T[b][:, 256:256 + HID], ACT.Exp).then_inc(ke, 1)

                tiles(s, [(0, exp)])

            @block.tensor
            def _(t_):
                t_.sem_inc(done, 2)
                t_.wait_ge(mm_ex, 1)
                pe.matmul(bank[2][:, 0:P + 1], mem_k, mem_v[:, 0:P + 1], start=True, stop=False, skip_group_check=True)

                def context(t, b, rows_, u):
                    t_.wait_ge(ke, t + 1)
                    t_.wait_ge(vs_, t + 1)
                    pe.matmul(bank[2][:, 0:P + 1], T[b][0:rows_, 256:256 + HID], vb[b][0:rows_, 0:P + 1],
                              start=False, stop=False, skip_group_check=True).then_inc(done, 1)

                tiles(t_, [(0, context)])
                pe.matmul(bank[2][:, 0:P + 1], zeros[:, 0:P], zeros[:, 0:P + 1], start=False, stop=True, skip_group_check=True)

        n_ch, n_pe = sem("h2_chain"), sem("h2_tensor")
        with nc.Block() as block:
            @block.vector
            def _(dve):
                c = Chain(dve, n_ch)
                c.link(vec.tensor_copy(col[2], bank[2][:, P:P + 1]))
                c.link(vec.reciprocal(col[2], col[2]))
                for j in range(MH):
                    c.link(vec.tensor_scalar(diag[:, j * MD:(j + 1) * MD], bank[2][:, j * MD:(j + 1) * MD], hmask[:, j:j + 1],
                                             col[2], ALU.mult, ALU.mult))
                dve.wait_ge(n_pe, 1)
                c.link(vec.tensor_copy(bdiag[:, 0:P], bank[3][:, 0:P]))
                dve.wait_ge(n_pe, 2)
                c.link(vec.tensor_copy(cw, bank[4][:, 0:D]))

            @block.tensor
            def _(t):
                t.wait_ge(n_ch, 2 + MH)
                pe.transpose(bank[3][:, 0:P], diag, ident[:, :]).then_inc(n_pe, 1)
                t.wait_ge(n_ch, 3 + MH)
                pe.matmul(bank[4][:, 0:D], bdiag[:, 0:P], w_om, start=True, stop=True).then_inc(n_pe, 1)

        recycle()
        qsum = sem("h3_sums")
        qch, qex, qn, qt, qts, outp, ysb, done = (sem(f"h3_{n}") for n in ("chain", "exp", "softmaxed", "turned", "turned_sb",
                                                                         "out", "stored", "done"))
        loaded = [dma_sem(f"h3_loaded{b}") for b in (0, 1)]
        QSCALE = float(MD) ** -0.5

        def mheads(v):
            return v.rearrange("p (h d) -> p h d", d=MD)

        def mspread(v):
            return v.rearrange("p (h a) -> p h a", a=1).broadcast_to([P, MH, MD])

        with nc.Block() as block:
            @block.sync
            def _(sp):
                def load(t, b, rows_, u):
                    if not first_use(u):
                        sp.wait_ge(qn, t - 1)
                    sp.dma_start(T[b][:, 0:HID], dram["qkv"][ds(t * P, P), 0:HID]).then_inc(loaded[b], 16)

                tiles(sp, [(0, load)])

            @block.vector
            def _(dve):
                def low(t, b, rows_, u):
                    dve.wait_ge(loaded[b], 16 * (u + 1))
                    c = Chain(dve, qch, 3 * t)
                    q, m = T[b][:, 0:HID], T[b][:, 384:384 + MH]
                    c.link(vec.tensor_scalar(q, q, inv_n[:, ds(t, 1)], None, ALU.mult))
                    c.link(vec.tensor_reduce(m, mheads(q), AX, ALU.max))
                    vec.tensor_tensor(mheads(q), mheads(q), mspread(m), ALU.subtract).then_inc(qch, 1)

                def share(t, b, rows_, u):
                    dve.wait_ge(qex, t + 1)
                    c = Chain(dve, qsum, 2 * t)
                    q, m = T[b][:, 0:HID], T[b][:, 384:384 + MH]
                    c.link(vec.tensor_reduce(m, mheads(q), AX, ALU.add))
                    c.link(vec.reciprocal(m, m))
                    if not first_use(u):
                        dve.wait_ge(qt, t - 1)
                    vec.scalar_tensor_tensor(mheads(T[2 + b][:, 0:HID]), mheads(q), QSCALE, mspread(m), ALU.mult, ALU.mult).then_inc(qn, 1)

                tiles(dve, [(0, low), (1, share)])

            @block.scalar
            def _(s):
                def exp(t, b, rows_, u):
                    s.wait_ge(qch, 3 * t + 3)
                    act.activation(T[b][:, 0:HID], T[b][:, 0:HID], ACT.Exp).then_inc(qex, 1)

                def copy(t, b, rows_, u):
                    s.wait_ge(qt, t + 1)
                    act.copy(T[4 + b][:, 0:HID], bank[b][:, 0:HID]).then_inc(qts, 1)

                def keep(t, b, rows_, u):
                    s.wait_ge(outp, t + 1)
                    act.copy(tile_of(ACC, t), bank[2 + b][:, 0:D]).then_inc(ysb, 1)
                    s.wait_ge(ysb, t + 1)
                    s.nop(nofuse=True)
                    act.activation(T[6][:, b * D:(b + 1) * D], tile_of(ACC, t), ACT.Square, accum_out=sumsq[:, ds(t, 1)]).then_inc(done, 1)
                    s.wait_ge(done, t + 3)

                s.sem_inc(done, 2)
                tiles(s, [(0, exp), (1, copy), (1, keep)])

            @block.tensor
            def _(t_):
                t_.wait_ge(m_in, 32)

                def turn1(t, b, rows_, u):
                    t_.wait_ge(qn, t + 1)
                    pe.transpose(bank[b][:, 0:HID], T[2 + b][:, 0:HID], ident[:, :]).then_inc(qt, 1)

                def out_rows(t, b, rows_, u):
                    t_.wait_ge(qts, t + 1)
                    t_.wait_ge(done, t + 1)
                    pe.matmul(bank[2 + b][:, 0:D], T[4 + b][:, 0:HID], cw, start=True, stop=False)
                    add_row(bank[2 + b][:, 0:D], brow[0:1, 0:D]).then_inc(outp, 1)

                tiles(t_, [(0, turn1), (0, out_rows)])

        r_ch, r_rt = sem("h4_chain"), sem("h4_root")
        with nc.Block() as block:
            @block.scalar
            def _(s):
                act.activation(inv_n, sumsq[:, :], ACT.Sqrt).then_inc(r_rt, 1)

            @block.vector
            def _(dve):
                c = Chain(dve, r_ch)
                dve.wait_ge(r_rt, 1)
                c.link(vec.tensor_scalar(inv_n, inv_n, 1e-12, None, ALU.max))
                c.link(vec.reciprocal(inv_n, inv_n))
                c.link(vec.tensor_scalar(inv_n, inv_n, float(D) ** 0.5, None, ALU.mult))
                y, x = wide(ACC[:, :]), wide(X[:, :])
                c.link(vec.tensor_tensor(y, y, per_tile(inv_n), ALU.mult))
                c.link(vec.tensor_tensor(y, y, per_feature(g_out), ALU.mult))
                c.link(vec.tensor_tensor(mean, mean, rstd[:, :], ALU.mult))
                c.link(vec.tensor_tensor(y, y, x, ALU.add))
                c.link(vec.tensor_tensor(x, x, per_tile(rstd[:, :]), ALU.mult))
                c.link(vec.tensor_tensor(y, y, x, ALU.add))
                c.link(vec.tensor_tensor(x, y, per_tile(mean), ALU.subtract))

        recycle()
        make_pairs(0)
        recycle()
        aggregate("agg2", dram["tab2"], D, dram["off0"], False, False)
        gb_in, gb_ch = dma_sem("g2_bias_in"), sem("g2_chain")
        with nc.Block() as block:
            @block.sync
            def _(sp):
                sp.dma_start(W[:, 0:D], a["L1_gnn_bias"].rearrange("(a d) -> a d", a=1).broadcast_to([P, D])).then_inc(gb_in, 16)

            @block.vector
            def _(dve):
                c = Chain(dve, gb_ch)
                dve.wait_ge(gb_in, 16)
                y, x = wide(ACC[:, :]), wide(X[:, :])
                c.link(vec.tensor_tensor(y, y, per_feature(W[:, 0:D]), ALU.add))
                c.link(vec.scalar_tensor_tensor(X[:, :], ACC[:, 0:NT * D], 0.0, X[:, :], ALU.max, ALU.add))

        recycle()
        layer_norm_stats("ln3")
        wr, br = small[:, 0:H * EX], brow[0:1, 2 * D:2 * D + EX]
        mean_row = brow[0:1, 0:D]
        mean_t = small[:, 32:32 + H]
        def rr(k):
            return brow[0:1, 2 * D + 16 * k:2 * D + 16 * k + EX]

        lrow, erow, wrow, top_v, oh0, oh1, dense, iorow = (rr(k) for k in range(1, 9))
        s1 = brow[0:1, 2 * D + 160:2 * D + 168]
        top_i = brow[0:1, 2 * D + 176:2 * D + 184].bitcast(mybir.dt.uint32)
        pick = brow[0:1, 2 * D + 192:2 * D + 196]
        picks = small[:, 40:44]
        dense_t, oh_t = small[0:EX, 44:45], small[0:EX, 45:47]
        b1_all, b2_all = T[0][0:EX, :], T[1][0:EX, 0:D]
        b1_col = small[:, 48:48 + 2 * (FF // P)]
        e_idx = small[:, 64:64 + 12].bitcast(I32)
        e_f = small[:, 80:92]
        pcol = small[:, 96:97]
        FC = FF // P
        w1 = [W[:, e * H * FF:(e + 1) * H * FF] for e in (0, 1)]
        w2 = [W[:, 2 * H * FF + e * FC * D:2 * H * FF + (e + 1) * FC * D] for e in (0, 1)]
        b2_row = brow[0:1, 3 * D:4 * D]
        CAP = math.ceil(N * 1.25 / EX) / N
        i_in, i_ch, i_pe, i_ex, i_w, i_p = (dma_sem("i0_in"), sem("i0_chain"), sem("i0_tensor"), sem("i0_exp"),
                                            dma_sem("i0_weights"), sem("i0_constants"))
        norm_t, summed_t = sem("i0_normalized"), sem("i0_summed")
        with nc.Block() as block:
            @block.sync
            def _(sp):
                for h in range(H):
                    sp.dma_start(wr[:, h * EX:(h + 1) * EX], a["L1_ffn_Wr"][h * P:(h + 1) * P, :]).then_inc(i_in, 16)
                sp.dma_start(br, a["L1_ffn_br"].rearrange("(a n) -> a n", a=1)).then_inc(i_in, 16)
                sp.dma_start(b1_all, a["L1_ffn_b1"]).then_inc(i_in, 16)
                sp.dma_start(b2_all, a["L1_ffn_b2"]).then_inc(i_in, 16)

            @block.vector
            def _(dve):
                dve.wait_ge(i_in, 80)

                def normal(t, b, rows_, u):
                    if not first_use(u):
                        dve.wait_ge(summed_t, t - 1)
                    normalize(T[2][:, b * D:(b + 1) * D], t).then_inc(norm_t, 1)

                tiles(dve, [(0, normal)])
                c = Chain(dve, i_ch)
                dve.wait_ge(i_pe, 1)
                c.link(vec.tensor_scalar(mean_row, bank[0][0:1, 0:D], 1.0 / N, None, ALU.mult))
                dve.wait_ge(i_pe, 2)
                c.link(vec.tensor_copy(mean_t, bank[1][:, 0:H]))
                dve.wait_ge(i_pe, 3)
                c.link(vec.tensor_tensor(lrow, bank[2][0:1, 0:EX], br, ALU.add))

                def softmax(dst, src, n, turn_):
                    c.link(vec.tensor_reduce(s1[:, 0:1], src, AX, ALU.max))
                    c.link(vec.tensor_scalar(dst, src, s1[:, 0:1], None, ALU.subtract))
                    dve.nop().then_inc(i_p, 1)
                    dve.wait_ge(i_ex, turn_)
                    c.link(vec.tensor_reduce(s1[:, 0:1], dst, AX, ALU.add))
                    c.link(vec.reciprocal(s1[:, 1:2], s1[:, 0:1]))
                    c.link(vec.tensor_scalar(dst, dst, s1[:, 1:2], None, ALU.mult))

                softmax(erow, lrow, EX, 1)
                c.link(vec.tensor_scalar(lrow, erow, CAP, None, ALU.min))
                softmax(wrow, lrow, EX, 2)
                dve.nop(nofuse=True)
                c.link(vec.max(top_v, wrow))
                c.link(vec.max_index(top_i, top_v, wrow))
                c.link(vec.tensor_copy(pick[:, 0:2], top_i[:, 0:2]))
                softmax(pick[:, 2:4], top_v[:, 0:2], 2, 3)
                c.link(vec.tensor_scalar(oh0, iota[0:1, 0:EX], pick[:, 0:1], None, ALU.is_equal))
                c.link(vec.tensor_scalar(oh1, iota[0:1, 0:EX], pick[:, 1:2], None, ALU.is_equal))
                c.link(vec.tensor_scalar(dense, oh0, pick[:, 2:3], None, ALU.mult))
                c.link(vec.scalar_tensor_tensor(dense, oh1, pick[:, 3:4], dense, ALU.mult, ALU.add))
                dve.nop().then_inc(i_p, 1)
                dve.wait_ge(i_pe, 4)
                c.link(vec.tensor_copy(picks, bank[3][:, 0:4]))
                c.link(vec.tensor_copy(dense_t, bank[4][0:EX, 0:1]))
                c.link(vec.tensor_copy(oh_t, bank[4][0:EX, 1:3]))
                dve.nop().then_inc(i_p, 1)
                for e in (0, 1):
                    for h in range(H):
                        c.link(vec.tensor_scalar(e_f[:, e * 6 + h:e * 6 + h + 1], picks[:, e:e + 1], float(D), float(h * P), ALU.mult, ALU.add))
                    for k in range(FC):
                        c.link(vec.tensor_scalar(e_f[:, e * 6 + 2 + k:e * 6 + 3 + k], picks[:, e:e + 1], float(FF), float(k * P), ALU.mult, ALU.add))
                c.link(vec.tensor_scalar(e_f, e_f, qcol[:, 0:1], None, ALU.add))
                vec.tensor_copy(e_idx, e_f).then_inc(i_p, 1)
                dve.wait_ge(i_pe, 5)
                c.link(vec.tensor_copy(b1_col, bank[5][:, 0:2 * FC]))
                c.link(vec.tensor_copy(b2_row, bank[6][0:1, 0:D]))
                dve.wait_ge(i_w, 16 * 12)
                for e in (0, 1):
                    c.link(vec.tensor_scalar(w2[e], w2[e], picks[:, 2 + e:3 + e], None, ALU.mult))

            @block.scalar
            def _(s):
                for k, v in enumerate((erow, wrow, pick[:, 2:4])):
                    s.wait_ge(i_p, k + 1)
                    act.activation(v, v, ACT.Exp).then_inc(i_ex, 1)

            @block.gpsimd
            def _(pool):
                pool.wait_ge(i_p, 6)
                w1_rows = a["L1_ffn_W1"].rearrange("e c f -> (e c) f")
                w2_rows = a["L1_ffn_W2"].rearrange("e f d -> (e f) d")
                for e in (0, 1):
                    for k in range(H + FC):
                        dst = w1[e][:, k * FF:(k + 1) * FF] if k < H else w2[e][:, (k - H) * D:(k - H + 1) * D]
                        pool.indirect_dma_start(dst, None, w1_rows if k < H else w2_rows,
                                                bass.IndirectOffsetOnAxis(ap=e_idx[:, e * 6 + k:e * 6 + k + 1], axis=0)).then_inc(i_w, 16)
                pool.wait_ge(i_w, 16 * 12)

            @block.tensor
            def _(t_):
                def column_sum(t, b, rows_, u):
                    t_.wait_ge(norm_t, t + 1)
                    pe.matmul(bank[0][0:1, 0:D], ones[0:rows_, 0:1], T[2][0:rows_, b * D:(b + 1) * D],
                              start=False, stop=False, skip_group_check=True).then_inc(summed_t, 1)

                pe.matmul(bank[0][0:1, 0:D], zeros[:, 0:1], W[:, 0:D], start=True, stop=False, skip_group_check=True)
                tiles(t_, [(0, column_sum)])
                pe.matmul(bank[0][0:1, 0:D], zeros[:, 0:1], W[:, 0:D], start=False, stop=True, skip_group_check=True).then_inc(i_pe, 1)
                t_.wait_ge(i_ch, 1)
                for h in range(H):
                    last = pe.matmul(bank[1][:, h:h + 1], mean_row[:, h * P:(h + 1) * P], ones[0:1, 0:1], start=True, stop=True)
                last.then_inc(i_pe, 1)
                t_.wait_ge(i_ch, 2)
                for h in range(H):
                    last = pe.matmul(bank[2][0:1, 0:EX], mean_t[:, h:h + 1], wr[:, h * EX:(h + 1) * EX], start=h == 0, stop=h == H - 1)
                last.then_inc(i_pe, 1)
                t_.wait_ge(i_p, 4)
                pe.matmul(bank[3][:, 0:4], ones[0:1, :], pick, start=True, stop=True)
                for k, v in enumerate((dense, oh0, oh1)):
                    last = pe.matmul(bank[4][0:EX, k:k + 1], v, ones[0:1, 0:1], start=True, stop=True)
                last.then_inc(i_pe, 1)
                t_.wait_ge(i_p, 5)
                for e in (0, 1):
                    for k in range(FC):
                        pe.matmul(bank[5][:, e * FC + k:e * FC + k + 1], b1_all[:, k * P:(k + 1) * P], oh_t[:, e:e + 1], start=True, stop=True)
                pe.matmul(bank[6][0:1, 0:D], dense_t, b2_all, start=True, stop=True).then_inc(i_pe, 1)

        nrm, turned, turned_sb, hid, act_out, prod, done, ready = (
            sem(f"i1_{n}") for n in ("normalized", "turned", "turned_sb", "hidden", "gelu", "product", "done", "ready"))
        hsb = [[T[2], T[3]], [T[4], T[5]]]
        with nc.Block() as block:
            @block.vector
            def _(dve):
                dve.sem_inc(done, 2)

                def normal(t, b, rows_, u):
                    dve.wait_ge(done, t + 1)
                    normalize(T[0][:, b * D:(b + 1) * D], t).then_inc(nrm, 1)

                def add(t, b, rows_, u):
                    dve.wait_ge(prod, t + 1)
                    vec.tensor_tensor(tile_of(ACC, t), T[0][:, b * D:(b + 1) * D], bank[6 + b][:, 0:D], ALU.add).then_inc(done, 1)

                tiles(dve, [(0, normal), (1, add)])

            @block.scalar
            def _(s):
                def copy(t, b, rows_, u):
                    s.wait_ge(turned, t + 1)
                    act.copy(T[1][:, b * D:(b + 1) * D], bank[b][:, 0:D]).then_inc(turned_sb, 1)

                def gelu(t, b, rows_, u):
                    for e in (0, 1):
                        s.wait_ge(hid, 2 * t + e + 1)
                        for k in range(FC):
                            ins = act.activation(hsb[e][b][:, k * P:(k + 1) * P], bank[2 + 2 * e + b][:, k * P:(k + 1) * P],
                                                 ACT.Gelu, bias=b1_col[:, e * FC + k:e * FC + k + 1])
                        ins.then_inc(act_out, 1)

                tiles(s, [(0, copy), (0, gelu)])

            @block.tensor
            def _(t_):
                def turn1(t, b, rows_, u):
                    t_.wait_ge(nrm, t + 1)
                    turn(bank[b][:, 0:D], T[0][:, b * D:(b + 1) * D]).then_inc(turned, 1)

                def hidden(t, b, rows_, u):
                    t_.wait_ge(turned_sb, t + 1)
                    for e in (0, 1):
                        for k in range(FC):
                            for h in range(H):
                                last = pe.matmul(bank[2 + 2 * e + b][:, k * P:(k + 1) * P], w1[e][:, h * FF + k * P:h * FF + (k + 1) * P],
                                                 T[1][:, b * D + h * P:b * D + (h + 1) * P], start=h == 0, stop=h == H - 1)
                        last.then_inc(hid, 1)

                def outputs(t, b, rows_, u):
                    for e in (0, 1):
                        t_.wait_ge(act_out, 2 * t + e + 1)
                        for k in range(FC):
                            pe.matmul(bank[6 + b][:, 0:D], hsb[e][b][:, k * P:(k + 1) * P], w2[e][:, k * D:(k + 1) * D],
                                      start=e == 0 and k == 0, stop=False)
                    add_row(bank[6 + b][:, 0:D], b2_row).then_inc(prod, 1)

                tiles(t_, [(0, turn1), (1, outputs), (0, hidden)])

        recycle()
        z_in, z_ch = dma_sem("z_in"), sem("z_chain")
        layer_norm_stats("ln4", ACC)
        with nc.Block() as block:
            @block.sync
            def _(sp):
                for k, n in enumerate(("gamma", "beta")):
                    sp.dma_start(W[:, k * D:(k + 1) * D], a[f"L1_ffn_{n}"].rearrange("(a d) -> a d", a=1).broadcast_to([P, D])).then_inc(z_in, 16)

            @block.vector
            def _(dve):
                c = Chain(dve, z_ch)
                dve.wait_ge(z_in, 32)
                y, x = wide(ACC[:, :]), wide(X[:, :])
                c.link(vec.tensor_tensor(y, y, per_tile(mean), ALU.subtract))
                c.link(vec.tensor_tensor(y, y, per_tile(rstd[:, :]), ALU.mult))
                c.link(vec.tensor_tensor(y, y, per_feature(W[:, 0:D]), ALU.mult))
                c.link(vec.tensor_tensor(x, x, per_feature(W[:, D:2 * D]), ALU.add))
                c.link(vec.tensor_tensor(x, x, y, ALU.add))

        stored = sem("stored")
        with nc.Block() as block:
            @block.sync
            def _(sp):
                full = out[0:(NT - 1) * P, :].rearrange("(t p) d -> p t d", p=P)
                sp.dma_start(full, X[:, 0:(NT - 1) * D].rearrange("p (t d) -> p t d", d=D)).then_inc(stored, 16)
                sp.dma_start(out[(NT - 1) * P:N, :], X[0:TAIL, (NT - 1) * D:NT * D]).then_inc(stored, 16)
                sp.wait_ge(stored, 32)


_SCRATCH_KIND = "Internal"


def kernel(**inputs):
    import numpy as np
    import concourse.bacc as bacc
    from concourse.bass_utils import run_bass_kernel_spmd

    nc = bacc.Bacc("TRN2", target_bir_lowering=False, num_devices=1)
    arrays, a = {}, {}
    for name, value in inputs.items():
        v = np.ascontiguousarray(value)
        arrays[f"in_{name}"] = v
        a[name] = nc.dram_tensor(f"in_{name}", v.shape, mybir.dt.from_np(v.dtype), kind="ExternalInput").ap()
    N, D = inputs["x"].shape
    E = inputs["src"].shape[0]
    R = inputs["L1_gnn_weight"].shape[0]
    NT = -(-N // P)
    J = -(-E // P)
    QB = -(-(-(-(J + NT - 1) // SLOTS)) * SLOTS // P)
    NPAD = NT * P
    INNER = inputs["L0_ffn_W_fx"].shape[1]
    scratch = {
        "rec": ([P * J, 4], F32), "rec_by_src": ([P * J, 4], F32), "rec_by_dst": ([P * J, 4], F32),
        "placed_rec": ([P, 5 * J], F32),
        "off0": ([QB * P], I32), "off1": ([QB * P], I32), "deg_in": ([(NT + 1) * P], F32),
        "tab0": ([NPAD, D + 1], F32), "tab1": ([NPAD, D], F32), "tab2": ([R * NPAD, D], F32),
        "sw": ([NPAD, INNER], F32), "qkv": ([NPAD, 3 * P], F32), "route": ([1, 64], F32),
    }
    dram = {n: nc.dram_tensor(n, s, d, kind=_SCRATCH_KIND).ap() for n, (s, d) in scratch.items()}
    out = nc.dram_tensor("out", [N, D], F32, kind="ExternalOutput").ap()
    gps_layers(nc, a, dram, out)
    r = run_bass_kernel_spmd(nc, [arrays], core_ids=[0])
    return r.results[0]["out"]
```
